# Optimizing a Trainium2 kernel written in Bass

```python
import numpy as np
import jax
import jax.numpy as jnp

def _softmax(x, axis=-1):
    return jax.nn.softmax(x, axis=axis)

def _gelu(x):
    return jax.nn.gelu(x, approximate=True)

def _silu(x):
    return jax.nn.silu(x)

def _sigmoid(x):
    return jax.nn.sigmoid(x)

def _layernorm(x, axis=-1, eps=1e-05):
    m = jnp.mean(x, axis=axis, keepdims=True)
    v = jnp.var(x, axis=axis, keepdims=True)
    return (x - m) / jnp.sqrt(v + eps)

def _scatter_add(tgt, idx, src, axis=0):
    return tgt.at[idx].add(src)

def _segment_sum(src, seg, n):
    return jax.ops.segment_sum(src, seg, n)
kernel_name = 'mk_adj_resnorm_d2_adj_r2_d7da6c'

def setup_inputs(seed: int=0):
    np.random.seed(seed)
    _w = jnp.asarray

    def _rec_inputs():
        import jax
        import jax.numpy as jnp
        _gk = jax.random.key(seed)
        x = -0.0001538 + 1 * jax.random.normal(jax.random.fold_in(_gk, 1), (128, 64, 384), jnp.float32)
        _a = jax.random.bernoulli(jax.random.fold_in(_gk, 2), 0.0625, (128, 64, 64))
        _a = jnp.logical_or(_a, jnp.swapaxes(_a, -1, -2))
        _a = jnp.logical_or(_a, jnp.eye(64, dtype=bool))
        _af = _a.astype(jnp.float32)
        _af = _af * jax.random.uniform(jax.random.fold_in(_gk, 3), (128, 64, 64), jnp.float32, 0.05, 5.06092)
        adj = _af
        return (x, adj)
    x, adj = _rec_inputs()

    def _L0_gnn_setup():
        import jax, jax.numpy as jnp
        import numpy as np
        D_MODEL = 384
        NHEADS = 8
        D_FF = 1536
        B, N = (8, 512)
        EPS = 1e-06

        def _rmsnorm(x, alpha, gamma):
            x = x * jax.lax.rsqrt(jnp.mean(x * x, axis=-1, keepdims=True) + EPS)
            return alpha * x + gamma
        key = jax.random.key(seed)
        ks = jax.random.split(key, 10)
        d, f = (D_MODEL, D_FF)
        s = 1.0 / np.sqrt(d)
        inp = {'x': jax.random.normal(ks[0], (B, N, d), dtype=jnp.float32), 'attn_bias': jax.random.normal(ks[1], (B, N, N), dtype=jnp.float32), 'wq': jax.random.normal(ks[2], (d, d), dtype=jnp.float32) * s, 'bq': jnp.zeros((d,), jnp.float32), 'wk': jax.random.normal(ks[3], (d, d), dtype=jnp.float32) * s, 'bk': jnp.zeros((d,), jnp.float32), 'wv': jax.random.normal(ks[4], (d, d), dtype=jnp.float32) * s, 'bv': jnp.zeros((d,), jnp.float32), 'wo': jax.random.normal(ks[5], (d, d), dtype=jnp.float32) * s, 'bo': jnp.zeros((d,), jnp.float32), 'w1': jax.random.normal(ks[6], (d, f), dtype=jnp.float32) * s, 'b1': jnp.zeros((f,), jnp.float32), 'w2': jax.random.normal(ks[7], (f, d), dtype=jnp.float32) * (1.0 / np.sqrt(f)), 'b2': jnp.zeros((d,), jnp.float32), 'alpha1': jnp.ones((d,), jnp.float32), 'gamma1': jnp.ones((d,), jnp.float32), 'alpha2': jnp.ones((d,), jnp.float32), 'gamma2': jnp.ones((d,), jnp.float32)}
        return inp
    _L0_gnn_all = _L0_gnn_setup()
    _L0_gnn_in = {k: v for k, v in _L0_gnn_all.items() if k in ('wq', 'bq', 'wk', 'bk', 'wv', 'bv', 'wo', 'bo', 'w1', 'b1', 'w2', 'b2', 'alpha1', 'gamma1', 'alpha2', 'gamma2')}
    del _L0_gnn_all

    def _L1_gnn_setup():
        import jax, jax.numpy as jnp
        import numpy as np
        NUM_HEADS = 12
        HIDDEN = 384
        HEAD = HIDDEN // NUM_HEADS
        B, N = (16, 256)
        key = jax.random.key(seed)
        ks = jax.random.split(key, 9)
        s = 0.02
        return {'x': jax.random.normal(ks[0], (B, N, HIDDEN), jnp.float32), 'spatial_encoding': jax.random.normal(ks[1], (B, N, N), jnp.float32), 'edge_encoding': jax.random.normal(ks[2], (B, N, N), jnp.float32), 'Wq': jax.random.normal(ks[3], (HIDDEN, HIDDEN), jnp.float32) * s, 'Wk': jax.random.normal(ks[4], (HIDDEN, HIDDEN), jnp.float32) * s, 'Wv': jax.random.normal(ks[5], (HIDDEN, HIDDEN), jnp.float32) * s, 'bv': jax.random.normal(ks[6], (HIDDEN,), jnp.float32) * s, 'Wo': jax.random.normal(ks[7], (HIDDEN, HIDDEN), jnp.float32) * s, 'bo': jax.random.normal(ks[8], (HIDDEN,), jnp.float32) * s}
    _L1_gnn_all = _L1_gnn_setup()
    _L1_gnn_in = {k: v for k, v in _L1_gnn_all.items() if k in ('Wq', 'Wk', 'Wv', 'bv', 'Wo', 'bo')}
    del _L1_gnn_all
    return {'x': x, 'adj': adj, 'L0_gnn_wq': _L0_gnn_in['wq'], 'L0_gnn_bq': _L0_gnn_in['bq'], 'L0_gnn_wk': _L0_gnn_in['wk'], 'L0_gnn_bk': _L0_gnn_in['bk'], 'L0_gnn_wv': _L0_gnn_in['wv'], 'L0_gnn_bv': _L0_gnn_in['bv'], 'L0_gnn_wo': _L0_gnn_in['wo'], 'L0_gnn_bo': _L0_gnn_in['bo'], 'L0_gnn_w1': _L0_gnn_in['w1'], 'L0_gnn_b1': _L0_gnn_in['b1'], 'L0_gnn_w2': _L0_gnn_in['w2'], 'L0_gnn_b2': _L0_gnn_in['b2'], 'L0_gnn_alpha1': _L0_gnn_in['alpha1'], 'L0_gnn_gamma1': _L0_gnn_in['gamma1'], 'L0_gnn_alpha2': _L0_gnn_in['alpha2'], 'L0_gnn_gamma2': _L0_gnn_in['gamma2'], 'L1_gnn_Wq': _L1_gnn_in['Wq'], 'L1_gnn_Wk': _L1_gnn_in['Wk'], 'L1_gnn_Wv': _L1_gnn_in['Wv'], 'L1_gnn_bv': _L1_gnn_in['bv'], 'L1_gnn_Wo': _L1_gnn_in['Wo'], 'L1_gnn_bo': _L1_gnn_in['bo']}

def reference(x, adj, L0_gnn_wq, L0_gnn_bq, L0_gnn_wk, L0_gnn_bk, L0_gnn_wv, L0_gnn_bv, L0_gnn_wo, L0_gnn_bo, L0_gnn_w1, L0_gnn_b1, L0_gnn_w2, L0_gnn_b2, L0_gnn_alpha1, L0_gnn_gamma1, L0_gnn_alpha2, L0_gnn_gamma2, L1_gnn_Wq, L1_gnn_Wk, L1_gnn_Wv, L1_gnn_bv, L1_gnn_Wo, L1_gnn_bo):
    import jax
    import jax.numpy as jnp

    def _L0_gnn_ref(x, attn_bias, wq, bq, wk, bk, wv, bv, wo, bo, w1, b1, w2, b2, alpha1, gamma1, alpha2, gamma2):
        import jax, jax.numpy as jnp
        import numpy as np
        D_MODEL = 384
        NHEADS = 8
        D_FF = 1536
        B, N = (8, 512)
        EPS = 1e-06

        def _rmsnorm(x, alpha, gamma):
            x = x * jax.lax.rsqrt(jnp.mean(x * x, axis=-1, keepdims=True) + EPS)
            return alpha * x + gamma
        b, n, d = x.shape
        h = NHEADS
        dh = d // h
        scaling = dh ** (-0.5)

        def split_heads(t):
            return t.reshape(b, n, h, dh).transpose(0, 2, 1, 3)
        q = split_heads(x @ wq + bq)
        k = split_heads(x @ wk + bk)
        v = split_heads(x @ wv + bv)
        scores = jnp.einsum('bhqd,bhkd->bhqk', q, k) * scaling
        scores = scores + attn_bias[:, None, :, :]
        attn = jax.nn.softmax(scores, axis=-1)
        ctx = jnp.einsum('bhij,bhjd->bhid', attn, v)
        ctx = ctx.transpose(0, 2, 1, 3).reshape(b, n, d)
        attn_out = ctx @ wo + bo
        x = _rmsnorm(x + attn_out, alpha1, gamma1)
        ff = jax.nn.silu(x @ w1 + b1) @ w2 + b2
        x = _rmsnorm(x + ff, alpha2, gamma2)
        return x

    def _L1_gnn_ref(x, spatial_encoding, edge_encoding, Wq, Wk, Wv, bv, Wo, bo):
        import jax, jax.numpy as jnp
        import numpy as np
        NUM_HEADS = 12
        HIDDEN = 384
        HEAD = HIDDEN // NUM_HEADS
        B, N = (16, 256)
        b, n, h = x.shape
        scale = jnp.asarray(HIDDEN, x.dtype) ** (-0.5)
        q = (x @ Wq.T).reshape(b, n, NUM_HEADS, HEAD)
        k = (x @ Wk.T).reshape(b, n, NUM_HEADS, HEAD)
        v = (x @ Wv.T + bv).reshape(b, n, NUM_HEADS, HEAD)
        bias = (spatial_encoding + edge_encoding)[:, None]
        scores = jnp.einsum('bqhd,bkhd->bhqk', q, k) * scale + bias
        row_nonzero = jnp.any(scores != 0, axis=-1, keepdims=True)
        scores = jnp.where(row_nonzero, scores, -jnp.inf)
        p = jax.nn.softmax(scores, axis=-1)
        p = jnp.nan_to_num(p)
        out = jnp.einsum('bhqk,bkhd->bqhd', p, v).reshape(b, n, h)
        return out @ Wo.T + bo
    x = _layernorm(x + _L0_gnn_ref(x, adj, L0_gnn_wq, L0_gnn_bq, L0_gnn_wk, L0_gnn_bk, L0_gnn_wv, L0_gnn_bv, L0_gnn_wo, L0_gnn_bo, L0_gnn_w1, L0_gnn_b1, L0_gnn_w2, L0_gnn_b2, L0_gnn_alpha1, L0_gnn_gamma1, L0_gnn_alpha2, L0_gnn_gamma2), axis=-1)
    x = _layernorm(x + _L1_gnn_ref(x, adj, adj, L1_gnn_Wq, L1_gnn_Wk, L1_gnn_Wv, L1_gnn_bv, L1_gnn_Wo, L1_gnn_bo), axis=-1)
    return x

_drawn_inputs = setup_inputs


def setup_inputs(seed=0):
    import zlib

    import numpy as np

    out = dict(_drawn_inputs(seed))
    spreads = {'L0_gnn_bq': (0.0, 0.642),
     'L0_gnn_bk': (0.0, 0.8),
     'L0_gnn_bv': (0.0, 0.1),
     'L0_gnn_bo': (0.0, 0.1),
     'L0_gnn_b1': (0.0, 0.335),
     'L0_gnn_b2': (0.0, 0.1),
     'L0_gnn_alpha1': (1.0, 0.2),
     'L0_gnn_gamma1': (1.0, 0.2),
     'L0_gnn_alpha2': (1.0, 0.2),
     'L0_gnn_gamma2': (1.0, 0.2)}
    factors = {'L1_gnn_Wq': 8.0, 'L1_gnn_Wk': 8.0, 'L1_gnn_bv': 6.316, 'L1_gnn_bo': 3.0}
    for name, (base, spread) in spreads.items():
        noise = np.random.default_rng([zlib.crc32(name.encode()), seed]).standard_normal(out[name].shape)
        drawn = base * np.exp(spread * noise) if base else spread * noise
        out[name] = jnp.asarray(drawn.astype(out[name].dtype))
    for name, factor in factors.items():
        out[name] = (out[name] * factor).astype(out[name].dtype)
    return out
```

```python
from contextlib import ExitStack

import concourse.bass as bass
from concourse import mybir

F32 = mybir.dt.float32
F32R = mybir.dt.float32r
ALU = mybir.AluOpType
ACT = mybir.ActivationFunctionType
AX_X = mybir.AxisListType.X

P = 128
GRAPHS, NODES, D = 128, 64, 384
TOKENS = GRAPHS * NODES
TILES = 2
GROUP = TILES * P
GB = GROUP // NODES
NG = TOKENS // GROUP
KT = D // P
H0, H1 = 8, 12
DH0, DH1 = D // H0, D // H1
F = 1536
FC = F // P
FP = FC // 2
RING = 3
EPS_RMS, EPS_LN = 1e-6, 1e-5
ROOT = float(D) ** -0.5
SCALE0, SCALE1 = float(DH0) ** -0.5, float(D) ** -0.5


def head_blocks(heads):
    dh = D // heads
    blocks, span = [], []
    for t in range(KT):
        own = [h for h in range(heads) if h * dh < (t + 1) * P and (h + 1) * dh > t * P]
        span.append((len(blocks), len(blocks) + len(own), own[0]))
        blocks += [(t, h) for h in own]
    return blocks, span


BLOCKS0, SPAN0 = head_blocks(H0)
BLOCKS1, SPAN1 = head_blocks(H1)
NB0, NB1 = len(BLOCKS0), len(BLOCKS1)


def wait(eng, sem, value):
    if not isinstance(value, int) or value > 0:
        eng.wait_ge(sem, value)


def layer0(nc, x, xT, adj, w, x2):
    VW = DH0 + 1
    VE = H0 // 2 * VW
    with ExitStack() as ctx:
        def sb(name, shape, dt=F32):
            return ctx.enter_context(nc.sbuf_tensor(name, shape, dt))

        def sem(name):
            return ctx.enter_context(nc.semaphore(name))

        bank = [ctx.enter_context(nc.psum_tensor(f"a_bank{i}", [P, 512], F32)) for i in range(8)]
        A, B, ACC = bank[0:3], bank[3:6], bank[6:8]

        wide = {"wq": D, "wk": D, "wv": 2 * VE, "wo": D, "w1": F, "w2": D}
        tall = {n: FC if n == "w2" else KT for n in wide}
        W = {n: [sb(f"a_{n}_{s}", [P, tall[n], wide[n]], F32R) for s in ("hi", "lo")] for n in wide}
        ident = sb("a_ident", [P, P])
        rows = {n: sb(f"a_{n}", [P, D]) for n in ("bo", "alpha1", "gamma1", "b2", "alpha2", "gamma2")}
        bv = sb("a_bv", [P, 2, H0 // 2, VW])
        mask = sb("a_mask", [P, NB0])
        kbias = sb("a_kbias", [P, NB0])
        bq, bk, b1 = sb("a_bq", [P, KT]), sb("a_bk", [P, KT]), sb("a_b1", [P, FC])
        half, eps_rms, eps_ln = (sb(f"a_{n}", [P, TILES]) for n in ("half", "eps_rms", "eps_ln"))

        sizes = [("xt_raw", KT * GROUP), ("x_in", TILES * D), ("x_bo", TILES * D), ("x_res", TILES * D),
                 ("q", KT * GROUP), ("k_blocks", GB * NB0 * NODES), ("v_nat", TILES * 2 * VE),
                 ("v_pairs", GB * 2 * VE), ("p", TILES * H0 * NODES), ("pt", TILES * H0 * NODES),
                 ("ctx", TILES * D), ("x1", TILES * D), ("x1_b2", TILES * D), ("silu", 2 * 512),
                 ("z", TILES * D)]
        work = sb("a_work", [P, sum(n for _, n in sizes)])
        at, v = 0, {}
        for name, n in sizes:
            v[name] = work[:, at:at + n]
            at += n
        xt_raw = v["xt_raw"]
        x_in, x_bo, x_res, ctxt, x1, x1_b2, z = (
            v[n].rearrange("p (t d) -> p t d", t=TILES) for n in ("x_in", "x_bo", "x_res", "ctx", "x1", "x1_b2", "z"))
        q = v["q"].rearrange("p (k n) -> p k n", k=KT)
        k_blocks = v["k_blocks"].rearrange("p (g b n) -> p g b n", g=GB, b=NB0)
        v_nat = v["v_nat"].rearrange("p (t c) -> p t c", t=TILES)
        v_pairs = v["v_pairs"].rearrange("p (g c) -> p g c", g=GB)
        prob = v["p"].rearrange("p (t c) -> p t c", t=TILES)
        pt = v["pt"].rearrange("p (t c) -> p t c", t=TILES)
        silu = v["silu"].rearrange("p (s c) -> p s c", s=2)

        adj_in = sb("a_adj", [P, TILES, NODES])
        xt = [sb(f"a_xt_{s}", [P, KT, GROUP], F32R) for s in ("hi", "lo")]
        ctx_t = [sb(f"a_ctxt_{s}", [P, TILES, D], F32R) for s in ("hi", "lo")]
        x1_t = [sb(f"a_x1t_{s}", [P, KT, GROUP], F32R) for s in ("hi", "lo")]
        hid = [sb(f"a_hid_{s}", [P, RING, 512], F32R) for s in ("hi", "lo")]
        smax = sb("a_smax", [P, TILES, H0])
        rden = sb("a_rden", [P, TILES, H0])
        ssq1, ssq2, ssq3 = (sb(f"a_ssq{i}", [P, TILES]) for i in (1, 2, 3))
        ms1, ms2, ms3 = (sb(f"a_ms{i}", [P, TILES]) for i in (1, 2, 3))
        rstd1, rstd2, rstd3 = (sb(f"a_rstd{i}", [P, TILES]) for i in (1, 2, 3))
        zsum, nmean, nmean_c = (sb(f"a_{n}", [P, TILES]) for n in ("zsum", "nmean", "nmean_c"))

        const_loaded, row_set = sem("const_loaded"), sem("row_set")
        xt_loaded, x_loaded, adj_loaded, x2_stored = sem("xt_loaded"), sem("x_loaded"), sem("adj_loaded"), sem("x2_stored")
        v_swapped = [sem(f"v_swapped{t}") for t in range(TILES)]
        stage_set, pairs_zeroed = sem("stage_set"), sem("pairs_zeroed")
        qk_mm, v_mm, s_mm, pt_mm, pv_mm, ct_mm, o_mm, x1t_mm, f1_mm, f2_mm = (
            sem(n) for n in ("qk_mm", "v_mm", "s_mm", "pt_mm", "pv_mm", "ct_mm", "o_mm", "x1t_mm", "f1_mm", "f2_mm"))
        w_hi, xt_hi, q_done, x1t_hi, silu_done, hid_hi, exp_done, pt_done, ctxt_hi, sq1_done, sq2_done, sq3_done = (
            sem(n) for n in ("w_hi", "xt_hi", "q_done", "x1t_hi", "silu_done", "hid_hi", "exp_done", "pt_done",
                             "ctxt_hi", "sq1_done", "sq2_done", "sq3_done"))
        w_lo, kbias_set, xt_lo, k_done, x1t_lo, v_done, hid_lo, biased, maxed, shifted, rden_done, ctx_done = (
            sem(n) for n in ("w_lo", "kbias_set", "xt_lo", "k_done", "x1t_lo", "v_done", "hid_lo", "biased", "maxed",
                             "shifted", "rden_done", "ctx_done"))
        ctxt_lo, y1_done, x1_scaled, y2_done, z_scaled, z_done, mean_done, x2_done = (
            sem(n) for n in ("ctxt_lo", "y1_done", "x1_scaled", "y2_done", "z_scaled", "z_done", "mean_done",
                             "x2_done"))
        half_set, xbo_done, v_kept, ms_done, rstd1_done, x1_done, x1b2_done, rstd2_done, rstd3_done, xres_done = (
            sem(n) for n in ("half_set", "xbo_done", "v_kept", "ms_done", "rstd1_done", "x1_done", "x1b2_done",
                             "rstd2_done", "rstd3_done", "xres_done"))

        chunks = [(n, 0, KT) for n in ("wq", "wk", "wv", "wo")]
        chunks += [("w1", t, 1) for t in range(KT)]
        chunks += [("w2", t, 4) for t in range(0, FC, 4)]
        SLOT = 1536
        NSLOT = 7
        stage_loaded = [sem(f"stage_loaded{i}") for i in range(NSLOT)]
        v_slots = [i for i, c in enumerate(chunks) if c[0] == "wv"]

        def stage(i):
            n, t, k = chunks[i]
            return work[:, (i % NSLOT) * SLOT:(i % NSLOT) * SLOT + k * wide[n]]

        def halves(i, s):
            n, t, k = chunks[i]
            return W[n][s][:, t:t + k, :].rearrange("p k c -> p (k c)")

        N_CONST = 5 + len(rows) + 2

        block = ctx.enter_context(nc.Block())

        @block.sync
        def _(sp):
            sp.dma_start(ident[:], w["ident"]).then_inc(const_loaded, 16)
            sp.dma_start(mask[:], w["mask0"]).then_inc(const_loaded, 16)
            for dst, name in ((bq, "bq"), (bk, "bk"), (b1, "b1")):
                sp.dma_start(dst[:], w[name]).then_inc(const_loaded, 16)
            for name in rows:
                sp.dma_start(rows[name][:], w[name].rearrange("(a d) -> a d", a=1).broadcast_to([P, D])).then_inc(const_loaded, 16)
            sp.wait_ge(row_set, 1)
            bv_row = w["bv"].rearrange("(a h r d) -> a r h d", a=1, r=2, d=DH0)
            sp.dma_start(bv[:, 0, :, 0:DH0], bv_row[:, 0].broadcast_to([P, H0 // 2, DH0])).then_inc(const_loaded, 16)
            sp.dma_start(bv[:, 1, :, 0:DH0], bv_row[:, 1].broadcast_to([P, H0 // 2, DH0])).then_inc(const_loaded, 16)
            for i, (n, t, k) in enumerate(chunks):
                if i >= NSLOT:
                    sp.wait_ge(w_lo, i - NSLOT + 1)
                src = w[n].rearrange("(t p) c -> p t c", p=P)[:, t:t + k]
                if n == "wv":
                    sp.wait_ge(stage_set, 1)
                    dst = stage(i).rearrange("p (k r h c) -> p k r h c", k=KT, r=2, h=H0 // 2)
                    src = src.rearrange("p k (h r d) -> p k r h d", r=2, d=DH0)
                    for kk in range(KT):
                        for r in range(2):
                            sp.dma_start(dst[:, kk, r, :, 0:DH0], src[:, kk, r]).then_inc(stage_loaded[i % NSLOT], 16)
                else:
                    dst = stage(i).rearrange("p (k c) -> p k c", k=k)
                    sp.dma_start(dst, src).then_inc(stage_loaded[i % NSLOT], 16)

            def load_xt(g):
                wait(sp, xt_lo, g)
                for k in range(KT):
                    sp.dma_start(xt_raw[:, k * GROUP:(k + 1) * GROUP], xT[k, g]).then_inc(xt_loaded, 16)

            def load_adj(g):
                wait(sp, biased, TILES * g)
                sp.dma_start(adj_in[:], adj[g]).then_inc(adj_loaded, 16)

            def load_x(g):
                wait(sp, xres_done, g)
                sp.dma_start(x_in, x[g]).then_inc(x_loaded, 16)

            def swap_v(g, t):
                a, b = TILES * t, TILES * t + 1
                sp.wait_ge(v_done, TILES * g + t + 1)
                sp.dma_start(v_pairs[64:P, a, VE:2 * VE], v_nat[0:64, t, VE:2 * VE]).then_inc(v_swapped[t], 16)
                sp.dma_start(v_pairs[0:64, b, 0:VE], v_nat[64:P, t, 0:VE]).then_inc(v_swapped[t], 16)

            def store(g):
                sp.wait_ge(x2_done, TILES * (g + 1))
                sp.dma_start(x2[g], z).then_inc(x2_stored, 16)

            sp.wait_ge(w_lo, len(chunks))
            sp.wait_ge(pairs_zeroed, 1)
            load_xt(0)
            load_adj(0)
            load_x(0)

            def step(g, att=True, ffn=True, more=True):
                if att:
                    if more:
                        load_xt(g + 1)
                    for t in range(TILES):
                        swap_v(g, t)
                    if more:
                        load_adj(g + 1)
                if ffn:
                    store(g - 1)
                if att and more:
                    load_x(g + 1)

            step(0, ffn=False)
            step(1)
            with sp.Fori(2, NG - 1) as g:
                step(g)
            step(NG - 1, more=False)
            step(NG, att=False)
            sp.wait_ge(x2_stored, 16 * NG)

        @block.tensor
        def _(pe):
            def mm3(out, lhs, rhs, first, last):
                for n, (a, b) in enumerate(((0, 0), (1, 0), (0, 1))):
                    r = pe.matmul(out, lhs[a], rhs[b], start=first and n == 0, stop=last and n == 2)
                return r

            def qk(g):
                wait(pe, xt_lo, g + 1)
                for u in range(3):
                    if isinstance(g, int) and g == 1:
                        pe.wait_ge(*((q_done, u + 1) if u < 2 else (k_done, 1)))
                    elif not isinstance(g, int) or g > 1:
                        pe.wait_ge(silu_done, FP * (g - 1) - 2 + u)
                    for s in range(2):
                        m = 2 * u + s
                        n, m = ("wq", m) if m < KT else ("wk", m - KT)
                        for k in range(KT):
                            r = mm3(A[u][:, s * GROUP:(s + 1) * GROUP],
                                    [W[n][j][:, k, m * P:(m + 1) * P] for j in range(2)],
                                    [xt[j][:, k, :] for j in range(2)], k == 0, k == KT - 1)
                    r.then_inc(qk_mm, 1)

            def values(g, t, ffn):
                if t == 0:
                    wait(pe, ctxt_lo, TILES * g)
                elif ffn:
                    pe.wait_ge(x1t_lo, TILES * (g - 1) + 1)
                out = B[2 if t == 0 else 0]
                for k in range(KT):
                    r = mm3(out[:, 0:2 * VE], [xt[j][:, k, t * P:(t + 1) * P] for j in range(2)],
                            [W["wv"][j][:, k, :] for j in range(2)], k == 0, k == KT - 1)
                r.then_inc(v_mm, 1)

            def scores(g, t, ffn):
                if t == 0:
                    pe.wait_ge(q_done, 2 * (g + 1))
                    pe.wait_ge(k_done, g + 1)
                    if ffn:
                        pe.wait_ge(x1t_lo, TILES * g)
                else:
                    pe.wait_ge(v_done, TILES * g + 1)
                out = B[1 + t]
                for k in range(KT):
                    b0, b1_, h = SPAN0[k]
                    for s in range(2):
                        n = TILES * t + s
                        r = pe.matmul(out[64 * s:64 * s + 64, h * NODES:(h + b1_ - b0) * NODES],
                                      q[:, k, n * NODES:(n + 1) * NODES],
                                      k_blocks[:, n, b0:b1_, :].rearrange("p b n -> p (b n)"),
                                      start=k == 0, stop=k == KT - 1, skip_group_check=True)
                r.then_inc(s_mm, 1)

            def turn_p(g, t):
                pe.wait_ge(exp_done, TILES * g + t + 1)
                if t == 0:
                    pe.wait_ge(v_done, TILES * g + 2)
                for h in range(H0 // 2):
                    r = pe.transpose(B[2 * t][:, h * P:(h + 1) * P], prob[:, t, h * P:(h + 1) * P], ident[:])
                r.then_inc(pt_mm, 1)

            def pv(g, t):
                pe.wait_ge(pt_done, TILES * g + t + 1)
                pe.wait_ge(v_swapped[t], 32 * (g + 1))
                pe.wait_ge(v_kept, TILES * g + t + 1)
                if t == 0:
                    pe.wait_ge(biased, TILES * g + 1)
                out = B[1 - t]
                for h in range(H0 // 2):
                    for s in range(2):
                        n = TILES * t + s
                        vv = v_pairs[:, n, :].rearrange("p (r h c) -> p h r c", r=2, h=H0 // 2)[:, h]
                        r = pe.matmul(out[64 * s:64 * s + 64, h * 2 * VW:(h + 1) * 2 * VW].rearrange("p (r c) -> p r c", r=2),
                                      pt[:, t, h * P + 64 * s:h * P + 64 * s + 64], vv, start=True, stop=True,
                                      skip_group_check=True)
                r.then_inc(pv_mm, 1)

            def turn_ctx(g, t):
                pe.wait_ge(ctx_done, TILES * g + t + 1)
                if t == 1:
                    pe.wait_ge(pt_done, TILES * g + 2)
                for k in range(KT):
                    r = pe.transpose(B[1 + t][:, k * P:(k + 1) * P], ctxt[:, t, k * P:(k + 1) * P], ident[:])
                r.then_inc(ct_mm, 1)

            def attn_out(g, t):
                pe.wait_ge(ctxt_lo, TILES * g + t + 1)
                if t == 0:
                    pe.wait_ge(ctx_done, TILES * g + 2)
                for k in range(KT):
                    r = mm3(B[t][:, 0:D], [ctx_t[j][:, t, k * P:(k + 1) * P] for j in range(2)],
                            [W["wo"][j][:, k, :] for j in range(2)], k == 0, k == KT - 1)
                r.then_inc(o_mm, 1)

            def turn_x1(f, t):
                pe.wait_ge(x1_done, TILES * f + t + 1)
                for k in range(KT):
                    r = pe.transpose(B[t][:, k * P:(k + 1) * P], x1[:, t, k * P:(k + 1) * P], ident[:])
                r.then_inc(x1t_mm, 1)

            def ffn1(f, p, att):
                if p == 0:
                    pe.wait_ge(x1t_lo, TILES * (f + 1))
                if p < 3 and att:
                    pe.wait_ge(*((q_done, 2 * (f + 1) + p + 1) if p < 2 else (k_done, f + 2)))
                else:
                    pe.wait_ge(silu_done, FP * f + p - 2)
                for s in range(2):
                    m = 2 * p + s
                    for k in range(KT):
                        r = mm3(A[p % 3][:, s * GROUP:(s + 1) * GROUP],
                                [W["w1"][j][:, k, m * P:(m + 1) * P] for j in range(2)],
                                [x1_t[j][:, k, :] for j in range(2)], k == 0, k == KT - 1)
                r.then_inc(f1_mm, 1)

            def ffn2(f, p):
                pe.wait_ge(hid_lo, FP * f + p + 1)
                if p == 0:
                    wait(pe, y2_done, TILES * f)
                for s in range(2):
                    for t in range(TILES):
                        c = s * GROUP + t * P
                        r = mm3(ACC[t][:, 0:D], [hid[j][:, p % RING, c:c + P] for j in range(2)],
                                [W["w2"][j][:, 2 * p + s, :] for j in range(2)],
                                p == 0 and s == 0, p == FP - 1 and s == 1)
                r.then_inc(f2_mm, 1)

            pe.wait_ge(const_loaded, 16 * N_CONST)
            pe.wait_ge(w_lo, len(chunks))

            def step(g, att=True, ffn=True, more=True):
                f = g - 1
                if att:
                    qk(g)
                if ffn:
                    for t in range(TILES):
                        turn_x1(f, t)
                if att:
                    for t in range(TILES):
                        values(g, t, ffn)
                if ffn:
                    ffn1(f, 0, att)
                    ffn1(f, 1, att)
                if att:
                    for t in range(TILES):
                        scores(g, t, ffn)
                if ffn:
                    ffn1(f, 2, att)
                    ffn2(f, 0)
                    ffn2(f, 1)
                if att:
                    turn_p(g, 0)
                if ffn:
                    ffn1(f, 3, att)
                if att:
                    pv(g, 0)
                    turn_p(g, 1)
                if ffn:
                    ffn2(f, 2)
                if att:
                    pv(g, 1)
                if ffn:
                    ffn1(f, 4, att)
                    ffn2(f, 3)
                if att:
                    for t in range(TILES):
                        turn_ctx(g, t)
                if ffn:
                    ffn1(f, 5, att)
                    ffn2(f, 4)
                if att:
                    for t in range(TILES):
                        attn_out(g, t)
                if ffn:
                    ffn2(f, 5)

            step(0, ffn=False)
            step(1)
            with pe.Fori(2, NG - 1) as g:
                step(g)
            step(NG - 1, more=False)
            step(NG, att=False)

        @block.scalar
        def _(act):
            for i in range(len(chunks)):
                past = sum(2 * KT if chunks[j][0] == "wv" else 1 for j in range(i % NSLOT, i + 1, NSLOT))
                act.wait_ge(stage_loaded[i % NSLOT], 16 * past)
                act.activation(halves(i, 0), stage(i), ACT.Copy).then_inc(w_hi, 1)
            act.wait_ge(const_loaded, 16 * N_CONST)
            act.wait_ge(pairs_zeroed, 1)
            act.wait_ge(kbias_set, 1)

            def split_x(g):
                act.wait_ge(xt_loaded, 16 * KT * (g + 1))
                wait(act, v_mm, TILES * g)
                act.activation(xt[0][:].rearrange("p k n -> p (k n)"), xt_raw, ACT.Copy).then_inc(xt_hi, 1)

            def take_q(g):
                wait(act, s_mm, TILES * g)
                act.wait_ge(qk_mm, 3 * g + 1)
                for m in range(2):
                    r = act.activation(q[:, m, :], A[0][:, m * GROUP:(m + 1) * GROUP], ACT.Identity, bias=bq[:, m:m + 1])
                r.then_inc(q_done, 1)
                act.wait_ge(qk_mm, 3 * g + 2)
                act.activation(q[:, 2, :], A[1][:, 0:GROUP], ACT.Identity, bias=bq[:, 2:3])
                for b in range(*SPAN0[0][:2]):
                    r = act.activation(k_blocks[:, :, b, :], A[1][:, GROUP:2 * GROUP].rearrange("p (g n) -> p g n", g=GB),
                                       ACT.Identity, bias=kbias[:, b:b + 1], scale=mask[:, b:b + 1])
                r.then_inc(q_done, 1)

            def keep_v(g, t):
                a, b = TILES * t, TILES * t + 1
                act.wait_ge(v_done, TILES * g + t + 1)
                act.activation(v_pairs[0:64, a, 0:VE], v_nat[0:64, t, 0:VE], ACT.Copy)
                act.activation(v_pairs[64:P, b, VE:2 * VE], v_nat[64:P, t, VE:2 * VE], ACT.Copy).then_inc(v_kept, 1)

            def x1t_high(f, t):
                act.wait_ge(x1t_mm, TILES * f + t + 1)
                wait(act, f1_mm, FP * f)
                act.activation(x1_t[0][:, :, t * P:(t + 1) * P], B[t][:, 0:D].rearrange("p (k n) -> p k n", k=KT),
                               ACT.Copy).then_inc(x1t_hi, 1)

            def hidden(f, p):
                act.wait_ge(f1_mm, FP * f + p + 1)
                wait(act, hid_lo, FP * f + p - 1)
                for s in range(2):
                    m = 2 * p + s
                    r = act.activation(silu[:, p % 2, s * GROUP:(s + 1) * GROUP], A[p % 3][:, s * GROUP:(s + 1) * GROUP],
                                       ACT.Silu, bias=b1[:, m:m + 1])
                r.then_inc(silu_done, 1)
                act.wait_ge(silu_done, FP * f + p + 1)
                wait(act, f2_mm, FP * f + p + 1 - RING)
                act.activation(hid[0][:, p % RING, :], silu[:, p % 2, :], ACT.Copy).then_inc(hid_hi, 1)

            def exp(g, t):
                act.wait_ge(shifted, TILES * g + t + 1)
                act.activation(prob[:, t, :], prob[:, t, :], ACT.Exp).then_inc(exp_done, 1)

            def take_pt(g, t):
                act.wait_ge(pt_mm, TILES * g + t + 1)
                wait(act, pv_mm, TILES * (g - 1) + t + 1)
                act.activation(pt[:, t, :], B[2 * t][:, :], ACT.Copy).then_inc(pt_done, 1)

            def ctxt_high(g, t):
                act.wait_ge(ct_mm, TILES * g + t + 1)
                wait(act, o_mm, TILES * (g - 1) + t + 1)
                act.activation(ctx_t[0][:, t, :], B[1 + t][:, 0:D], ACT.Copy).then_inc(ctxt_hi, 1)

            def square(src, done, out, result, n, t, junk, bias=0.0):
                act.wait_ge(done, n)
                act.activation(junk, src[:, t, :], ACT.Square, bias=bias, scale=ROOT, accum_out=out[:, t:t + 1]).then_inc(result, 1)

            split_x(0)

            def step(g, att=True, ffn=True, more=True):
                f = g - 1
                if att:
                    take_q(g)
                if ffn:
                    for t in range(TILES):
                        x1t_high(f, t)
                    hidden(f, 0)
                if att:
                    for t in range(TILES):
                        keep_v(g, t)
                if ffn:
                    hidden(f, 1)
                    hidden(f, 2)
                if att:
                    for t in range(TILES):
                        exp(g, t)
                    for t in range(TILES):
                        take_pt(g, t)
                if ffn:
                    hidden(f, 3)
                    hidden(f, 4)
                if att:
                    for t in range(TILES):
                        ctxt_high(g, t)
                if ffn:
                    hidden(f, 5)
                if att:
                    for t in range(TILES):
                        square(x1, y1_done, ssq1, sq1_done, TILES * g + t + 1, t, ctxt[:, t, :])
                    if more:
                        split_x(g + 1)
                if ffn:
                    for t in range(TILES):
                        square(z, y2_done, ssq2, sq2_done, TILES * f + t + 1, t, silu[:, t, 0:D])
                    for t in range(TILES):
                        square(z, mean_done, ssq3, sq3_done, 2 * (f + 1), t, silu[:, t, 0:D], bias=nmean_c[:, t:t + 1])

            step(0, ffn=False)
            step(1)
            with act.Fori(2, NG - 1) as g:
                step(g)
            step(NG - 1, more=False)
            step(NG, att=False)

        @block.vector
        def _(dve):
            dve.memset(bv[:], 1.0).then_inc(row_set, 1)
            for i in v_slots:
                dve.memset(stage(i), 0.0).then_inc(stage_set, 1)
            for i in range(len(chunks)):
                dve.wait_ge(w_hi, i + 1)
                dve.tensor_tensor(halves(i, 1), stage(i), halves(i, 0).bitcast(F32), ALU.subtract).then_inc(w_lo, 1)
            dve.wait_ge(const_loaded, 16 * N_CONST)
            dve.wait_ge(w_lo, len(chunks))
            for k in range(KT):
                b0, b1_, _h = SPAN0[k]
                r = dve.tensor_scalar(kbias[:, b0:b1_], mask[:, b0:b1_], bk[:, k:k + 1], None, ALU.mult)
            r.then_inc(kbias_set, 1)
            dve.memset(v["v_pairs"], 0.0).then_inc(pairs_zeroed, 1)

            def split_x(g):
                dve.wait_ge(xt_hi, g + 1)
                dve.tensor_tensor(xt[1][:].rearrange("p k n -> p (k n)"), xt_raw,
                                  xt[0][:].bitcast(F32).rearrange("p k n -> p (k n)"), ALU.subtract).then_inc(xt_lo, 1)

            def take_k(g):
                dve.wait_ge(qk_mm, 3 * g + 3)
                wait(dve, s_mm, TILES * g)
                for k in (1, 2):
                    for b in range(*SPAN0[k][:2]):
                        r = dve.tensor_scalar(k_blocks[:, :, b, :],
                                              A[2][:, (k - 1) * GROUP:k * GROUP].rearrange("p (g n) -> p g n", g=GB),
                                              bk[:, k:k + 1], mask[:, b:b + 1], ALU.add, ALU.mult)
                r.then_inc(k_done, 1)

            def x1t_low(f, t):
                dve.wait_ge(x1t_hi, TILES * f + t + 1)
                hi, lo = (x1_t[j][:, :, t * P:(t + 1) * P] for j in range(2))
                dve.tensor_tensor(lo, B[t][:, 0:D].rearrange("p (k n) -> p k n", k=KT), hi.bitcast(F32),
                                  ALU.subtract).then_inc(x1t_lo, 1)

            def take_v(g, t):
                dve.wait_ge(v_mm, TILES * g + t + 1)
                wait(dve, v_swapped[t], 32 * g)
                wait(dve, v_kept, TILES * (g - 1) + t + 1)
                wait(dve, pv_mm, TILES * (g - 1) + t + 1)
                dve.tensor_tensor(v_nat[:, t, :], B[2 if t == 0 else 0][:, 0:2 * VE],
                                  bv[:].rearrange("p r h c -> p (r h c)"), ALU.add).then_inc(v_done, 1)

            def hidden_low(f, p):
                dve.wait_ge(hid_hi, FP * f + p + 1)
                dve.tensor_tensor(hid[1][:, p % RING, :], silu[:, p % 2, :], hid[0][:, p % RING, :].bitcast(F32),
                                  ALU.subtract).then_inc(hid_lo, 1)

            def soften(g, t):
                s = prob[:, t, :].rearrange("p (h n) -> p h n", h=H0)
                dve.wait_ge(s_mm, TILES * g + t + 1)
                if t == 0:
                    dve.wait_ge(adj_loaded, 16 * (g + 1))
                wait(dve, pt_mm, TILES * (g - 1) + t + 1)
                dve.scalar_tensor_tensor(out=s, in0=B[1 + t][:, :].rearrange("p (h n) -> p h n", h=H0), scalar=SCALE0,
                                         in1=adj_in[:, t, :].unsqueeze(1).broadcast_to([P, H0, NODES]),
                                         op0=ALU.mult, op1=ALU.add).then_inc(biased, 1)
                dve.wait_ge(biased, TILES * g + t + 1)
                dve.tensor_reduce(smax[:, t, :], s, AX_X, ALU.max).then_inc(maxed, 1)
                dve.wait_ge(maxed, TILES * g + t + 1)
                dve.tensor_tensor(s, s, smax[:, t, :].unsqueeze(2).broadcast_to([P, H0, NODES]),
                                  ALU.subtract).then_inc(shifted, 1)

            def take_ctx(g, t):
                o = B[1 - t][:, 0:2 * VE].rearrange("p (h c) -> p h c", c=VW)
                dve.wait_ge(pv_mm, TILES * g + t + 1)
                dve.reciprocal(rden[:, t, :], o[:, :, DH0]).then_inc(rden_done, 1)
                dve.wait_ge(rden_done, TILES * g + t + 1)
                wait(dve, ct_mm, TILES * (g - 1) + t + 1)
                dve.tensor_tensor(ctxt[:, t, :].rearrange("p (h c) -> p h c", h=H0), o[:, :, 0:DH0],
                                  rden[:, t, :].unsqueeze(2).broadcast_to([P, H0, DH0]), ALU.mult).then_inc(ctx_done, 1)

            def ctxt_low(g, t):
                dve.wait_ge(ctxt_hi, TILES * g + t + 1)
                dve.tensor_tensor(ctx_t[1][:, t, :], B[1 + t][:, 0:D], ctx_t[0][:, t, :].bitcast(F32),
                                  ALU.subtract).then_inc(ctxt_lo, 1)

            def take_y1(g, t):
                dve.wait_ge(o_mm, TILES * g + t + 1)
                if t == 0:
                    dve.wait_ge(xbo_done, g + 1)
                wait(dve, x1t_mm, TILES * (g - 1) + t + 1)
                wait(dve, x1b2_done, TILES * (g - 1) + t + 1)
                dve.tensor_tensor(x1[:, t, :], B[t][:, 0:D], x_bo[:, t, :], ALU.add).then_inc(y1_done, 1)

            def scale_x1(g, t):
                dve.wait_ge(rstd1_done, g + 1)
                dve.scalar_tensor_tensor(out=x1[:, t, :], in0=x1[:, t, :], scalar=rstd1[:, t:t + 1], in1=rows["alpha1"][:],
                                         op0=ALU.mult, op1=ALU.mult).then_inc(x1_scaled, 1)

            def take_y2(f, t):
                dve.wait_ge(f2_mm, FP * (f + 1))
                dve.wait_ge(x1b2_done, TILES * f + t + 1)
                if t == 0:
                    wait(dve, x2_stored, 16 * f)
                dve.tensor_tensor(z[:, t, :], ACC[t][:, 0:D], x1_b2[:, t, :], ALU.add).then_inc(y2_done, 1)

            def finish(f):
                dve.wait_ge(rstd2_done, f + 1)
                for t in range(TILES):
                    dve.scalar_tensor_tensor(out=z[:, t, :], in0=z[:, t, :], scalar=rstd2[:, t:t + 1],
                                             in1=rows["alpha2"][:], op0=ALU.mult, op1=ALU.mult).then_inc(z_scaled, 1)
                dve.wait_ge(xres_done, f + 1)
                for t in range(TILES):
                    dve.wait_ge(z_scaled, TILES * f + t + 1)
                    dve.scalar_tensor_tensor(out=z[:, t, :], in0=z[:, t, :], scalar=1.0, in1=x_res[:, t, :], op0=ALU.mult,
                                             op1=ALU.add, accum_out=zsum[:, t:t + 1]).then_inc(z_done, 1)
                dve.wait_ge(z_done, TILES * (f + 1))
                dve.tensor_scalar(nmean[:], zsum[:], -1.0 / D, None, ALU.mult).then_inc(mean_done, 1)
                dve.tensor_scalar(nmean_c[:], zsum[:], -ROOT / D, None, ALU.mult).then_inc(mean_done, 1)
                dve.wait_ge(rstd3_done, f + 1)
                for t in range(TILES):
                    dve.tensor_scalar(z[:, t, :], z[:, t, :], nmean[:, t:t + 1], rstd3[:, t:t + 1],
                                      ALU.add, ALU.mult).then_inc(x2_done, 1)

            split_x(0)

            def step(g, att=True, ffn=True, more=True):
                f = g - 1
                if att:
                    take_k(g)
                if ffn:
                    for t in range(TILES):
                        x1t_low(f, t)
                if att:
                    for t in range(TILES):
                        take_v(g, t)
                if ffn:
                    hidden_low(f, 0)
                    hidden_low(f, 1)
                if att:
                    for t in range(TILES):
                        soften(g, t)
                if ffn:
                    hidden_low(f, 2)
                if att:
                    take_ctx(g, 0)
                if ffn:
                    hidden_low(f, 3)
                if att:
                    take_ctx(g, 1)
                if ffn:
                    hidden_low(f, 4)
                if att:
                    for t in range(TILES):
                        ctxt_low(g, t)
                if ffn:
                    hidden_low(f, 5)
                if att:
                    for t in range(TILES):
                        take_y1(g, t)
                    if more:
                        split_x(g + 1)
                    for t in range(TILES):
                        scale_x1(g, t)
                if ffn:
                    for t in range(TILES):
                        take_y2(f, t)
                    finish(f)

            step(0, ffn=False)
            step(1)
            with dve.Fori(2, NG - 1) as g:
                step(g)
            step(NG - 1, more=False)
            step(NG, att=False)

        @block.gpsimd
        def _(pool):
            pool.memset(half[:], -0.5).then_inc(half_set, 1)
            pool.memset(eps_rms[:], EPS_RMS).then_inc(half_set, 1)
            pool.memset(eps_ln[:], EPS_LN).then_inc(half_set, 1)
            pool.wait_ge(half_set, 3)
            pool.wait_ge(const_loaded, 16 * N_CONST)

            def add_row(out, in_, row, t):
                return pool.tensor_tensor(out[:, t, :], in_[:, t, :], rows[row][:], ALU.add)

            def bias_x(g):
                pool.wait_ge(x_loaded, 16 * (g + 1))
                wait(pool, y1_done, TILES * g)
                for t in range(TILES):
                    r = add_row(x_bo, x_in, "bo", t)
                r.then_inc(xbo_done, 1)

            def root(mean_sq, ready, n, ms, eps, out, done, count):
                pool.wait_ge(ready, n)
                pool.tensor_tensor(ms[:], mean_sq[:], eps[:], ALU.add).then_inc(ms_done, 1)
                pool.wait_ge(ms_done, count)
                pool.tensor_tensor(out[:], ms[:], half[:], ALU.pow).then_inc(done, 1)

            def step(g, att=True, ffn=True, more=True):
                f = g - 1
                if att:
                    bias_x(g)
                    root(ssq1, sq1_done, TILES * (g + 1), ms1, eps_rms, rstd1, rstd1_done,
                         3 * g + 1 - (2 if ffn else 0))
                    for t in range(TILES):
                        pool.wait_ge(x1_scaled, TILES * g + t + 1)
                        add_row(x1, x1, "gamma1", t).then_inc(x1_done, 1)
                    done = 3 * g - 1
                else:
                    done = 3 * g - 2
                if ffn:
                    root(ssq2, sq2_done, TILES * (f + 1), ms2, eps_rms, rstd2, rstd2_done, done + 1)
                if att:
                    for t in range(TILES):
                        pool.wait_ge(x1_done, TILES * g + t + 1)
                        wait(pool, y2_done, TILES * (g - 1) + t + 1  )
                        add_row(x1_b2, x1, "b2", t).then_inc(x1b2_done, 1)
                if ffn:
                    root(ssq3, sq3_done, TILES * (f + 1), ms3, eps_ln, rstd3, rstd3_done, done + 2)
                if att:
                    wait(pool, z_done, TILES * g)
                    for t in range(TILES):
                        r = add_row(x_res, x_in, "gamma2", t)
                    r.then_inc(xres_done, 1)

            step(0, ffn=False)
            step(1)
            with pool.Fori(2, NG - 1) as g:
                step(g)
            step(NG - 1, more=False)
            step(NG, att=False)


def layer1(nc, x2, adj, w, out):
    VW = DH1 + 1
    VE = H1 // 2 * VW
    S = H1 * NODES
    with ExitStack() as ctx:
        def sb(name, shape, dt=F32):
            return ctx.enter_context(nc.sbuf_tensor(name, shape, dt))

        def sem(name):
            return ctx.enter_context(nc.semaphore(name))

        one = [ctx.enter_context(nc.psum_tensor(f"b_bank{i}", [P, 512], F32)) for i in range(4)]
        two = [ctx.enter_context(nc.psum_tensor(f"b_banks{i}", [P, 1024], F32)) for i in range(2)]

        names = ("Wq", "Wk", "Wv", "Wo")
        wide = {n: 2 * VE if n == "Wv" else D for n in names}
        W = {n: [sb(f"b_{n}_{s}", [P, KT, wide[n]], F32R) for s in ("hi", "lo")] for n in names}
        stage = {n: sb(f"b_stage_{n}", [P, KT, wide[n]]) for n in names}
        ident, mask = sb("b_ident", [P, P]), sb("b_mask", [P, NB1])
        half, eps_ln = sb("b_half", [P, TILES]), sb("b_eps_ln", [P, TILES])
        bo = sb("b_bo", [P, D])
        bv = sb("b_bv", [P, 2, H1 // 2, VW])

        x_in, res, y = sb("b_x", [P, TILES, D]), sb("b_res", [P, TILES, D]), sb("b_y", [P, TILES, D])
        adj_in, bias = sb("b_adj", [P, TILES, NODES]), sb("b_bias", [P, TILES, NODES])
        xt = [sb(f"b_xt_{s}", [P, KT, GROUP], F32R) for s in ("hi", "lo")]
        q = sb("b_q", [P, KT, GROUP])
        k_blocks = sb("b_k_blocks", [P, GB, NB1, NODES])
        v_nat, v_pairs = sb("b_v_nat", [P, TILES, 2 * VE]), sb("b_v_pairs", [P, GB, 2 * VE])
        prob, pt = sb("b_p", [P, TILES, S]), sb("b_pt", [P, TILES, S])
        ctxt = sb("b_ctx", [P, TILES, D])
        ctx_t = [sb(f"b_ctxt_{s}", [P, TILES, D], F32R) for s in ("hi", "lo")]
        smax, samax, rden = (sb(f"b_{n}", [P, TILES, H1]) for n in ("smax", "samax", "rden"))
        ysum, nmean, nmean_c, ssq = (sb(f"b_{n}", [P, TILES]) for n in ("ysum", "nmean", "nmean_c", "ssq"))
        var, rstd = sb("b_var", [P, TILES]), sb("b_rstd", [P, TILES])

        const_loaded, row_set, stage_set, pairs_zeroed = (sem("b_" + n) for n in (
            "const_loaded", "row_set", "stage_set", "pairs_zeroed"))
        w_loaded = {n: sem(f"b_{n}_loaded") for n in names}
        x_loaded, res_loaded, adj_loaded, out_stored = (sem("b_" + n) for n in (
            "x_loaded", "res_loaded", "adj_loaded", "out_stored"))
        v_swapped = [sem(f"b_v_swapped{t}") for t in range(TILES)]
        xt_mm, qk_mm, v_mm, s_mm, pt_mm, pv_mm, ct_mm, o_mm = (sem("b_" + n) for n in (
            "xt_mm", "qk_mm", "v_mm", "s_mm", "pt_mm", "pv_mm", "ct_mm", "o_mm"))
        w_hi, xt_hi, q_done, exp_done, pt_done, ctxt_hi = (sem("b_" + n) for n in (
            "w_hi", "xt_hi", "q_done", "exp_done", "pt_done", "ctxt_hi"))
        w_lo, xt_lo, k_done, v_done, biased, maxed, magnitude, rden_done, rden_masked, ctx_done, ctxt_lo = (
            sem("b_" + n) for n in ("w_lo", "xt_lo", "k_done", "v_done", "biased", "maxed", "magnitude", "rden_done",
                                    "rden_masked", "ctx_done", "ctxt_lo"))
        y_done, mean_done, out_done, sq_done = (sem("b_" + n) for n in ("y_done", "mean_done", "out_done", "sq_done"))
        half_set, bias_done, v_kept, shifted, var_done, rstd_done, res_done = (sem("b_" + n) for n in (
            "half_set", "bias_done", "v_kept", "shifted", "var_done", "rstd_done", "res_done"))
        N_CONST = 5

        block = ctx.enter_context(nc.Block())

        @block.sync
        def _(sp):
            def load_x(g):
                wait(sp, xt_mm, TILES * g)
                sp.dma_start(x_in[:], x2[g]).then_inc(x_loaded, 16)

            def load_res(g):
                wait(sp, y_done, TILES * g)
                sp.dma_start(res[:], x2[g]).then_inc(res_loaded, 16)

            def load_adj(g):
                wait(sp, bias_done, g)
                sp.dma_start(adj_in[:], adj[g]).then_inc(adj_loaded, 16)

            def swap_v(g, t):
                a, b = TILES * t, TILES * t + 1
                sp.wait_ge(v_done, TILES * g + t + 1)
                sp.dma_start(v_pairs[64:P, a, VE:2 * VE], v_nat[0:64, t, VE:2 * VE]).then_inc(v_swapped[t], 16)
                sp.dma_start(v_pairs[0:64, b, 0:VE], v_nat[64:P, t, 0:VE]).then_inc(v_swapped[t], 16)

            def store(g):
                sp.wait_ge(out_done, TILES * (g + 1))
                sp.dma_start(out[g], y[:]).then_inc(out_stored, 16)

            load_x(0)
            sp.dma_start(ident[:], w["ident"]).then_inc(const_loaded, 16)
            sp.dma_start(mask[:], w["mask1"]).then_inc(const_loaded, 16)
            for n in names:
                src = w[n].rearrange("(t p) c -> p t c", p=P)
                if n == "Wv":
                    sp.wait_ge(stage_set, 1)
                    dst = stage[n][:].rearrange("p k (r h c) -> p k r h c", r=2, h=H1 // 2)
                    src = src.rearrange("p k (h r d) -> p k r h d", r=2, d=DH1)
                    for k in range(KT):
                        for r in range(2):
                            sp.dma_start(dst[:, k, r, :, 0:DH1], src[:, k, r]).then_inc(w_loaded[n], 16)
                else:
                    sp.dma_start(stage[n][:], src).then_inc(w_loaded[n], 16)
            sp.dma_start(bo[:], w["bo1"].rearrange("(a d) -> a d", a=1).broadcast_to([P, D])).then_inc(const_loaded, 16)
            sp.wait_ge(row_set, 1)
            bv_row = w["bv1"].rearrange("(a h r d) -> a r h d", a=1, r=2, d=DH1)
            for r in range(2):
                sp.dma_start(bv[:, r, :, 0:DH1], bv_row[:, r].broadcast_to([P, H1 // 2, DH1])).then_inc(const_loaded, 16)
            load_adj(0)

            def step(g, front=True, back=True, more=True):
                if front and more:
                    load_x(g + 1)
                if back:
                    load_res(g - 1)
                if front:
                    for t in range(TILES):
                        swap_v(g, t)
                    if more:
                        load_adj(g + 1)
                if back:
                    store(g - 1)

            step(0, back=False)
            step(1)
            with sp.Fori(2, NG - 1) as g:
                step(g)
            step(NG - 1, more=False)
            step(NG, front=False)
            sp.wait_ge(out_stored, 16 * NG)

        @block.tensor
        def _(pe):
            def mm3(out, lhs, rhs, first, last):
                for n, (a, b) in enumerate(((0, 0), (1, 0), (0, 1))):
                    r = pe.matmul(out, lhs[a], rhs[b], start=first and n == 0, stop=last and n == 2)
                return r

            def turn_x(g, t):
                pe.wait_ge(x_loaded, 16 * (g + 1))
                wait(pe, k_done, g)
                for k in range(KT):
                    r = pe.transpose(one[1 + t][:, k * P:(k + 1) * P], x_in[:, t, k * P:(k + 1) * P], ident[:])
                r.then_inc(xt_mm, 1)

            def qk(g):
                pe.wait_ge(xt_lo, TILES * (g + 1))
                wait(pe, ctxt_lo, TILES * (g - 1))
                for u in range(3):
                    for s in range(2):
                        m = 2 * u + s
                        n, m = ("Wq", m) if m < KT else ("Wk", m - KT)
                        for k in range(KT):
                            r = mm3(one[u][:, s * GROUP:(s + 1) * GROUP],
                                    [W[n][j][:, k, m * P:(m + 1) * P] for j in range(2)],
                                    [xt[j][:, k, :] for j in range(2)], k == 0, k == KT - 1)
                    r.then_inc(qk_mm, 1)

            def values(g, t):
                if t == 0:
                    wait(pe, y_done, TILES * (g - 1))
                else:
                    pe.wait_ge(q_done, 2 * g + 1)
                out = one[3 if t == 0 else 0]
                for k in range(KT):
                    r = mm3(out[:, 0:2 * VE], [xt[j][:, k, t * P:(t + 1) * P] for j in range(2)],
                            [W["Wv"][j][:, k, :] for j in range(2)], k == 0, k == KT - 1)
                r.then_inc(v_mm, 1)

            def scores(g, t, back):
                pe.wait_ge(q_done, 2 * (g + 1))
                pe.wait_ge(k_done, g + 1)
                if back:
                    pe.wait_ge(pt_done, TILES * (g - 1) + t + 1)
                for k in range(KT):
                    b0, b1_, h = SPAN1[k]
                    for s in range(2):
                        n = TILES * t + s
                        r = pe.matmul(two[t][64 * s:64 * s + 64, h * NODES:(h + b1_ - b0) * NODES],
                                      q[:, k, n * NODES:(n + 1) * NODES],
                                      k_blocks[:, n, b0:b1_, :].rearrange("p b n -> p (b n)"),
                                      start=True, stop=True, skip_group_check=True)
                r.then_inc(s_mm, 1)

            def turn_p(g, t):
                pe.wait_ge(exp_done, TILES * g + t + 1)
                if t == 0:
                    wait(pe, y_done, TILES * g)
                for h in range(H1 // 2):
                    r = pe.transpose(two[t][:, h * P:(h + 1) * P], prob[:, t, h * P:(h + 1) * P], ident[:])
                r.then_inc(pt_mm, 1)

            def pv(g, t, front):
                pe.wait_ge(pt_done, TILES * g + t + 1)
                pe.wait_ge(v_swapped[t], 32 * (g + 1))
                pe.wait_ge(v_kept, TILES * g + t + 1)
                if front:
                    pe.wait_ge(*((q_done, 2 * (g + 2)) if t == 0 else (k_done, g + 2)))
                for s in range(2):
                    for h in range(H1 // 2):
                        n = TILES * t + s
                        vv = v_pairs[:, n, :].rearrange("p (r h c) -> p h r c", r=2, h=H1 // 2)[:, h]
                        r = pe.matmul(one[1 + t][64 * s:64 * s + 64, h * 2 * VW:(h + 1) * 2 * VW].rearrange("p (r c) -> p r c", r=2),
                                      pt[:, t, h * P + 64 * s:h * P + 64 * s + 64], vv, start=True, stop=True,
                                      skip_group_check=True)
                r.then_inc(pv_mm, 1)

            def turn_ctx(g, t, front):
                pe.wait_ge(ctx_done, TILES * g + t + 1)
                if front:
                    pe.wait_ge(v_done, TILES * (g + 1) + t + 1)
                for k in range(KT):
                    r = pe.transpose(one[3 if t == 0 else 0][:, k * P:(k + 1) * P], ctxt[:, t, k * P:(k + 1) * P], ident[:])
                r.then_inc(ct_mm, 1)

            def attn_out(g, t, front):
                pe.wait_ge(ctxt_lo, TILES * g + t + 1)
                if t == 1 and front:
                    pe.wait_ge(biased, TILES * (g + 1) + 1)
                o = one[3] if t == 0 else two[0]
                for k in range(KT):
                    r = mm3(o[:, 0:D], [ctx_t[j][:, t, k * P:(k + 1) * P] for j in range(2)],
                            [W["Wo"][j][:, k, :] for j in range(2)], k == 0, k == KT - 1)
                r.then_inc(o_mm, 1)

            pe.wait_ge(const_loaded, 16 * N_CONST)
            for t in range(TILES):
                turn_x(0, t)
            pe.wait_ge(w_lo, len(names))

            def step(g, front=True, back=True, more=True):
                b = g - 1
                if front:
                    qk(g)
                if back:
                    for t in range(TILES):
                        turn_p(b, t)
                for t in range(TILES):
                    if front:
                        values(g, t)
                    if back:
                        pv(b, t, front)
                if front:
                    scores(g, 0, back)
                if back:
                    for t in range(TILES):
                        turn_ctx(b, t, front)
                if front:
                    scores(g, 1, back)
                if front and more:
                    for t in range(TILES):
                        if back:
                            pe.wait_ge(ctx_done, TILES * b + t + 1)
                        turn_x(g + 1, t)
                if back:
                    for t in range(TILES):
                        attn_out(b, t, front)

            step(0, back=False)
            step(1)
            with pe.Fori(2, NG - 1) as g:
                step(g)
            step(NG - 1, more=False)
            step(NG, front=False)

        @block.scalar
        def _(act):
            for i, n in enumerate(names):
                act.wait_ge(w_loaded[n], 16 * (2 * KT if n == "Wv" else 1))
                act.activation(W[n][0][:], stage[n][:], ACT.Copy).then_inc(w_hi, 1)
            act.wait_ge(const_loaded, 16 * N_CONST)
            act.wait_ge(pairs_zeroed, 1)

            def xt_high(g, t):
                act.wait_ge(xt_mm, TILES * g + t + 1)
                wait(act, v_mm, TILES * g)
                act.activation(xt[0][:, :, t * P:(t + 1) * P], one[1 + t][:, 0:D].rearrange("p (k n) -> p k n", k=KT),
                               ACT.Copy).then_inc(xt_hi, 1)

            def take_q(g):
                wait(act, s_mm, TILES * g)
                act.wait_ge(qk_mm, 3 * g + 1)
                act.activation(q[:, 0:2, :].rearrange("p k n -> p (k n)"), one[0][:], ACT.Copy).then_inc(q_done, 1)
                act.wait_ge(qk_mm, 3 * g + 2)
                act.activation(q[:, 2, :], one[1][:, 0:GROUP], ACT.Copy)
                for b in range(*SPAN1[0][:2]):
                    r = act.activation(k_blocks[:, :, b, :], one[1][:, GROUP:2 * GROUP].rearrange("p (g n) -> p g n", g=GB),
                                       ACT.Copy, scale=mask[:, b:b + 1])
                r.then_inc(q_done, 1)

            def keep_v(g, t):
                a, b = TILES * t, TILES * t + 1
                act.wait_ge(v_done, TILES * g + t + 1)
                act.activation(v_pairs[0:64, a, 0:VE], v_nat[0:64, t, 0:VE], ACT.Copy)
                act.activation(v_pairs[64:P, b, VE:2 * VE], v_nat[64:P, t, VE:2 * VE], ACT.Copy).then_inc(v_kept, 1)

            def exp(g, t):
                act.wait_ge(shifted, TILES * g + t + 1)
                act.activation(prob[:, t, :], prob[:, t, :], ACT.Exp).then_inc(exp_done, 1)

            def take_pt(g, t):
                act.wait_ge(pt_mm, TILES * g + t + 1)
                wait(act, pv_mm, TILES * (g - 1) + t + 1)
                act.activation(pt[:, t, :], two[t][:, 0:S], ACT.Copy).then_inc(pt_done, 1)

            def ctxt_high(g, t):
                act.wait_ge(ct_mm, TILES * g + t + 1)
                wait(act, o_mm, TILES * (g - 1) + t + 1)
                act.activation(ctx_t[0][:, t, :], one[3 if t == 0 else 0][:, 0:D], ACT.Copy).then_inc(ctxt_hi, 1)

            def square(g, t):
                act.wait_ge(mean_done, 2 * (g + 1))
                act.activation(ctxt[:, t, :], y[:, t, :], ACT.Square, bias=nmean_c[:, t:t + 1], scale=ROOT,
                               accum_out=ssq[:, t:t + 1]).then_inc(sq_done, 1)

            for t in range(TILES):
                xt_high(0, t)

            def step(g, front=True, back=True, more=True):
                b = g - 1
                if back:
                    exp(b, 1)
                    take_pt(b, 0)
                if front:
                    take_q(g)
                if back:
                    take_pt(b, 1)
                if front:
                    for t in range(TILES):
                        keep_v(g, t)
                if back:
                    for t in range(TILES):
                        ctxt_high(b, t)
                if front and more:
                    for t in range(TILES):
                        xt_high(g + 1, t)
                if front:
                    exp(g, 0)
                if back:
                    for t in range(TILES):
                        square(b, t)

            step(0, back=False)
            step(1)
            with act.Fori(2, NG - 1) as g:
                step(g)
            step(NG - 1, more=False)
            step(NG, front=False)

        @block.vector
        def _(dve):
            dve.memset(bv[:], 1.0).then_inc(row_set, 1)
            dve.memset(stage["Wv"][:], 0.0).then_inc(stage_set, 1)
            dve.memset(v_pairs[:], 0.0).then_inc(pairs_zeroed, 1)
            for i, n in enumerate(names):
                dve.wait_ge(w_hi, i + 1)
                dve.tensor_tensor(W[n][1][:], stage[n][:], W[n][0][:].bitcast(F32), ALU.subtract).then_inc(w_lo, 1)
            dve.wait_ge(const_loaded, 16 * N_CONST)

            def xt_low(g, t):
                dve.wait_ge(xt_hi, TILES * g + t + 1)
                hi, lo = (xt[j][:, :, t * P:(t + 1) * P] for j in range(2))
                dve.tensor_tensor(lo, one[1 + t][:, 0:D].rearrange("p (k n) -> p k n", k=KT), hi.bitcast(F32),
                                  ALU.subtract).then_inc(xt_lo, 1)

            def take_k(g):
                dve.wait_ge(qk_mm, 3 * g + 3)
                wait(dve, s_mm, TILES * g)
                for k in (1, 2):
                    for b in range(*SPAN1[k][:2]):
                        r = dve.tensor_scalar(k_blocks[:, :, b, :],
                                              one[2][:, (k - 1) * GROUP:k * GROUP].rearrange("p (g n) -> p g n", g=GB),
                                              mask[:, b:b + 1], None, ALU.mult)
                r.then_inc(k_done, 1)

            def take_v(g, t):
                dve.wait_ge(v_mm, TILES * g + t + 1)
                wait(dve, v_swapped[t], 32 * g)
                wait(dve, v_kept, TILES * (g - 1) + t + 1)
                wait(dve, pv_mm, TILES * (g - 1) + t + 1)
                dve.tensor_tensor(v_nat[:, t, :], one[3 if t == 0 else 0][:, 0:2 * VE],
                                  bv[:].rearrange("p r h c -> p (r h c)"), ALU.add).then_inc(v_done, 1)

            def soften(g, t):
                s = prob[:, t, :].rearrange("p (h n) -> p h n", h=H1)
                dve.wait_ge(s_mm, TILES * g + t + 1)
                if t == 0:
                    dve.wait_ge(bias_done, g + 1)
                wait(dve, pt_mm, TILES * (g - 1) + t + 1)
                dve.scalar_tensor_tensor(out=s, in0=two[t][:, 0:S].rearrange("p (h n) -> p h n", h=H1), scalar=SCALE1,
                                         in1=bias[:, t, :].unsqueeze(1).broadcast_to([P, H1, NODES]),
                                         op0=ALU.mult, op1=ALU.add).then_inc(biased, 1)
                dve.wait_ge(biased, TILES * g + t + 1)
                dve.tensor_reduce(smax[:, t, :], s, AX_X, ALU.max).then_inc(maxed, 1)
                wait(dve, rden_masked, TILES * (g - 1) + t + 1)
                dve.tensor_reduce(samax[:, t, :], s, AX_X, ALU.max, apply_absolute_value=True).then_inc(magnitude, 1)

            def take_ctx(g, t):
                o = one[1 + t][:, 0:2 * VE].rearrange("p (h c) -> p h c", c=VW)
                dve.wait_ge(pv_mm, TILES * g + t + 1)
                dve.reciprocal(rden[:, t, :], o[:, :, DH1]).then_inc(rden_done, 1)
                dve.wait_ge(rden_done, TILES * g + t + 1)
                dve.wait_ge(magnitude, TILES * g + t + 1)
                dve.scalar_tensor_tensor(out=rden[:, t, :], in0=samax[:, t, :], scalar=0.0, in1=rden[:, t, :],
                                         op0=ALU.is_gt, op1=ALU.mult).then_inc(rden_masked, 1)
                dve.wait_ge(rden_masked, TILES * g + t + 1)
                wait(dve, ct_mm, TILES * (g - 1) + t + 1)
                dve.tensor_tensor(ctxt[:, t, :].rearrange("p (h c) -> p h c", h=H1), o[:, :, 0:DH1],
                                  rden[:, t, :].unsqueeze(2).broadcast_to([P, H1, DH1]), ALU.mult).then_inc(ctx_done, 1)

            def ctxt_low(g, t):
                dve.wait_ge(ctxt_hi, TILES * g + t + 1)
                dve.tensor_tensor(ctx_t[1][:, t, :], one[3 if t == 0 else 0][:, 0:D], ctx_t[0][:, t, :].bitcast(F32),
                                  ALU.subtract).then_inc(ctxt_lo, 1)

            def finish(g):
                dve.wait_ge(res_done, g + 1)
                wait(dve, out_stored, 16 * g)
                for t in range(TILES):
                    dve.wait_ge(o_mm, TILES * g + t + 1)
                    o = one[3] if t == 0 else two[0]
                    dve.scalar_tensor_tensor(out=y[:, t, :], in0=o[:, 0:D], scalar=1.0, in1=res[:, t, :], op0=ALU.mult,
                                             op1=ALU.add, accum_out=ysum[:, t:t + 1]).then_inc(y_done, 1)
                dve.wait_ge(y_done, TILES * (g + 1))
                dve.tensor_scalar(nmean[:], ysum[:], -1.0 / D, None, ALU.mult).then_inc(mean_done, 1)
                dve.tensor_scalar(nmean_c[:], ysum[:], -ROOT / D, None, ALU.mult).then_inc(mean_done, 1)

            def norm(g):
                dve.wait_ge(rstd_done, g + 1)
                for t in range(TILES):
                    dve.tensor_scalar(y[:, t, :], y[:, t, :], nmean[:, t:t + 1], rstd[:, t:t + 1],
                                      ALU.add, ALU.mult).then_inc(out_done, 1)

            for t in range(TILES):
                xt_low(0, t)

            def step(g, front=True, back=True, more=True):
                b = g - 1
                if front:
                    take_k(g)
                    for t in range(TILES):
                        take_v(g, t)
                if back:
                    for t in range(TILES):
                        take_ctx(b, t)
                if front:
                    soften(g, 0)
                if back:
                    for t in range(TILES):
                        ctxt_low(b, t)
                if front and more:
                    for t in range(TILES):
                        xt_low(g + 1, t)
                if front:
                    soften(g, 1)
                if back:
                    finish(b)
                    norm(b)

            step(0, back=False)
            step(1)
            with dve.Fori(2, NG - 1) as g:
                step(g)
            step(NG - 1, more=False)
            step(NG, front=False)

        @block.gpsimd
        def _(pool):
            pool.memset(half[:], -0.5).then_inc(half_set, 1)
            pool.memset(eps_ln[:], EPS_LN).then_inc(half_set, 1)
            pool.wait_ge(half_set, 2)
            pool.wait_ge(const_loaded, 16 * N_CONST)

            def double_adj(g):
                pool.wait_ge(adj_loaded, 16 * (g + 1))
                wait(pool, biased, TILES * g)
                pool.tensor_tensor(bias[:], adj_in[:], adj_in[:], ALU.add).then_inc(bias_done, 1)

            def bias_res(g):
                pool.wait_ge(res_loaded, 16 * (g + 1))
                for t in range(TILES):
                    r = pool.tensor_tensor(res[:, t, :], res[:, t, :], bo[:], ALU.add)
                r.then_inc(res_done, 1)

            def shift(g, t):
                s = prob[:, t, :].rearrange("p (h n) -> p h n", h=H1)
                pool.wait_ge(maxed, TILES * g + t + 1)
                pool.wait_ge(magnitude, TILES * g + t + 1)
                pool.tensor_tensor(s, s, smax[:, t, :].unsqueeze(2).broadcast_to([P, H1, NODES]),
                                   ALU.subtract).then_inc(shifted, 1)

            def root(g):
                pool.wait_ge(sq_done, TILES * (g + 1))
                pool.tensor_tensor(var[:], ssq[:], eps_ln[:], ALU.add).then_inc(var_done, 1)
                pool.wait_ge(var_done, g + 1)
                pool.tensor_tensor(rstd[:], var[:], half[:], ALU.pow).then_inc(rstd_done, 1)

            def step(g, front=True, back=True, more=True):
                if front:
                    double_adj(g)
                if back:
                    bias_res(g - 1)
                if front:
                    for t in range(TILES):
                        shift(g, t)
                if back:
                    root(g - 1)

            step(0, back=False)
            step(1)
            with pool.Fori(2, NG - 1) as g:
                step(g)
            step(NG - 1, more=False)
            step(NG, front=False)


def program(nc, a, out):
    x2 = nc.dram_tensor("x2", (TOKENS, D), F32).ap()

    def groups(ap):
        return ap.rearrange("(g t p) d -> g p t d", t=TILES, p=P)

    xT = a["xT"].rearrange("(k p) (g n) -> k g p n", p=P, n=GROUP)
    w0 = {n: a[f"L0_gnn_{n}"] for n in ("wq", "bq", "wk", "bk", "wv", "bv", "wo", "bo", "w1", "b1", "w2", "b2",
                                        "alpha1", "gamma1", "alpha2", "gamma2")}
    w0 |= {"ident": a["ident"], "mask0": a["mask0"]}
    w1 = {n: a[f"L1_gnn_{n}"] for n in ("Wq", "Wk", "Wv", "Wo")}
    w1 |= {"bv1": a["L1_gnn_bv"], "bo1": a["L1_gnn_bo"], "ident": a["ident"], "mask1": a["mask1"]}
    layer0(nc, groups(a["x"]), xT, groups(a["adj"]), w0, groups(x2))
    layer1(nc, groups(x2), groups(a["adj"]), w1, groups(out))


def kernel(**inputs):
    import numpy as np
    import concourse.bacc as bacc
    from concourse.bass_utils import run_bass_kernel_spmd

    def block_mask(heads, blocks):
        rows = np.arange(P)[:, None]
        tile = np.array([t for t, _ in blocks])[None, :]
        head = np.array([h for _, h in blocks])[None, :]
        return ((rows + P * tile) // (D // heads) == head).astype(np.float32)

    host = {}
    for name, value in inputs.items():
        value = np.asarray(value)
        if name in ("x", "adj"):
            value = value.reshape(TOKENS, -1)
        elif name.startswith("L1_gnn_W"):
            value = value.T
        elif name in ("L0_gnn_bq", "L0_gnn_bk", "L0_gnn_b1"):
            value = value.reshape(-1, P).T
        host[name] = np.ascontiguousarray(value)
    host["xT"] = np.ascontiguousarray(host["x"].T)
    host["ident"] = np.eye(P, dtype=np.float32)
    host["mask0"] = block_mask(H0, BLOCKS0)
    host["mask1"] = block_mask(H1, BLOCKS1)

    nc = bacc.Bacc("TRN2", target_bir_lowering=False, num_devices=1, dynamic_dma_scratch_size=8192)
    arrays, args = {}, {}
    for name, value in host.items():
        arrays[f"in_{name}"] = value
        args[name] = nc.dram_tensor(f"in_{name}", value.shape, F32, kind="ExternalInput").ap()
    out = nc.dram_tensor("out", (TOKENS, D), F32, kind="ExternalOutput").ap()
    program(nc, args, out)
    r = run_bass_kernel_spmd(nc, [arrays], core_ids=[0])
    return np.asarray(r.results[0]["out"]).reshape(GRAPHS, NODES, D)
```

```python
from contextlib import ExitStack

import concourse.bass as bass
from concourse import mybir

F32 = mybir.dt.float32
F32R = mybir.dt.float32r
ALU = mybir.AluOpType
ACT = mybir.ActivationFunctionType
AX_X = mybir.AxisListType.X

P = 128
GRAPHS, NODES, D = 128, 64, 384
TOKENS = GRAPHS * NODES
TILES = 2
GROUP = TILES * P
GB = GROUP // NODES
NG = TOKENS // GROUP
KT = D // P
H0, H1 = 8, 12
DH0, DH1 = D // H0, D // H1
F = 1536
FC = F // P
FP = FC // 2
RING = 3
EPS_RMS, EPS_LN = 1e-6, 1e-5
ROOT = float(D) ** -0.5
SCALE0, SCALE1 = float(DH0) ** -0.5, float(D) ** -0.5


def head_blocks(heads):
    dh = D // heads
    blocks, span = [], []
    for t in range(KT):
        own = [h for h in range(heads) if h * dh < (t + 1) * P and (h + 1) * dh > t * P]
        span.append((len(blocks), len(blocks) + len(own), own[0]))
        blocks += [(t, h) for h in own]
    return blocks, span


BLOCKS0, SPAN0 = head_blocks(H0)
BLOCKS1, SPAN1 = head_blocks(H1)
NB0, NB1 = len(BLOCKS0), len(BLOCKS1)


def wait(eng, sem, value):
    if not isinstance(value, int) or value > 0:
        eng.wait_ge(sem, value)


def layer0(nc, x, xT, adj, w, w_next, x2, shared):
    VW = DH0 + 1
    VE = H0 // 2 * VW
    with ExitStack() as ctx:
        def sb(name, shape, dt=F32):
            return ctx.enter_context(nc.sbuf_tensor(name, shape, dt))

        def sem(name):
            return ctx.enter_context(nc.semaphore(name))

        bank = [ctx.enter_context(nc.psum_tensor(f"a_bank{i}", [P, 512], F32)) for i in range(8)]
        A, B, ACC = bank[0:3], bank[3:6], bank[6:8]

        wide = {"wq": D, "wk": D, "wv": 2 * VE, "wo": D, "w1": F, "w2": D}
        tall = {n: FC if n == "w2" else KT for n in wide}
        W = {n: [sb(f"a_{n}_{s}", [P, tall[n], wide[n]], F32R) for s in ("hi", "lo")] for n in ("w1", "w2")}
        attn_W, ident = shared["W"], shared["ident"]
        for n in ("wq", "wk", "wv", "wo"):
            W[n] = [part[:, :, 0:wide[n]] for part in attn_W[n]]
        rows = {n: sb(f"a_{n}", [P, D]) for n in ("bo", "alpha1", "gamma1", "b2", "alpha2", "gamma2")}
        bv = sb("a_bv", [P, 2, H0 // 2, VW])
        mask = sb("a_mask", [P, NB0])
        kbias = sb("a_kbias", [P, NB0])
        bq, bk, b1 = sb("a_bq", [P, KT]), sb("a_bk", [P, KT]), sb("a_b1", [P, FC])
        half, eps_rms, eps_ln = (sb(f"a_{n}", [P, TILES]) for n in ("half", "eps_rms", "eps_ln"))

        sizes = [("xt_raw", KT * GROUP), ("x_bo", TILES * D), ("x_res", TILES * D),
                 ("q", KT * GROUP), ("k_blocks", GB * NB0 * NODES), ("v_nat", TILES * 2 * VE),
                 ("v_pairs", GB * 2 * VE), ("p", TILES * H0 * NODES), ("pt", TILES * H0 * NODES),
                 ("ctx", TILES * D), ("x1", TILES * D), ("x1_b2", TILES * D), ("silu", 2 * 512),
                 ("z", TILES * D)]
        work = sb("a_work", [P, sum(n for _, n in sizes)])
        at, v = 0, {}
        for name, n in sizes:
            v[name] = work[:, at:at + n]
            at += n
        STAGE_AT = sum(n for name, n in sizes[:[name for name, _ in sizes].index("q")])
        xt_raw = v["xt_raw"]
        x_bo, x_res, ctxt, x1, x1_b2, z = (
            v[n].rearrange("p (t d) -> p t d", t=TILES) for n in ("x_bo", "x_res", "ctx", "x1", "x1_b2", "z"))
        q = v["q"].rearrange("p (k n) -> p k n", k=KT)
        k_blocks = v["k_blocks"].rearrange("p (g b n) -> p g b n", g=GB, b=NB0)
        v_nat = v["v_nat"].rearrange("p (t c) -> p t c", t=TILES)
        v_pairs = v["v_pairs"].rearrange("p (g c) -> p g c", g=GB)
        prob = v["p"].rearrange("p (t c) -> p t c", t=TILES)
        pt = v["pt"].rearrange("p (t c) -> p t c", t=TILES)
        silu = v["silu"].rearrange("p (s c) -> p s c", s=2)

        adj_in = sb("a_adj", [P, TILES, NODES])
        xt = [sb(f"a_xt_{s}", [P, KT, GROUP], F32R) for s in ("hi", "lo")]
        ctx_t = [sb(f"a_ctxt_{s}", [P, TILES, D], F32R) for s in ("hi", "lo")]
        x1_t = [sb(f"a_x1t_{s}", [P, KT, GROUP], F32R) for s in ("hi", "lo")]
        hid = [sb(f"a_hid_{s}", [P, RING, 512], F32R) for s in ("hi", "lo")]
        smax = sb("a_smax", [P, TILES, H0])
        rden = sb("a_rden", [P, TILES, H0])
        ssq1, ssq2, ssq3 = (sb(f"a_ssq{i}", [P, TILES]) for i in (1, 2, 3))
        ms1, ms2, ms3 = (sb(f"a_ms{i}", [P, TILES]) for i in (1, 2, 3))
        rstd1, rstd2, rstd3 = (sb(f"a_rstd{i}", [P, TILES]) for i in (1, 2, 3))
        zsum, nmean, nmean_c = (sb(f"a_{n}", [P, TILES]) for n in ("zsum", "nmean", "nmean_c"))

        const_loaded, row_set = sem("const_loaded"), sem("row_set")
        xt_loaded, x_loaded, res_loaded, adj_loaded, x2_stored = (
            sem(n) for n in ("xt_loaded", "x_loaded", "res_loaded", "adj_loaded", "x2_stored"))
        v_swapped = [sem(f"v_swapped{t}") for t in range(TILES)]
        stage_set, pairs_zeroed = sem("stage_set"), sem("pairs_zeroed")
        qk_mm, v_mm, s_mm, pt_mm, pv_mm, ct_mm, o_mm, x1t_mm, f1_mm, f2_mm = (
            sem(n) for n in ("qk_mm", "v_mm", "s_mm", "pt_mm", "pv_mm", "ct_mm", "o_mm", "x1t_mm", "f1_mm", "f2_mm"))
        w_hi, xt_hi, q_done, x1t_hi, silu_done, hid_hi, exp_done, pt_done, ctxt_hi, sq1_done, sq2_done, sq3_done = (
            sem(n) for n in ("w_hi", "xt_hi", "q_done", "x1t_hi", "silu_done", "hid_hi", "exp_done", "pt_done",
                             "ctxt_hi", "sq1_done", "sq2_done", "sq3_done"))
        w_lo, kbias_set, xt_lo, k_done, x1t_lo, v_done, hid_lo, biased, maxed, shifted, rden_done, ctx_done = (
            sem(n) for n in ("w_lo", "kbias_set", "xt_lo", "k_done", "x1t_lo", "v_done", "hid_lo", "biased", "maxed",
                             "shifted", "rden_done", "ctx_done"))
        ctxt_lo, y1_done, x1_scaled, y2_done, z_scaled, z_done, mean_done, x2_done = (
            sem(n) for n in ("ctxt_lo", "y1_done", "x1_scaled", "y2_done", "z_scaled", "z_done", "mean_done",
                             "x2_done"))
        half_set, xbo_done, v_kept, rstd1_done, x1_done, x1b2_done, rstd2_done, rstd3_done, xres_done = (
            sem(n) for n in ("half_set", "xbo_done", "v_kept", "rstd1_done", "x1_done", "x1b2_done",
                             "rstd2_done", "rstd3_done", "xres_done"))
        ms1_done, ms2_done, ms3_done = (sem(f"ms{i}_done") for i in (1, 2, 3))

        SLOT = KT * 2 * shared["VE1"]
        first = [(n, w[n], attn_W[n], 0, KT, wide[n], i) for i, n in enumerate(("wq", "wk", "wv", "wo"))]
        spare = [v["silu"][:, 0:512], v["silu"][:, 512:1024], v["z"][:, 0:512], v["x_res"][:, 0:512]]
        second = [("w1", w["w1"], t, c, 512) for t in range(KT) for c in range(0, F, 512)]
        second += [("w2", w["w2"], t, 0, D) for t in range(FC)]
        third = [(n, w_next[m], attn_W[n], 0, KT, 2 * shared["VE1"] if n == "wv" else D, i)
                 for i, (n, m) in enumerate(zip(("wq", "wk", "wv", "wo"), ("Wq", "Wk", "Wv", "Wo")))]
        first_loaded = [sem(f"first_loaded{i}") for i in range(4)]
        second_loaded = [sem(f"second_loaded{i}") for i in range(len(spare))]
        third_loaded = [sem(f"third_loaded{i}") for i in range(4)]
        second_hi, second_lo, third_hi, third_lo, third_set = (
            sem(n) for n in ("second_hi", "second_lo", "third_hi", "third_lo", "third_set"))

        def stage(piece):
            return work[:, STAGE_AT + piece[6] * SLOT:STAGE_AT + piece[6] * SLOT + KT * piece[5]]

        def load_piece(sp, piece, loaded, dh):
            name, dram, _, t, k, cols, _ = piece
            src = dram.rearrange("(t p) c -> p t c", p=P)
            dst = stage(piece).rearrange("p (k c) -> p k c", k=KT)
            if name != "wv":
                sp.dma_start(dst, src).then_inc(loaded, 16)
                return
            dst = stage(piece).rearrange("p (k r h c) -> p k r h c", k=KT, r=2, c=dh + 1)
            src = src.rearrange("p k (h r d) -> p k r h d", r=2, d=dh)
            for kk in range(KT):
                for r in range(2):
                    sp.dma_start(dst[:, kk, r, :, 0:dh], src[:, kk, r]).then_inc(loaded, 16)

        def pieces_of(piece):
            return 16 * (2 * KT if piece[0] == "wv" else 1)

        def halves(piece, s):
            return piece[2][s][:, :, 0:piece[5]]

        def part(i, s):
            name, _, t, c, n = second[i]
            return W[name][s][:, t, c:c + n]

        SECOND = (range(0, 8), range(8, 16), range(16, len(second)))

        N_CONST = 7 + len(rows) + 4

        block = ctx.enter_context(nc.Block())

        @block.sync
        def _(sp):
            def load_xt(g):
                wait(sp, xt_lo, g)
                for k in range(KT):
                    sp.dma_start(xt_raw[:, k * GROUP:(k + 1) * GROUP], xT[k, g]).then_inc(xt_loaded, 16)

            def load_adj(g):
                wait(sp, biased, TILES * g)
                sp.dma_start(adj_in[:], adj[g]).then_inc(adj_loaded, 16)

            def load_x(g):
                wait(sp, y1_done, TILES * g)
                sp.dma_start(x_bo, x[g]).then_inc(x_loaded, 16)

            def load_res(g):
                wait(sp, z_done, TILES * g)
                if isinstance(g, int) and g == 0:
                    sp.wait_ge(second_lo, len(second))
                sp.dma_start(x_res, x[g]).then_inc(res_loaded, 16)

            def swap_v(g, t):
                a, b = TILES * t, TILES * t + 1
                sp.wait_ge(v_done, TILES * g + t + 1)
                sp.dma_start(v_pairs[64:P, a, VE:2 * VE], v_nat[0:64, t, VE:2 * VE]).then_inc(v_swapped[t], 16)
                sp.dma_start(v_pairs[0:64, b, 0:VE], v_nat[64:P, t, 0:VE]).then_inc(v_swapped[t], 16)

            def store(g):
                sp.wait_ge(x2_done, TILES * (g + 1))
                sp.dma_start(x2[g], z).then_inc(x2_stored, 16)

            load_xt(0)
            for i, piece in enumerate(first):
                if piece[0] == "wv":
                    sp.wait_ge(stage_set, 1)
                load_piece(sp, piece, first_loaded[i], DH0)
                if i == 1:
                    sp.dma_start(ident[:], w["ident"]).then_inc(const_loaded, 16)
                    sp.dma_start(mask[:], w["mask0"]).then_inc(const_loaded, 16)
                    sp.dma_start(shared["mask"][:], w["mask1"]).then_inc(const_loaded, 16)
                    sp.dma_start(shared["bo"][:], w["bo1"].rearrange("(a d) -> a d", a=1).broadcast_to([P, D])).then_inc(const_loaded, 16)
                    for dst, name in ((bq, "bq"), (bk, "bk"), (b1, "b1")):
                        sp.dma_start(dst[:], w[name]).then_inc(const_loaded, 16)
                    for name in rows:
                        sp.dma_start(rows[name][:], w[name].rearrange("(a d) -> a d", a=1).broadcast_to([P, D])).then_inc(const_loaded, 16)
                    sp.wait_ge(row_set, 1)
                    for row, name, dh, heads in ((bv, "bv", DH0, H0), (shared["bv"], "bv1", DH1, H1)):
                        src = w[name].rearrange("(a h r d) -> a r h d", a=1, r=2, d=dh)
                        for r in range(2):
                            sp.dma_start(row[:, r, :, 0:dh], src[:, r].broadcast_to([P, heads // 2, dh])).then_inc(const_loaded, 16)
            sp.wait_ge(w_lo, len(first))
            load_adj(0)
            load_x(0)

            def load_second(parts):
                for i in parts:
                    _, dram, t, c, n = second[i]
                    s = i % len(spare)
                    if i >= len(spare):
                        sp.wait_ge(second_lo, i - len(spare) + 1)
                    sp.dma_start(spare[s][:, 0:n], dram[t * P:(t + 1) * P, c:c + n]).then_inc(second_loaded[s], 16)

            def load_third():
                sp.wait_ge(third_set, 1)
                for i, piece in enumerate(third):
                    load_piece(sp, piece, third_loaded[i], DH1)

            def step(g, att=True, ffn=True, late=True, more=True):
                if att:
                    if more:
                        load_xt(g + 1)
                    if not ffn:
                        load_second(SECOND[0])
                    for t in range(TILES):
                        swap_v(g, t)
                    if not ffn:
                        load_second(range(SECOND[1][0], len(second)))
                    if more:
                        load_adj(g + 1)
                elif ffn:
                    load_third()
                if late:
                    store(g - 2)
                if ffn:
                    load_res(g - 1)
                if att and more:
                    load_x(g + 1)

            step(0, ffn=False, late=False)
            step(1, late=False)
            with sp.Fori(2, NG - 1) as g:
                step(g)
            step(NG - 1, more=False)
            step(NG, att=False)
            step(NG + 1, att=False, ffn=False)
            sp.wait_ge(x2_stored, 16 * NG)

        @block.tensor
        def _(pe):
            def mm3(out, lhs, rhs, first, last):
                for n, (a, b) in enumerate(((0, 0), (1, 0), (0, 1))):
                    r = pe.matmul(out, lhs[a], rhs[b], start=first and n == 0, stop=last and n == 2)
                return r

            def qk(g):
                wait(pe, xt_lo, g + 1)
                for u in range(3):
                    if isinstance(g, int) and g == 0:
                        pe.wait_ge(w_lo, 1 if u == 0 else 2)
                    if isinstance(g, int) and g == 1:
                        pe.wait_ge(*((q_done, u + 1) if u < 2 else (k_done, 1)))
                    elif not isinstance(g, int) or g > 1:
                        pe.wait_ge(silu_done, FP * (g - 1) - 2 + u)
                    for s in range(2):
                        m = 2 * u + s
                        n, m = ("wq", m) if m < KT else ("wk", m - KT)
                        for k in range(KT):
                            r = mm3(A[u][:, s * GROUP:(s + 1) * GROUP],
                                    [W[n][j][:, k, m * P:(m + 1) * P] for j in range(2)],
                                    [xt[j][:, k, :] for j in range(2)], k == 0, k == KT - 1)
                    r.then_inc(qk_mm, 1)

            def values(g, t, ffn):
                if isinstance(g, int) and g == 0:
                    pe.wait_ge(w_lo, 3)
                if t == 0:
                    wait(pe, ctxt_lo, TILES * g)
                elif ffn:
                    pe.wait_ge(x1t_lo, TILES * (g - 1) + 1)
                out = B[2 if t == 0 else 0]
                for k in range(KT):
                    r = mm3(out[:, 0:2 * VE], [xt[j][:, k, t * P:(t + 1) * P] for j in range(2)],
                            [W["wv"][j][:, k, :] for j in range(2)], k == 0, k == KT - 1)
                r.then_inc(v_mm, 1)

            def scores(g, t, ffn):
                if t == 0:
                    pe.wait_ge(q_done, 2 * (g + 1))
                    pe.wait_ge(k_done, g + 1)
                    if ffn:
                        pe.wait_ge(x1t_lo, TILES * g)
                else:
                    pe.wait_ge(v_done, TILES * g + 1)
                out = B[1 + t]
                for k in range(KT):
                    b0, b1_, h = SPAN0[k]
                    for s in range(2):
                        n = TILES * t + s
                        r = pe.matmul(out[64 * s:64 * s + 64, h * NODES:(h + b1_ - b0) * NODES],
                                      q[:, k, n * NODES:(n + 1) * NODES],
                                      k_blocks[:, n, b0:b1_, :].rearrange("p b n -> p (b n)"),
                                      start=k == 0, stop=k == KT - 1, skip_group_check=True)
                r.then_inc(s_mm, 1)

            def turn_p(g, t):
                if isinstance(g, int) and g == 0:
                    pe.wait_ge(const_loaded, 16 * N_CONST)
                pe.wait_ge(exp_done, TILES * g + t + 1)
                if t == 0:
                    pe.wait_ge(v_done, TILES * g + 2)
                for h in range(H0 // 2):
                    r = pe.transpose(B[2 * t][:, h * P:(h + 1) * P], prob[:, t, h * P:(h + 1) * P], ident[:])
                r.then_inc(pt_mm, 1)

            def pv(g, t):
                pe.wait_ge(pt_done, TILES * g + t + 1)
                pe.wait_ge(v_swapped[t], 32 * (g + 1))
                pe.wait_ge(v_kept, TILES * g + t + 1)
                if t == 0:
                    pe.wait_ge(biased, TILES * g + 1)
                out = B[1 - t]
                for h in range(H0 // 2):
                    for s in range(2):
                        n = TILES * t + s
                        vv = v_pairs[:, n, :].rearrange("p (r h c) -> p h r c", r=2, h=H0 // 2)[:, h]
                        r = pe.matmul(out[64 * s:64 * s + 64, h * 2 * VW:(h + 1) * 2 * VW].rearrange("p (r c) -> p r c", r=2),
                                      pt[:, t, h * P + 64 * s:h * P + 64 * s + 64], vv, start=True, stop=True,
                                      skip_group_check=True)
                r.then_inc(pv_mm, 1)

            def turn_ctx(g, t):
                pe.wait_ge(ctx_done, TILES * g + t + 1)
                if t == 1:
                    pe.wait_ge(pt_done, TILES * g + 2)
                for k in range(KT):
                    r = pe.transpose(B[1 + t][:, k * P:(k + 1) * P], ctxt[:, t, k * P:(k + 1) * P], ident[:])
                r.then_inc(ct_mm, 1)

            def attn_out(g, t):
                if isinstance(g, int) and g == 0:
                    pe.wait_ge(w_lo, 4)
                pe.wait_ge(ctxt_lo, TILES * g + t + 1)
                if t == 0:
                    pe.wait_ge(ctx_done, TILES * g + 2)
                for k in range(KT):
                    r = mm3(B[t][:, 0:D], [ctx_t[j][:, t, k * P:(k + 1) * P] for j in range(2)],
                            [W["wo"][j][:, k, :] for j in range(2)], k == 0, k == KT - 1)
                r.then_inc(o_mm, 1)

            def turn_x1(f, t):
                pe.wait_ge(x1_done, TILES * f + t + 1)
                for k in range(KT):
                    r = pe.transpose(B[t][:, k * P:(k + 1) * P], x1[:, t, k * P:(k + 1) * P], ident[:])
                r.then_inc(x1t_mm, 1)

            def ffn1(f, p, att):
                if isinstance(f, int) and f == 0 and p == 0:
                    pe.wait_ge(second_lo, len(second))
                if p == 0:
                    pe.wait_ge(x1t_lo, TILES * (f + 1))
                if p < 3 and att:
                    pe.wait_ge(*((q_done, 2 * (f + 1) + p + 1) if p < 2 else (k_done, f + 2)))
                else:
                    pe.wait_ge(silu_done, FP * f + p - 2)
                for s in range(2):
                    m = 2 * p + s
                    for k in range(KT):
                        r = mm3(A[p % 3][:, s * GROUP:(s + 1) * GROUP],
                                [W["w1"][j][:, k, m * P:(m + 1) * P] for j in range(2)],
                                [x1_t[j][:, k, :] for j in range(2)], k == 0, k == KT - 1)
                r.then_inc(f1_mm, 1)

            def ffn2(f, p):
                pe.wait_ge(hid_lo, FP * f + p + 1)
                if p == 0:
                    wait(pe, y2_done, TILES * f)
                for s in range(2):
                    for t in range(TILES):
                        c = s * GROUP + t * P
                        r = mm3(ACC[t][:, 0:D], [hid[j][:, p % RING, c:c + P] for j in range(2)],
                                [W["w2"][j][:, 2 * p + s, :] for j in range(2)],
                                p == 0 and s == 0, p == FP - 1 and s == 1)
                r.then_inc(f2_mm, 1)

            def step(g, att=True, ffn=True, more=True):
                f = g - 1
                if att:
                    qk(g)
                if ffn:
                    for t in range(TILES):
                        turn_x1(f, t)
                if att:
                    for t in range(TILES):
                        values(g, t, ffn)
                if ffn:
                    ffn1(f, 0, att)
                    ffn1(f, 1, att)
                if att:
                    for t in range(TILES):
                        scores(g, t, ffn)
                if ffn:
                    ffn1(f, 2, att)
                    ffn2(f, 0)
                    ffn2(f, 1)
                if att:
                    turn_p(g, 0)
                if ffn:
                    ffn1(f, 3, att)
                if att:
                    pv(g, 0)
                    turn_p(g, 1)
                if ffn:
                    ffn2(f, 2)
                if att:
                    pv(g, 1)
                if ffn:
                    ffn1(f, 4, att)
                    ffn2(f, 3)
                if att:
                    for t in range(TILES):
                        turn_ctx(g, t)
                if ffn:
                    ffn1(f, 5, att)
                    ffn2(f, 4)
                if att:
                    for t in range(TILES):
                        attn_out(g, t)
                if ffn:
                    ffn2(f, 5)

            step(0, ffn=False)
            step(1)
            with pe.Fori(2, NG - 1) as g:
                step(g)
            step(NG - 1, more=False)
            step(NG, att=False)

        @block.scalar
        def _(act):
            def high(piece, loaded, done):
                act.wait_ge(loaded, pieces_of(piece))
                act.activation(halves(piece, 0), stage(piece).rearrange("p (k c) -> p k c", k=KT), ACT.Copy).then_inc(done, 1)

            def second_high(i):
                act.wait_ge(second_loaded[i % len(spare)], 16 * (i // len(spare) + 1))
                act.activation(part(i, 0), spare[i % len(spare)][:, 0:second[i][4]], ACT.Copy).then_inc(second_hi, 1)

            def split_x(g):
                act.wait_ge(xt_loaded, 16 * KT * (g + 1))
                wait(act, v_mm, TILES * g)
                act.activation(xt[0][:].rearrange("p k n -> p (k n)"), xt_raw, ACT.Copy).then_inc(xt_hi, 1)

            def take_q(g):
                wait(act, s_mm, TILES * g)
                act.wait_ge(qk_mm, 3 * g + 1)
                for m in range(2):
                    r = act.activation(q[:, m, :], A[0][:, m * GROUP:(m + 1) * GROUP], ACT.Identity, bias=bq[:, m:m + 1])
                r.then_inc(q_done, 1)
                act.wait_ge(qk_mm, 3 * g + 2)
                act.activation(q[:, 2, :], A[1][:, 0:GROUP], ACT.Identity, bias=bq[:, 2:3])
                for b in range(*SPAN0[0][:2]):
                    r = act.activation(k_blocks[:, :, b, :], A[1][:, GROUP:2 * GROUP].rearrange("p (g n) -> p g n", g=GB),
                                       ACT.Identity, bias=kbias[:, b:b + 1], scale=mask[:, b:b + 1])
                r.then_inc(q_done, 1)

            def keep_v(g, t):
                a, b = TILES * t, TILES * t + 1
                act.wait_ge(v_done, TILES * g + t + 1)
                act.activation(v_pairs[0:64, a, 0:VE], v_nat[0:64, t, 0:VE], ACT.Copy)
                act.activation(v_pairs[64:P, b, VE:2 * VE], v_nat[64:P, t, VE:2 * VE], ACT.Copy).then_inc(v_kept, 1)

            def x1t_high(f, t):
                act.wait_ge(x1t_mm, TILES * f + t + 1)
                wait(act, f1_mm, FP * f)
                act.activation(x1_t[0][:, :, t * P:(t + 1) * P], B[t][:, 0:D].rearrange("p (k n) -> p k n", k=KT),
                               ACT.Copy).then_inc(x1t_hi, 1)

            def hidden(f, p):
                act.wait_ge(f1_mm, FP * f + p + 1)
                wait(act, hid_lo, FP * f + p - 1)
                for s in range(2):
                    m = 2 * p + s
                    r = act.activation(silu[:, p % 2, s * GROUP:(s + 1) * GROUP], A[p % 3][:, s * GROUP:(s + 1) * GROUP],
                                       ACT.Silu, bias=b1[:, m:m + 1])
                r.then_inc(silu_done, 1)
                act.wait_ge(silu_done, FP * f + p + 1)
                wait(act, f2_mm, FP * f + p + 1 - RING)
                act.activation(hid[0][:, p % RING, :], silu[:, p % 2, :], ACT.Copy).then_inc(hid_hi, 1)

            def exp(g, t):
                act.wait_ge(shifted, TILES * g + t + 1)
                act.activation(prob[:, t, :], prob[:, t, :], ACT.Exp).then_inc(exp_done, 1)

            def take_pt(g, t):
                act.wait_ge(pt_mm, TILES * g + t + 1)
                wait(act, pv_mm, TILES * (g - 1) + t + 1)
                act.activation(pt[:, t, :], B[2 * t][:, :], ACT.Copy).then_inc(pt_done, 1)

            def ctxt_high(g, t):
                act.wait_ge(ct_mm, TILES * g + t + 1)
                wait(act, o_mm, TILES * (g - 1) + t + 1)
                act.activation(ctx_t[0][:, t, :], B[1 + t][:, 0:D], ACT.Copy).then_inc(ctxt_hi, 1)

            def square(src, done, out, result, n, t, junk, bias=0.0):
                act.wait_ge(done, n)
                act.activation(junk, src[:, t, :], ACT.Square, bias=bias, scale=ROOT, accum_out=out[:, t:t + 1]).then_inc(result, 1)

            high(first[0], first_loaded[0], w_hi)
            split_x(0)
            for i in range(1, 4):
                high(first[i], first_loaded[i], w_hi)
            act.wait_ge(const_loaded, 16 * N_CONST)
            act.wait_ge(pairs_zeroed, 1)
            act.wait_ge(kbias_set, 1)

            def step(g, att=True, ffn=True, late=True, more=True):
                f, e = g - 1, g - 2
                fresh = att and not ffn
                if att:
                    take_q(g)
                if ffn:
                    for t in range(TILES):
                        x1t_high(f, t)
                    hidden(f, 0)
                if att:
                    for t in range(TILES):
                        keep_v(g, t)
                if ffn:
                    hidden(f, 1)
                    hidden(f, 2)
                if late:
                    for t in range(TILES):
                        square(z, mean_done, ssq3, sq3_done, 2 * (e + 1), t, ctxt[:, t, :], bias=nmean_c[:, t:t + 1])
                if fresh:
                    for i in SECOND[0]:
                        second_high(i)
                if att:
                    for t in range(TILES):
                        exp(g, t)
                    for t in range(TILES):
                        take_pt(g, t)
                if ffn:
                    hidden(f, 3)
                    hidden(f, 4)
                if att and more:
                    split_x(g + 1)
                if fresh:
                    for i in SECOND[1]:
                        second_high(i)
                if att:
                    for t in range(TILES):
                        ctxt_high(g, t)
                if ffn:
                    hidden(f, 5)
                if fresh:
                    for i in SECOND[2]:
                        second_high(i)
                if att:
                    for t in range(TILES):
                        square(x1, y1_done, ssq1, sq1_done, TILES * g + t + 1, t, ctxt[:, t, :])
                elif ffn:
                    for i in range(4):
                        high(third[i], third_loaded[i], third_hi)
                if ffn:
                    for t in range(TILES):
                        square(z, y2_done, ssq2, sq2_done, TILES * f + t + 1, t, silu[:, t, 0:D])

            step(0, ffn=False, late=False)
            step(1, late=False)
            with act.Fori(2, NG - 1) as g:
                step(g)
            step(NG - 1, more=False)
            step(NG, att=False)
            step(NG + 1, att=False, ffn=False)

        @block.vector
        def _(dve):
            dve.memset(bv[:], 1.0)
            dve.memset(shared["bv"][:], 1.0).then_inc(row_set, 1)
            dve.memset(stage(first[2]), 0.0).then_inc(stage_set, 1)

            def low(piece, hi, count, done):
                dve.wait_ge(hi, count)
                dve.tensor_tensor(halves(piece, 1), stage(piece).rearrange("p (k c) -> p k c", k=KT),
                                  halves(piece, 0).bitcast(F32), ALU.subtract).then_inc(done, 1)

            def split_second(i):
                dve.wait_ge(second_hi, i + 1)
                dve.tensor_tensor(part(i, 1), spare[i % len(spare)][:, 0:second[i][4]], part(i, 0).bitcast(F32),
                                  ALU.subtract).then_inc(second_lo, 1)

            def split_x(g):
                dve.wait_ge(xt_hi, g + 1)
                dve.tensor_tensor(xt[1][:].rearrange("p k n -> p (k n)"), xt_raw,
                                  xt[0][:].bitcast(F32).rearrange("p k n -> p (k n)"), ALU.subtract).then_inc(xt_lo, 1)

            def take_k(g):
                dve.wait_ge(qk_mm, 3 * g + 3)
                wait(dve, s_mm, TILES * g)
                for k in (1, 2):
                    for b in range(*SPAN0[k][:2]):
                        r = dve.tensor_scalar(k_blocks[:, :, b, :],
                                              A[2][:, (k - 1) * GROUP:k * GROUP].rearrange("p (g n) -> p g n", g=GB),
                                              bk[:, k:k + 1], mask[:, b:b + 1], ALU.add, ALU.mult)
                r.then_inc(k_done, 1)

            def x1t_low(f, t):
                dve.wait_ge(x1t_hi, TILES * f + t + 1)
                hi, lo = (x1_t[j][:, :, t * P:(t + 1) * P] for j in range(2))
                dve.tensor_tensor(lo, B[t][:, 0:D].rearrange("p (k n) -> p k n", k=KT), hi.bitcast(F32),
                                  ALU.subtract).then_inc(x1t_lo, 1)

            def take_v(g, t):
                dve.wait_ge(v_mm, TILES * g + t + 1)
                wait(dve, v_swapped[t], 32 * g)
                wait(dve, v_kept, TILES * (g - 1) + t + 1)
                wait(dve, pv_mm, TILES * (g - 1) + t + 1)
                dve.tensor_tensor(v_nat[:, t, :], B[2 if t == 0 else 0][:, 0:2 * VE],
                                  bv[:].rearrange("p r h c -> p (r h c)"), ALU.add).then_inc(v_done, 1)

            def hidden_low(f, p):
                dve.wait_ge(hid_hi, FP * f + p + 1)
                dve.tensor_tensor(hid[1][:, p % RING, :], silu[:, p % 2, :], hid[0][:, p % RING, :].bitcast(F32),
                                  ALU.subtract).then_inc(hid_lo, 1)

            def soften(g, t):
                s = prob[:, t, :].rearrange("p (h n) -> p h n", h=H0)
                dve.wait_ge(s_mm, TILES * g + t + 1)
                if t == 0:
                    dve.wait_ge(adj_loaded, 16 * (g + 1))
                wait(dve, pt_mm, TILES * (g - 1) + t + 1)
                dve.scalar_tensor_tensor(out=s, in0=B[1 + t][:, :].rearrange("p (h n) -> p h n", h=H0), scalar=SCALE0,
                                         in1=adj_in[:, t, :].unsqueeze(1).broadcast_to([P, H0, NODES]),
                                         op0=ALU.mult, op1=ALU.add).then_inc(biased, 1)
                dve.wait_ge(biased, TILES * g + t + 1)
                dve.tensor_reduce(smax[:, t, :], s, AX_X, ALU.max).then_inc(maxed, 1)
                dve.wait_ge(maxed, TILES * g + t + 1)
                dve.tensor_tensor(s, s, smax[:, t, :].unsqueeze(2).broadcast_to([P, H0, NODES]),
                                  ALU.subtract).then_inc(shifted, 1)

            def take_ctx(g, t):
                o = B[1 - t][:, 0:2 * VE].rearrange("p (h c) -> p h c", c=VW)
                dve.wait_ge(pv_mm, TILES * g + t + 1)
                dve.reciprocal(rden[:, t, :], o[:, :, DH0]).then_inc(rden_done, 1)
                dve.wait_ge(rden_done, TILES * g + t + 1)
                wait(dve, ct_mm, TILES * (g - 1) + t + 1)
                dve.tensor_tensor(ctxt[:, t, :].rearrange("p (h c) -> p h c", h=H0), o[:, :, 0:DH0],
                                  rden[:, t, :].unsqueeze(2).broadcast_to([P, H0, DH0]), ALU.mult).then_inc(ctx_done, 1)

            def ctxt_low(g, t):
                dve.wait_ge(ctxt_hi, TILES * g + t + 1)
                dve.tensor_tensor(ctx_t[1][:, t, :], B[1 + t][:, 0:D], ctx_t[0][:, t, :].bitcast(F32),
                                  ALU.subtract).then_inc(ctxt_lo, 1)

            def take_y1(g, t):
                dve.wait_ge(o_mm, TILES * g + t + 1)
                if t == 0:
                    dve.wait_ge(xbo_done, g + 1)
                wait(dve, x1t_mm, TILES * (g - 1) + t + 1)
                wait(dve, x1b2_done, TILES * (g - 1) + t + 1)
                dve.tensor_tensor(x1[:, t, :], B[t][:, 0:D], x_bo[:, t, :], ALU.add).then_inc(y1_done, 1)

            def scale_x1(g, t):
                dve.wait_ge(rstd1_done, g + 1)
                dve.scalar_tensor_tensor(out=x1[:, t, :], in0=x1[:, t, :], scalar=rstd1[:, t:t + 1], in1=rows["alpha1"][:],
                                         op0=ALU.mult, op1=ALU.mult).then_inc(x1_scaled, 1)

            def take_y2(f, t):
                dve.wait_ge(f2_mm, FP * (f + 1))
                dve.wait_ge(x1b2_done, TILES * f + t + 1)
                if t == 0:
                    wait(dve, x2_stored, 16 * f)
                dve.tensor_tensor(z[:, t, :], ACC[t][:, 0:D], x1_b2[:, t, :], ALU.add).then_inc(y2_done, 1)

            def rms_norm(e):
                dve.wait_ge(rstd2_done, e + 1)
                for t in range(TILES):
                    dve.scalar_tensor_tensor(out=z[:, t, :], in0=z[:, t, :], scalar=rstd2[:, t:t + 1],
                                             in1=rows["alpha2"][:], op0=ALU.mult, op1=ALU.mult).then_inc(z_scaled, 1)
                dve.wait_ge(xres_done, e + 1)
                for t in range(TILES):
                    dve.wait_ge(z_scaled, TILES * e + t + 1)
                    dve.scalar_tensor_tensor(out=z[:, t, :], in0=z[:, t, :], scalar=1.0, in1=x_res[:, t, :], op0=ALU.mult,
                                             op1=ALU.add, accum_out=zsum[:, t:t + 1]).then_inc(z_done, 1)
                dve.wait_ge(z_done, TILES * (e + 1))
                dve.tensor_scalar(nmean[:], zsum[:], -1.0 / D, None, ALU.mult).then_inc(mean_done, 1)
                dve.tensor_scalar(nmean_c[:], zsum[:], -ROOT / D, None, ALU.mult).then_inc(mean_done, 1)

            def layer_norm(e):
                dve.wait_ge(rstd3_done, e + 1)
                for t in range(TILES):
                    dve.tensor_scalar(z[:, t, :], z[:, t, :], nmean[:, t:t + 1], rstd3[:, t:t + 1],
                                      ALU.add, ALU.mult).then_inc(x2_done, 1)

            low(first[0], w_hi, 1, w_lo)
            split_x(0)
            for i in range(1, 4):
                low(first[i], w_hi, i + 1, w_lo)
            dve.wait_ge(const_loaded, 16 * N_CONST)
            dve.wait_ge(w_lo, len(first))
            for k in range(KT):
                b0, b1_, _h = SPAN0[k]
                r = dve.tensor_scalar(kbias[:, b0:b1_], mask[:, b0:b1_], bk[:, k:k + 1], None, ALU.mult)
            r.then_inc(kbias_set, 1)
            dve.memset(v["v_pairs"], 0.0).then_inc(pairs_zeroed, 1)

            def step(g, att=True, ffn=True, late=True, more=True):
                f, e = g - 1, g - 2
                fresh = att and not ffn
                if ffn:
                    for t in range(TILES):
                        x1t_low(f, t)
                if att:
                    take_k(g)
                    for t in range(TILES):
                        take_v(g, t)
                elif ffn:
                    dve.wait_ge(o_mm, TILES * NG)
                    dve.memset(stage(third[2]), 0.0).then_inc(third_set, 1)
                if late:
                    rms_norm(e)
                if ffn:
                    hidden_low(f, 0)
                    hidden_low(f, 1)
                if fresh:
                    for i in SECOND[0]:
                        split_second(i)
                if att:
                    for t in range(TILES):
                        soften(g, t)
                if ffn:
                    hidden_low(f, 2)
                if late:
                    layer_norm(e)
                if att:
                    take_ctx(g, 0)
                if ffn:
                    hidden_low(f, 3)
                if att:
                    take_ctx(g, 1)
                if ffn:
                    hidden_low(f, 4)
                if att and more:
                    split_x(g + 1)
                if fresh:
                    for i in SECOND[1]:
                        split_second(i)
                if att:
                    for t in range(TILES):
                        ctxt_low(g, t)
                if ffn:
                    hidden_low(f, 5)
                if fresh:
                    for i in SECOND[2]:
                        split_second(i)
                if att:
                    for t in range(TILES):
                        take_y1(g, t)
                    for t in range(TILES):
                        scale_x1(g, t)
                elif ffn:
                    for i in range(4):
                        low(third[i], third_hi, i + 1, third_lo)
                if ffn:
                    for t in range(TILES):
                        take_y2(f, t)

            step(0, ffn=False, late=False)
            step(1, late=False)
            with dve.Fori(2, NG - 1) as g:
                step(g)
            step(NG - 1, more=False)
            step(NG, att=False)
            step(NG + 1, att=False, ffn=False)

        @block.gpsimd
        def _(pool):
            pool.memset(half[:], -0.5).then_inc(half_set, 1)
            pool.memset(eps_rms[:], EPS_RMS).then_inc(half_set, 1)
            pool.memset(eps_ln[:], EPS_LN).then_inc(half_set, 1)
            pool.wait_ge(half_set, 3)
            pool.wait_ge(const_loaded, 16 * N_CONST)

            def add_row(tensor, row, t):
                return pool.tensor_tensor(tensor[:, t, :], tensor[:, t, :], rows[row][:], ALU.add)

            def bias_x(g):
                pool.wait_ge(x_loaded, 16 * (g + 1))
                for t in range(TILES):
                    r = add_row(x_bo, "bo", t)
                r.then_inc(xbo_done, 1)

            def bias_res(e):
                pool.wait_ge(res_loaded, 16 * (e + 1))
                for t in range(TILES):
                    r = add_row(x_res, "gamma2", t)
                r.then_inc(xres_done, 1)

            def root(g, mean_sq, ready, ms, ms_done, eps, out, done):
                pool.wait_ge(ready, TILES * (g + 1))
                pool.tensor_tensor(ms[:], mean_sq[:], eps[:], ALU.add).then_inc(ms_done, 1)
                pool.wait_ge(ms_done, g + 1)
                pool.tensor_tensor(out[:], ms[:], half[:], ALU.pow).then_inc(done, 1)

            def step(g, att=True, ffn=True, late=True, more=True):
                f, e = g - 1, g - 2
                if late:
                    root(e, ssq2, sq2_done, ms2, ms2_done, eps_rms, rstd2, rstd2_done)
                    bias_res(e)
                if att:
                    bias_x(g)
                if late:
                    root(e, ssq3, sq3_done, ms3, ms3_done, eps_ln, rstd3, rstd3_done)
                if att:
                    root(g, ssq1, sq1_done, ms1, ms1_done, eps_rms, rstd1, rstd1_done)
                    for t in range(TILES):
                        pool.wait_ge(x1_scaled, TILES * g + t + 1)
                        add_row(x1, "gamma1", t).then_inc(x1_done, 1)
                    for t in range(TILES):
                        pool.wait_ge(x1_done, TILES * g + t + 1)
                        wait(pool, y2_done, TILES * (g - 1) + t + 1)
                        pool.tensor_tensor(x1_b2[:, t, :], x1[:, t, :], rows["b2"][:], ALU.add).then_inc(x1b2_done, 1)

            step(0, ffn=False, late=False)
            step(1, late=False)
            with pool.Fori(2, NG - 1) as g:
                step(g)
            step(NG - 1, more=False)
            step(NG, att=False)
            step(NG + 1, att=False, ffn=False)


def layer1(nc, x2, adj, out, shared):
    VW = DH1 + 1
    VE = H1 // 2 * VW
    S = H1 * NODES
    with ExitStack() as ctx:
        def sb(name, shape, dt=F32):
            return ctx.enter_context(nc.sbuf_tensor(name, shape, dt))

        def sem(name):
            return ctx.enter_context(nc.semaphore(name))

        one = [ctx.enter_context(nc.psum_tensor(f"b_bank{i}", [P, 512], F32)) for i in range(4)]
        two = [ctx.enter_context(nc.psum_tensor(f"b_banks{i}", [P, 1024], F32)) for i in range(2)]

        W = {n: shared["W"][n.lower()] for n in ("Wq", "Wk", "Wv", "Wo")}
        ident, mask, bo = shared["ident"], shared["mask"], shared["bo"]
        half, eps_ln = sb("b_half", [P, TILES]), sb("b_eps_ln", [P, TILES])
        bv = shared["bv"]

        x_in, res, y = sb("b_x", [P, TILES, D]), sb("b_res", [P, TILES, D]), sb("b_y", [P, TILES, D])
        adj_in, bias = sb("b_adj", [P, TILES, NODES]), sb("b_bias", [P, TILES, NODES])
        xt = [sb(f"b_xt_{s}", [P, KT, GROUP], F32R) for s in ("hi", "lo")]
        q = sb("b_q", [P, KT, GROUP])
        k_blocks = sb("b_k_blocks", [P, GB, NB1, NODES])
        v_nat, v_pairs = sb("b_v_nat", [P, TILES, 2 * VE]), sb("b_v_pairs", [P, GB, 2 * VE])
        prob, pt = sb("b_p", [P, TILES, S]), sb("b_pt", [P, TILES, S])
        ctxt = sb("b_ctx", [P, TILES, D])
        ctx_t = [sb(f"b_ctxt_{s}", [P, TILES, D], F32R) for s in ("hi", "lo")]
        smax, samax, rden = (sb(f"b_{n}", [P, TILES, H1]) for n in ("smax", "samax", "rden"))
        ysum, nmean, nmean_c, ssq = (sb(f"b_{n}", [P, TILES]) for n in ("ysum", "nmean", "nmean_c", "ssq"))
        var, rstd = sb("b_var", [P, TILES]), sb("b_rstd", [P, TILES])

        pairs_zeroed = sem("b_pairs_zeroed")
        x_loaded, res_loaded, adj_loaded, out_stored = (sem("b_" + n) for n in (
            "x_loaded", "res_loaded", "adj_loaded", "out_stored"))
        v_swapped = [sem(f"b_v_swapped{t}") for t in range(TILES)]
        xt_mm, qk_mm, v_mm, s_mm, pt_mm, pv_mm, ct_mm, o_mm = (sem("b_" + n) for n in (
            "xt_mm", "qk_mm", "v_mm", "s_mm", "pt_mm", "pv_mm", "ct_mm", "o_mm"))
        xt_hi, q_done, exp_done, pt_done, ctxt_hi = (sem("b_" + n) for n in (
            "xt_hi", "q_done", "exp_done", "pt_done", "ctxt_hi"))
        xt_lo, k_done, v_done, biased, maxed, magnitude, rden_done, rden_masked, ctx_done, ctxt_lo = (
            sem("b_" + n) for n in ("xt_lo", "k_done", "v_done", "biased", "maxed", "magnitude", "rden_done",
                                    "rden_masked", "ctx_done", "ctxt_lo"))
        y_done, mean_done, out_done, sq_done = (sem("b_" + n) for n in ("y_done", "mean_done", "out_done", "sq_done"))
        half_set, bias_done, v_kept, shifted, var_done, rstd_done, res_done = (sem("b_" + n) for n in (
            "half_set", "bias_done", "v_kept", "shifted", "var_done", "rstd_done", "res_done"))

        block = ctx.enter_context(nc.Block())

        @block.sync
        def _(sp):
            def load_x(g):
                wait(sp, xt_mm, TILES * g)
                sp.dma_start(x_in[:], x2[g]).then_inc(x_loaded, 16)

            def load_res(g):
                wait(sp, y_done, TILES * g)
                sp.dma_start(res[:], x2[g]).then_inc(res_loaded, 16)

            def load_adj(g):
                wait(sp, bias_done, g)
                sp.dma_start(adj_in[:], adj[g]).then_inc(adj_loaded, 16)

            def swap_v(g, t):
                a, b = TILES * t, TILES * t + 1
                sp.wait_ge(v_done, TILES * g + t + 1)
                sp.dma_start(v_pairs[64:P, a, VE:2 * VE], v_nat[0:64, t, VE:2 * VE]).then_inc(v_swapped[t], 16)
                sp.dma_start(v_pairs[0:64, b, 0:VE], v_nat[64:P, t, 0:VE]).then_inc(v_swapped[t], 16)

            def store(g):
                sp.wait_ge(out_done, TILES * (g + 1))
                sp.dma_start(out[g], y[:]).then_inc(out_stored, 16)

            load_x(0)
            load_adj(0)

            def step(g, front=True, back=True, late=True, more=True):
                if front and more:
                    load_x(g + 1)
                if late:
                    store(g - 2)
                if back:
                    load_res(g - 1)
                if front:
                    for t in range(TILES):
                        swap_v(g, t)
                    if more:
                        load_adj(g + 1)

            step(0, back=False, late=False)
            step(1, late=False)
            with sp.Fori(2, NG - 1) as g:
                step(g)
            step(NG - 1, more=False)
            step(NG, front=False)
            step(NG + 1, front=False, back=False)
            sp.wait_ge(out_stored, 16 * NG)

        @block.tensor
        def _(pe):
            def mm3(out, lhs, rhs, first, last):
                for n, (a, b) in enumerate(((0, 0), (1, 0), (0, 1))):
                    r = pe.matmul(out, lhs[a], rhs[b], start=first and n == 0, stop=last and n == 2)
                return r

            def turn_x(g, t):
                pe.wait_ge(x_loaded, 16 * (g + 1))
                wait(pe, k_done, g)
                for k in range(KT):
                    r = pe.transpose(one[1 + t][:, k * P:(k + 1) * P], x_in[:, t, k * P:(k + 1) * P], ident[:])
                r.then_inc(xt_mm, 1)

            def qk(g):
                pe.wait_ge(xt_lo, TILES * (g + 1))
                wait(pe, ctxt_lo, TILES * (g - 1))
                for u in range(3):
                    for s in range(2):
                        m = 2 * u + s
                        n, m = ("Wq", m) if m < KT else ("Wk", m - KT)
                        for k in range(KT):
                            r = mm3(one[u][:, s * GROUP:(s + 1) * GROUP],
                                    [W[n][j][:, k, m * P:(m + 1) * P] for j in range(2)],
                                    [xt[j][:, k, :] for j in range(2)], k == 0, k == KT - 1)
                    r.then_inc(qk_mm, 1)

            def values(g, t):
                if t == 0:
                    wait(pe, y_done, TILES * (g - 1))
                else:
                    pe.wait_ge(q_done, 2 * g + 1)
                out = one[3 if t == 0 else 0]
                for k in range(KT):
                    r = mm3(out[:, 0:2 * VE], [xt[j][:, k, t * P:(t + 1) * P] for j in range(2)],
                            [W["Wv"][j][:, k, :] for j in range(2)], k == 0, k == KT - 1)
                r.then_inc(v_mm, 1)

            def scores(g, t, back):
                pe.wait_ge(q_done, 2 * (g + 1))
                pe.wait_ge(k_done, g + 1)
                if back:
                    pe.wait_ge(pt_done, TILES * (g - 1) + t + 1)
                for k in range(KT):
                    b0, b1_, h = SPAN1[k]
                    for s in range(2):
                        n = TILES * t + s
                        r = pe.matmul(two[t][64 * s:64 * s + 64, h * NODES:(h + b1_ - b0) * NODES],
                                      q[:, k, n * NODES:(n + 1) * NODES],
                                      k_blocks[:, n, b0:b1_, :].rearrange("p b n -> p (b n)"),
                                      start=True, stop=True, skip_group_check=True)
                r.then_inc(s_mm, 1)

            def turn_p(g, t):
                pe.wait_ge(exp_done, TILES * g + t + 1)
                if t == 0:
                    wait(pe, y_done, TILES * g)
                for h in range(H1 // 2):
                    r = pe.transpose(two[t][:, h * P:(h + 1) * P], prob[:, t, h * P:(h + 1) * P], ident[:])
                r.then_inc(pt_mm, 1)

            def pv(g, t, front):
                pe.wait_ge(pt_done, TILES * g + t + 1)
                pe.wait_ge(v_swapped[t], 32 * (g + 1))
                pe.wait_ge(v_kept, TILES * g + t + 1)
                if front:
                    pe.wait_ge(*((q_done, 2 * (g + 2)) if t == 0 else (k_done, g + 2)))
                for s in range(2):
                    for h in range(H1 // 2):
                        n = TILES * t + s
                        vv = v_pairs[:, n, :].rearrange("p (r h c) -> p h r c", r=2, h=H1 // 2)[:, h]
                        r = pe.matmul(one[1 + t][64 * s:64 * s + 64, h * 2 * VW:(h + 1) * 2 * VW].rearrange("p (r c) -> p r c", r=2),
                                      pt[:, t, h * P + 64 * s:h * P + 64 * s + 64], vv, start=True, stop=True,
                                      skip_group_check=True)
                r.then_inc(pv_mm, 1)

            def turn_ctx(g, t, front):
                pe.wait_ge(ctx_done, TILES * g + t + 1)
                if front:
                    pe.wait_ge(v_done, TILES * (g + 1) + t + 1)
                for k in range(KT):
                    r = pe.transpose(one[3 if t == 0 else 0][:, k * P:(k + 1) * P], ctxt[:, t, k * P:(k + 1) * P], ident[:])
                r.then_inc(ct_mm, 1)

            def attn_out(g, t, front):
                pe.wait_ge(ctxt_lo, TILES * g + t + 1)
                if t == 1 and front:
                    pe.wait_ge(biased, TILES * (g + 1) + 1)
                o = one[3] if t == 0 else two[0]
                for k in range(KT):
                    r = mm3(o[:, 0:D], [ctx_t[j][:, t, k * P:(k + 1) * P] for j in range(2)],
                            [W["Wo"][j][:, k, :] for j in range(2)], k == 0, k == KT - 1)
                r.then_inc(o_mm, 1)

            for t in range(TILES):
                turn_x(0, t)
            def step(g, front=True, back=True, more=True):
                b = g - 1
                if front:
                    qk(g)
                if back:
                    for t in range(TILES):
                        turn_p(b, t)
                for t in range(TILES):
                    if front:
                        values(g, t)
                    if back:
                        pv(b, t, front)
                for t in range(TILES):
                    if back:
                        turn_ctx(b, t, front)
                    if front:
                        scores(g, t, back)
                if front and more:
                    for t in range(TILES):
                        if back:
                            pe.wait_ge(ctx_done, TILES * b + t + 1)
                        turn_x(g + 1, t)
                if back:
                    for t in range(TILES):
                        attn_out(b, t, front)

            step(0, back=False)
            step(1)
            with pe.Fori(2, NG - 1) as g:
                step(g)
            step(NG - 1, more=False)
            step(NG, front=False)

        @block.scalar
        def _(act):
            act.wait_ge(pairs_zeroed, 1)

            def xt_high(g, t):
                act.wait_ge(xt_mm, TILES * g + t + 1)
                wait(act, v_mm, TILES * g)
                act.activation(xt[0][:, :, t * P:(t + 1) * P], one[1 + t][:, 0:D].rearrange("p (k n) -> p k n", k=KT),
                               ACT.Copy).then_inc(xt_hi, 1)

            def take_q(g):
                wait(act, s_mm, TILES * g)
                act.wait_ge(qk_mm, 3 * g + 1)
                act.activation(q[:, 0:2, :].rearrange("p k n -> p (k n)"), one[0][:], ACT.Copy).then_inc(q_done, 1)
                act.wait_ge(qk_mm, 3 * g + 2)
                act.activation(q[:, 2, :], one[1][:, 0:GROUP], ACT.Copy)
                for b in range(*SPAN1[0][:2]):
                    r = act.activation(k_blocks[:, :, b, :], one[1][:, GROUP:2 * GROUP].rearrange("p (g n) -> p g n", g=GB),
                                       ACT.Copy, scale=mask[:, b:b + 1])
                r.then_inc(q_done, 1)

            def keep_v(g, t):
                a, b = TILES * t, TILES * t + 1
                act.wait_ge(v_done, TILES * g + t + 1)
                act.activation(v_pairs[0:64, a, 0:VE], v_nat[0:64, t, 0:VE], ACT.Copy)
                act.activation(v_pairs[64:P, b, VE:2 * VE], v_nat[64:P, t, VE:2 * VE], ACT.Copy).then_inc(v_kept, 1)

            def exp(g, t):
                act.wait_ge(shifted, TILES * g + t + 1)
                act.activation(prob[:, t, :], prob[:, t, :], ACT.Exp).then_inc(exp_done, 1)

            def take_pt(g, t):
                act.wait_ge(pt_mm, TILES * g + t + 1)
                wait(act, pv_mm, TILES * (g - 1) + t + 1)
                act.activation(pt[:, t, :], two[t][:, 0:S], ACT.Copy).then_inc(pt_done, 1)

            def ctxt_high(g, t):
                act.wait_ge(ct_mm, TILES * g + t + 1)
                wait(act, o_mm, TILES * (g - 1) + t + 1)
                act.activation(ctx_t[0][:, t, :], one[3 if t == 0 else 0][:, 0:D], ACT.Copy).then_inc(ctxt_hi, 1)

            def square(g, t):
                act.wait_ge(mean_done, 2 * (g + 1))
                act.activation(ctxt[:, t, :], y[:, t, :], ACT.Square, bias=nmean_c[:, t:t + 1], scale=ROOT,
                               accum_out=ssq[:, t:t + 1]).then_inc(sq_done, 1)

            for t in range(TILES):
                xt_high(0, t)

            def step(g, front=True, back=True, more=True):
                b = g - 1
                if back:
                    exp(b, 1)
                if front:
                    take_q(g)
                if back:
                    for t in range(TILES):
                        take_pt(b, t)
                if front:
                    for t in range(TILES):
                        keep_v(g, t)
                if back:
                    for t in range(TILES):
                        ctxt_high(b, t)
                if front and more:
                    for t in range(TILES):
                        xt_high(g + 1, t)
                if front:
                    exp(g, 0)
                if back:
                    for t in range(TILES):
                        square(b, t)

            step(0, back=False)
            step(1)
            with act.Fori(2, NG - 1) as g:
                step(g)
            step(NG - 1, more=False)
            step(NG, front=False)

        @block.vector
        def _(dve):
            dve.memset(v_pairs[:], 0.0).then_inc(pairs_zeroed, 1)

            def xt_low(g, t):
                dve.wait_ge(xt_hi, TILES * g + t + 1)
                hi, lo = (xt[j][:, :, t * P:(t + 1) * P] for j in range(2))
                dve.tensor_tensor(lo, one[1 + t][:, 0:D].rearrange("p (k n) -> p k n", k=KT), hi.bitcast(F32),
                                  ALU.subtract).then_inc(xt_lo, 1)

            def take_k(g):
                dve.wait_ge(qk_mm, 3 * g + 3)
                wait(dve, s_mm, TILES * g)
                for k in (1, 2):
                    for b in range(*SPAN1[k][:2]):
                        r = dve.tensor_scalar(k_blocks[:, :, b, :],
                                              one[2][:, (k - 1) * GROUP:k * GROUP].rearrange("p (g n) -> p g n", g=GB),
                                              mask[:, b:b + 1], None, ALU.mult)
                r.then_inc(k_done, 1)

            def take_v(g, t):
                dve.wait_ge(v_mm, TILES * g + t + 1)
                wait(dve, v_swapped[t], 32 * g)
                wait(dve, v_kept, TILES * (g - 1) + t + 1)
                wait(dve, pv_mm, TILES * (g - 1) + t + 1)
                dve.tensor_tensor(v_nat[:, t, :], one[3 if t == 0 else 0][:, 0:2 * VE],
                                  bv[:].rearrange("p r h c -> p (r h c)"), ALU.add).then_inc(v_done, 1)

            def soften(g, t):
                s = prob[:, t, :].rearrange("p (h n) -> p h n", h=H1)
                dve.wait_ge(s_mm, TILES * g + t + 1)
                if t == 0:
                    dve.wait_ge(bias_done, g + 1)
                wait(dve, pt_mm, TILES * (g - 1) + t + 1)
                dve.scalar_tensor_tensor(out=s, in0=two[t][:, 0:S].rearrange("p (h n) -> p h n", h=H1), scalar=SCALE1,
                                         in1=bias[:, t, :].unsqueeze(1).broadcast_to([P, H1, NODES]),
                                         op0=ALU.mult, op1=ALU.add).then_inc(biased, 1)
                dve.wait_ge(biased, TILES * g + t + 1)
                dve.tensor_reduce(smax[:, t, :], s, AX_X, ALU.max).then_inc(maxed, 1)
                wait(dve, rden_masked, TILES * (g - 1) + t + 1)
                dve.tensor_reduce(samax[:, t, :], s, AX_X, ALU.max, apply_absolute_value=True).then_inc(magnitude, 1)

            def take_ctx(g, t):
                o = one[1 + t][:, 0:2 * VE].rearrange("p (h c) -> p h c", c=VW)
                dve.wait_ge(pv_mm, TILES * g + t + 1)
                dve.reciprocal(rden[:, t, :], o[:, :, DH1]).then_inc(rden_done, 1)
                dve.wait_ge(rden_done, TILES * g + t + 1)
                dve.wait_ge(magnitude, TILES * g + t + 1)
                dve.scalar_tensor_tensor(out=rden[:, t, :], in0=samax[:, t, :], scalar=0.0, in1=rden[:, t, :],
                                         op0=ALU.is_gt, op1=ALU.mult).then_inc(rden_masked, 1)
                dve.wait_ge(rden_masked, TILES * g + t + 1)
                wait(dve, ct_mm, TILES * (g - 1) + t + 1)
                dve.tensor_tensor(ctxt[:, t, :].rearrange("p (h c) -> p h c", h=H1), o[:, :, 0:DH1],
                                  rden[:, t, :].unsqueeze(2).broadcast_to([P, H1, DH1]), ALU.mult).then_inc(ctx_done, 1)

            def ctxt_low(g, t):
                dve.wait_ge(ctxt_hi, TILES * g + t + 1)
                dve.tensor_tensor(ctx_t[1][:, t, :], one[3 if t == 0 else 0][:, 0:D], ctx_t[0][:, t, :].bitcast(F32),
                                  ALU.subtract).then_inc(ctxt_lo, 1)

            def finish(g):
                dve.wait_ge(res_done, g + 1)
                wait(dve, out_stored, 16 * g)
                for t in range(TILES):
                    dve.wait_ge(o_mm, TILES * g + t + 1)
                    o = one[3] if t == 0 else two[0]
                    dve.scalar_tensor_tensor(out=y[:, t, :], in0=o[:, 0:D], scalar=1.0, in1=res[:, t, :], op0=ALU.mult,
                                             op1=ALU.add, accum_out=ysum[:, t:t + 1]).then_inc(y_done, 1)
                dve.wait_ge(y_done, TILES * (g + 1))
                dve.tensor_scalar(nmean[:], ysum[:], -1.0 / D, None, ALU.mult).then_inc(mean_done, 1)
                dve.tensor_scalar(nmean_c[:], ysum[:], -ROOT / D, None, ALU.mult).then_inc(mean_done, 1)

            def norm(g):
                dve.wait_ge(rstd_done, g + 1)
                for t in range(TILES):
                    dve.tensor_scalar(y[:, t, :], y[:, t, :], nmean[:, t:t + 1], rstd[:, t:t + 1],
                                      ALU.add, ALU.mult).then_inc(out_done, 1)

            for t in range(TILES):
                xt_low(0, t)

            def step(g, front=True, back=True, late=True, more=True):
                b = g - 1
                if front:
                    take_k(g)
                if late:
                    norm(g - 2)
                for t in range(TILES):
                    if front:
                        take_v(g, t)
                    if back:
                        take_ctx(b, t)
                if back:
                    ctxt_low(b, 0)
                if front:
                    soften(g, 0)
                if back:
                    ctxt_low(b, 1)
                if front and more:
                    for t in range(TILES):
                        xt_low(g + 1, t)
                if front:
                    soften(g, 1)
                if back:
                    finish(b)

            step(0, back=False, late=False)
            step(1, late=False)
            with dve.Fori(2, NG - 1) as g:
                step(g)
            step(NG - 1, more=False)
            step(NG, front=False)
            step(NG + 1, front=False, back=False)

        @block.gpsimd
        def _(pool):
            pool.memset(half[:], -0.5).then_inc(half_set, 1)
            pool.memset(eps_ln[:], EPS_LN).then_inc(half_set, 1)
            pool.wait_ge(half_set, 2)

            def double_adj(g):
                pool.wait_ge(adj_loaded, 16 * (g + 1))
                wait(pool, biased, TILES * g)
                pool.tensor_tensor(bias[:], adj_in[:], adj_in[:], ALU.add).then_inc(bias_done, 1)

            def bias_res(g):
                pool.wait_ge(res_loaded, 16 * (g + 1))
                for t in range(TILES):
                    r = pool.tensor_tensor(res[:, t, :], res[:, t, :], bo[:], ALU.add)
                r.then_inc(res_done, 1)

            def shift(g, t):
                s = prob[:, t, :].rearrange("p (h n) -> p h n", h=H1)
                pool.wait_ge(maxed, TILES * g + t + 1)
                pool.wait_ge(magnitude, TILES * g + t + 1)
                pool.tensor_tensor(s, s, smax[:, t, :].unsqueeze(2).broadcast_to([P, H1, NODES]),
                                   ALU.subtract).then_inc(shifted, 1)

            def root(g):
                pool.wait_ge(sq_done, TILES * (g + 1))
                pool.tensor_tensor(var[:], ssq[:], eps_ln[:], ALU.add).then_inc(var_done, 1)
                pool.wait_ge(var_done, g + 1)
                pool.tensor_tensor(rstd[:], var[:], half[:], ALU.pow).then_inc(rstd_done, 1)

            def step(g, front=True, back=True, more=True):
                if front:
                    double_adj(g)
                if back:
                    bias_res(g - 1)
                if front:
                    for t in range(TILES):
                        shift(g, t)
                if back:
                    root(g - 1)

            step(0, back=False)
            step(1)
            with pool.Fori(2, NG - 1) as g:
                step(g)
            step(NG - 1, more=False)
            step(NG, front=False)


def program(nc, a, out):
    x2 = nc.dram_tensor("x2", (TOKENS, D), F32).ap()

    def groups(ap):
        return ap.rearrange("(g t p) d -> g p t d", t=TILES, p=P)

    xT = a["xT"].rearrange("(k p) (g n) -> k g p n", p=P, n=GROUP)
    w0 = {n: a[f"L0_gnn_{n}"] for n in ("wq", "bq", "wk", "bk", "wv", "bv", "wo", "bo", "w1", "b1", "w2", "b2",
                                        "alpha1", "gamma1", "alpha2", "gamma2")}
    w0 |= {"ident": a["ident"], "mask0": a["mask0"]}
    w1 = {n: a[f"L1_gnn_{n}"] for n in ("Wq", "Wk", "Wv", "Wo")}
    w0 |= {"mask1": a["mask1"], "bv1": a["L1_gnn_bv"], "bo1": a["L1_gnn_bo"]}
    VE1 = H1 // 2 * (DH1 + 1)
    with ExitStack() as ctx:
        def sb(name, shape, dt=F32):
            return ctx.enter_context(nc.sbuf_tensor(name, shape, dt))

        shared = {"W": {n: [sb(f"{n}_{s}", [P, KT, 2 * VE1 if n == "wv" else D], F32R) for s in ("hi", "lo")]
                        for n in ("wq", "wk", "wv", "wo")},
                  "ident": sb("ident", [P, P]), "mask": sb("mask_l1", [P, NB1]), "bo": sb("bo_l1", [P, D]),
                  "bv": sb("bv_l1", [P, 2, H1 // 2, DH1 + 1]), "VE1": VE1}
        layer0(nc, groups(a["x"]), xT, groups(a["adj"]), w0, w1, groups(x2), shared)
        layer1(nc, groups(x2), groups(a["adj"]), groups(out), shared)


def kernel(**inputs):
    import numpy as np
    import concourse.bacc as bacc
    from concourse.bass_utils import run_bass_kernel_spmd

    def block_mask(heads, blocks):
        rows = np.arange(P)[:, None]
        tile = np.array([t for t, _ in blocks])[None, :]
        head = np.array([h for _, h in blocks])[None, :]
        return ((rows + P * tile) // (D // heads) == head).astype(np.float32)

    host = {}
    for name, value in inputs.items():
        value = np.asarray(value)
        if name in ("x", "adj"):
            value = value.reshape(TOKENS, -1)
        elif name.startswith("L1_gnn_W"):
            value = value.T
        elif name in ("L0_gnn_bq", "L0_gnn_bk", "L0_gnn_b1"):
            value = value.reshape(-1, P).T
        host[name] = np.ascontiguousarray(value)
    host["xT"] = np.ascontiguousarray(host["x"].T)
    host["ident"] = np.eye(P, dtype=np.float32)
    host["mask0"] = block_mask(H0, BLOCKS0)
    host["mask1"] = block_mask(H1, BLOCKS1)

    nc = bacc.Bacc("TRN2", target_bir_lowering=False, num_devices=1, dynamic_dma_scratch_size=8192)
    arrays, args = {}, {}
    for name, value in host.items():
        arrays[f"in_{name}"] = value
        args[name] = nc.dram_tensor(f"in_{name}", value.shape, F32, kind="ExternalInput").ap()
    out = nc.dram_tensor("out", (TOKENS, D), F32, kind="ExternalOutput").ap()
    program(nc, args, out)
    r = run_bass_kernel_spmd(nc, [arrays], core_ids=[0])
    return np.asarray(r.results[0]["out"]).reshape(GRAPHS, NODES, D)
```

```python
from contextlib import ExitStack

import concourse.bass as bass
from concourse import mybir

F32 = mybir.dt.float32
F32R = mybir.dt.float32r
ALU = mybir.AluOpType
ACT = mybir.ActivationFunctionType
AX_X = mybir.AxisListType.X

P = 128
GRAPHS, NODES, D = 128, 64, 384
TOKENS = GRAPHS * NODES
TILES = 2
GROUP = TILES * P
GB = GROUP // NODES
NG = TOKENS // GROUP
KT = D // P
H0, H1 = 8, 12
DH0, DH1 = D // H0, D // H1
F = 1536
FC = F // P
FP = FC // 2
RING = 3
EPS_RMS, EPS_LN = 1e-6, 1e-5
ROOT = float(D) ** -0.5
SCALE0, SCALE1 = float(DH0) ** -0.5, float(D) ** -0.5


def head_blocks(heads):
    dh = D // heads
    blocks, span = [], []
    for t in range(KT):
        own = [h for h in range(heads) if h * dh < (t + 1) * P and (h + 1) * dh > t * P]
        span.append((len(blocks), len(blocks) + len(own), own[0]))
        blocks += [(t, h) for h in own]
    return blocks, span


BLOCKS0, SPAN0 = head_blocks(H0)
BLOCKS1, SPAN1 = head_blocks(H1)
NB0, NB1 = len(BLOCKS0), len(BLOCKS1)


def wait(eng, sem, value):
    if not isinstance(value, int) or value > 0:
        eng.wait_ge(sem, value)


def layer0(nc, block, sem, x, xT, adj, w, next_w, x2, shared):
    VW = DH0 + 1
    VE = H0 // 2 * VW
    with ExitStack() as ctx:
        def sb(name, shape, dt=F32):
            return ctx.enter_context(nc.sbuf_tensor(name, shape, dt))

        bank = [ctx.enter_context(nc.psum_tensor(f"a_bank{i}", [P, 512], F32)) for i in range(8)]
        A, B, ACC = bank[0:3], bank[3:6], bank[6:8]

        wide = {"wq": D, "wk": D, "wv": 2 * VE, "wo": D, "w1": F, "w2": D}
        tall = {n: FC if n == "w2" else KT for n in wide}
        W = {n: [sb(f"a_{n}_{s}", [P, tall[n], wide[n]], F32R) for s in ("hi", "lo")] for n in ("w1", "w2")}
        attn_W, ident = shared["W"], shared["ident"]
        for n in ("wq", "wk", "wv", "wo"):
            W[n] = [part[:, :, 0:wide[n]] for part in attn_W[n]]
        rows = {n: sb(f"a_{n}", [P, D]) for n in ("bo", "alpha1", "gamma1", "b2", "alpha2", "gamma2")}
        bv = sb("a_bv", [P, 2, H0 // 2, VW])
        mask = sb("a_mask", [P, NB0])
        kbias = sb("a_kbias", [P, NB0])
        bq, bk, b1 = sb("a_bq", [P, KT]), sb("a_bk", [P, KT]), sb("a_b1", [P, FC])
        half, eps_rms, eps_ln = (shared[n] for n in ("half", "eps_rms", "eps_ln"))

        sizes = [("xt_raw", KT * GROUP), ("x_bo", TILES * D), ("x_res", TILES * D),
                 ("q", KT * GROUP), ("k_blocks", GB * NB0 * NODES), ("v_nat", TILES * 2 * VE),
                 ("v_pairs", GB * 2 * VE), ("p", TILES * H0 * NODES), ("pt", TILES * H0 * NODES),
                 ("ctx", TILES * D), ("x1", TILES * D), ("x1_b2", TILES * D), ("silu", 2 * 512),
                 ("z", TILES * D)]
        work = sb("a_work", [P, sum(n for _, n in sizes)])
        start = {name: sum(n for _, n in sizes[:i]) for i, (name, _) in enumerate(sizes)}
        v = {name: work[:, start[name]:start[name] + n] for name, n in sizes}
        xt_raw = v["xt_raw"]
        x_bo, x_res, ctxt, x1, x1_b2, z = (
            v[n].rearrange("p (t d) -> p t d", t=TILES) for n in ("x_bo", "x_res", "ctx", "x1", "x1_b2", "z"))
        q = v["q"].rearrange("p (k n) -> p k n", k=KT)
        k_blocks = v["k_blocks"].rearrange("p (g b n) -> p g b n", g=GB, b=NB0)
        v_nat = v["v_nat"].rearrange("p (t c) -> p t c", t=TILES)
        v_pairs = v["v_pairs"].rearrange("p (g c) -> p g c", g=GB)
        prob = v["p"].rearrange("p (t c) -> p t c", t=TILES)
        pt = v["pt"].rearrange("p (t c) -> p t c", t=TILES)
        silu = v["silu"].rearrange("p (s c) -> p s c", s=2)

        adj_in = sb("a_adj", [P, TILES, NODES])
        xt = [sb(f"a_xt_{s}", [P, KT, GROUP], F32R) for s in ("hi", "lo")]
        ctx_t = [sb(f"a_ctxt_{s}", [P, TILES, D], F32R) for s in ("hi", "lo")]
        x1_t = [sb(f"a_x1t_{s}", [P, KT, GROUP], F32R) for s in ("hi", "lo")]
        hid = [sb(f"a_hid_{s}", [P, RING, 512], F32R) for s in ("hi", "lo")]
        smax = sb("a_smax", [P, TILES, H0])
        rden = sb("a_rden", [P, TILES, H0])
        ssq1, ssq2, ssq3 = (sb(f"a_ssq{i}", [P, TILES]) for i in (1, 2, 3))
        ms1, ms2, ms3 = (sb(f"a_ms{i}", [P, TILES]) for i in (1, 2, 3))
        rstd1, rstd2, rstd3 = (sb(f"a_rstd{i}", [P, TILES]) for i in (1, 2, 3))
        zsum, nmean, nmean_c = (sb(f"a_{n}", [P, TILES]) for n in ("zsum", "nmean", "nmean_c"))

        early_loaded, const_loaded, row_set = sem("early_loaded"), sem("const_loaded"), sem("row_set")
        xt_loaded, x_loaded, res_loaded, adj_loaded, x2_stored = (
            sem(n) for n in ("xt_loaded", "x_loaded", "res_loaded", "adj_loaded", "x2_stored"))
        v_swapped = [sem(f"v_swapped{t}") for t in range(TILES)]
        stage_set, pairs_zeroed = sem("stage_set"), sem("pairs_zeroed")
        qk_mm, v_mm, s_mm, pt_mm, pv_mm, ct_mm, o_mm, x1t_mm, f1_mm, f2_mm = (
            sem(n) for n in ("qk_mm", "v_mm", "s_mm", "pt_mm", "pv_mm", "ct_mm", "o_mm", "x1t_mm", "f1_mm", "f2_mm"))
        w_hi, xt_hi, q_done, x1t_hi, silu_done, hid_hi, exp_done, pt_done, ctxt_hi, sq1_done, sq2_done, sq3_done = (
            sem(n) for n in ("w_hi", "xt_hi", "q_done", "x1t_hi", "silu_done", "hid_hi", "exp_done", "pt_done",
                             "ctxt_hi", "sq1_done", "sq2_done", "sq3_done"))
        w_lo, kbias_set, xt_lo, k_done, x1t_lo, v_done, hid_lo, biased, maxed, shifted, rden_done, ctx_done = (
            sem(n) for n in ("w_lo", "kbias_set", "xt_lo", "k_done", "x1t_lo", "v_done", "hid_lo", "biased", "maxed",
                             "shifted", "rden_done", "ctx_done"))
        ctxt_lo, y1_done, x1_scaled, y2_done, z_scaled, z_done, mean_done, x2_done = (
            sem(n) for n in ("ctxt_lo", "y1_done", "x1_scaled", "y2_done", "z_scaled", "z_done", "mean_done",
                             "x2_done"))
        half_set, xbo_done, v_kept, rstd1_done, x1_done, x1b2_done, rstd2_done, rstd3_done, xres_done = (
            sem(n) for n in ("half_set", "xbo_done", "v_kept", "rstd1_done", "x1_done", "x1b2_done",
                             "rstd2_done", "rstd3_done", "xres_done"))
        ms1_done, ms2_done, ms3_done = (sem(f"ms{i}_done") for i in (1, 2, 3))

        SLOT = KT * 2 * shared["VE1"]
        pieces = [("wq", w["wq"], attn_W["wq"], k, 1, D, 0) for k in range(KT)]
        pieces += [(n, w[n], attn_W[n], 0, KT, wide[n], i + 1) for i, n in enumerate(("wk", "wv", "wo"))]
        WK, WV, WO = range(KT, KT + 3)
        parts = {"w1": [(t, c, 512) for t in range(KT) for c in range(0, F, 512)],
                 "w2": [(t, 0, D) for t in range(FC)]}
        slots = {"w1": [work[:, start[n] + i * 512:start[n] + (i + 1) * 512] for n in ("x1", "x_bo") for i in range(3)],
                 "w2": [work[:, start["silu"] + i * D:start["silu"] + (i + 1) * D] for i in range(4)]}
        next_pieces = [(n, next_w[m], attn_W[n], 0, KT, 2 * shared["VE1"] if n == "wv" else D, i)
                 for i, (n, m) in enumerate(zip(("wq", "wk", "wv", "wo"), ("Wq", "Wk", "Wv", "Wo")))]
        w_loaded = [sem(f"w_loaded{i}") for i in range(len(pieces))]
        part_loaded = {n: [sem(f"{n}_loaded{i}") for i in range(len(slots[n]))] for n in slots}
        part_hi, part_lo = ({n: sem(f"{n}_{s}_done") for n in slots} for s in ("hi", "lo"))
        next_loaded = [sem(f"next_loaded{i}") for i in range(4)]
        next_hi, next_lo, next_set = (sem(n) for n in ("next_hi", "next_lo", "next_set"))

        def stage(piece):
            _, _, _, t, k, cols, slot = piece
            at = (start["q"] + slot * SLOT if slot < 3 else start["p"]) + t * cols
            return work[:, at:at + k * cols].rearrange("p (k c) -> p k c", k=k)

        def load_piece(sp, piece, loaded, dh):
            name, dram, _, t, k, cols, _ = piece
            src = dram.rearrange("(t p) c -> p t c", p=P)[:, t:t + k]
            if name != "wv":
                sp.dma_start(stage(piece), src).then_inc(loaded, 16)
                return
            dst = stage(piece).rearrange("p k (r h c) -> p k r h c", r=2, c=dh + 1)
            src = src.rearrange("p k (h r d) -> p k r h d", r=2, d=dh)
            for kk in range(KT):
                for r in range(2):
                    sp.dma_start(dst[:, kk, r, :, 0:dh], src[:, kk, r]).then_inc(loaded, 16)

        def pieces_of(piece):
            return 16 * (2 * KT if piece[0] == "wv" else 1)

        def halves(piece, s):
            _, _, dst, t, k, cols, _ = piece
            return dst[s][:, t:t + k, 0:cols]

        def part(name, i, s):
            t, c, n = parts[name][i]
            return W[name][s][:, t, c:c + n]

        def staged(name, i):
            return slots[name][i % len(slots[name])][:, 0:parts[name][i][2]]

        N_EARLY = 5 + 2
        N_CONST = 3 + len(rows) - 1 + 2
        last = {}

        @block.sync
        def _(sp):
            def load_xt(g):
                wait(sp, xt_lo, g)
                for k in range(KT):
                    sp.dma_start(xt_raw[:, k * GROUP:(k + 1) * GROUP], xT[k, g]).then_inc(xt_loaded, 16)

            def load_adj(g):
                wait(sp, biased, TILES * g)
                sp.dma_start(adj_in[:], adj[g]).then_inc(adj_loaded, 16)

            def load_x(g):
                wait(sp, y1_done, TILES * g)
                sp.dma_start(x_bo, x[g]).then_inc(x_loaded, 16)

            def load_res(g):
                wait(sp, z_done, TILES * g)
                sp.dma_start(x_res, x[g]).then_inc(res_loaded, 16)

            def swap_v(g, t):
                a, b = TILES * t, TILES * t + 1
                sp.wait_ge(v_done, TILES * g + t + 1)
                sp.dma_start(v_pairs[64:P, a, VE:2 * VE], v_nat[0:64, t, VE:2 * VE]).then_inc(v_swapped[t], 16)
                sp.dma_start(v_pairs[0:64, b, 0:VE], v_nat[64:P, t, 0:VE]).then_inc(v_swapped[t], 16)

            def store(g):
                sp.wait_ge(x2_done, TILES * (g + 1))
                sp.dma_start(x2[g], z).then_inc(x2_stored, 16)

            def load_row(dst, name, loaded):
                sp.dma_start(dst[:], w[name].rearrange("(a d) -> a d", a=1).broadcast_to([P, D])).then_inc(loaded, 16)

            def load_bv(row, name, dh, heads, loaded):
                src = w[name].rearrange("(a h r d) -> a r h d", a=1, r=2, d=dh)
                for r in range(2):
                    sp.dma_start(row[:, r, :, 0:dh], src[:, r].broadcast_to([P, heads // 2, dh])).then_inc(loaded, 16)

            def load_consts():
                sp.wait_ge(part_lo["w1"], len(slots["w1"]))
                load_x(0)
                for name in rows:
                    if name != "bo":
                        load_row(rows[name], name, const_loaded)
                for dst, name in ((shared["mask"], "mask1"), (b1, "b1")):
                    sp.dma_start(dst[:], w[name]).then_inc(const_loaded, 16)
                load_row(shared["bo"], "bo1", const_loaded)
                load_bv(shared["bv"], "bv1", DH1, H1, const_loaded)

            load_xt(0)
            for i in range(WK + 1):
                load_piece(sp, pieces[i], w_loaded[i], DH0)
            for dst, name in ((bq, "bq"), (bk, "bk"), (mask, "mask0"), (ident, "ident")):
                sp.dma_start(dst[:], w[name]).then_inc(early_loaded, 16)
            sp.wait_ge(stage_set, 1)
            load_piece(sp, pieces[WV], w_loaded[WV], DH0)
            sp.wait_ge(row_set, 1)
            load_bv(bv, "bv", DH0, H0, early_loaded)
            load_row(rows["bo"], "bo", early_loaded)
            load_piece(sp, pieces[WO], w_loaded[WO], DH0)
            load_adj(0)

            def load_parts(name, which):
                for i in which:
                    t, c, n = parts[name][i]
                    if i >= len(slots[name]):
                        sp.wait_ge(part_lo[name], i - len(slots[name]) + 1)
                    sp.dma_start(staged(name, i), w[name][t * P:(t + 1) * P, c:c + n]).then_inc(
                        part_loaded[name][i % len(slots[name])], 16)

            def load_next():
                sp.wait_ge(next_set, 1)
                for i, piece in enumerate(next_pieces):
                    load_piece(sp, piece, next_loaded[i], DH1)

            def step(g, att=True, ffn=True, late=True, more=True):
                if att:
                    if more:
                        load_xt(g + 1)
                    if not ffn:
                        load_parts("w1", range(0, 6))
                        load_parts("w2", range(0, 2))
                        sp.wait_ge(pairs_zeroed, 1)
                    for t in range(TILES):
                        swap_v(g, t)
                    if not ffn:
                        load_parts("w2", range(2, 4))
                        load_parts("w1", range(6, 9))
                        load_consts()
                        load_parts("w2", range(4, FC))
                    if more:
                        load_adj(g + 1)
                elif ffn:
                    load_next()
                if late:
                    store(g - 2)
                if ffn:
                    load_res(g - 1)
                if att and more:
                    load_x(g + 1)

            step(0, ffn=False, late=False)
            step(1, late=False)
            with sp.Fori(2, NG - 1) as g:
                step(g)
            step(NG - 1, more=False)
            step(NG, att=False)
            last["sync"] = lambda: store(NG - 1)

        @block.tensor
        def _(pe):
            def mm3(out, lhs, rhs, first, last):
                for n, (a, b) in enumerate(((0, 0), (1, 0), (0, 1))):
                    r = pe.matmul(out, lhs[a], rhs[b], start=first and n == 0, stop=last and n == 2)
                return r

            def qk(g):
                wait(pe, xt_lo, g + 1)
                for u in range(3):
                    if isinstance(g, int) and g == 0:
                        pe.wait_ge(w_lo, WK if u == 0 else WK + 1)
                    if isinstance(g, int) and g == 1:
                        pe.wait_ge(*((q_done, u + 1) if u < 2 else (k_done, 1)))
                    elif not isinstance(g, int) or g > 1:
                        pe.wait_ge(silu_done, FP * (g - 1) - 2 + u)
                    for s in range(2):
                        m = 2 * u + s
                        n, m = ("wq", m) if m < KT else ("wk", m - KT)
                        for k in range(KT):
                            r = mm3(A[u][:, s * GROUP:(s + 1) * GROUP],
                                    [W[n][j][:, k, m * P:(m + 1) * P] for j in range(2)],
                                    [xt[j][:, k, :] for j in range(2)], k == 0, k == KT - 1)
                    r.then_inc(qk_mm, 1)

            def values(g, t, ffn):
                if isinstance(g, int) and g == 0:
                    pe.wait_ge(w_lo, WV + 1)
                if t == 0:
                    wait(pe, ctxt_lo, TILES * g)
                elif ffn:
                    pe.wait_ge(x1t_lo, TILES * (g - 1) + 1)
                out = B[2 if t == 0 else 0]
                for k in range(KT):
                    r = mm3(out[:, 0:2 * VE], [xt[j][:, k, t * P:(t + 1) * P] for j in range(2)],
                            [W["wv"][j][:, k, :] for j in range(2)], k == 0, k == KT - 1)
                r.then_inc(v_mm, 1)

            def scores(g, t, ffn):
                if t == 0:
                    pe.wait_ge(q_done, 2 * (g + 1))
                    pe.wait_ge(k_done, g + 1)
                    if ffn:
                        pe.wait_ge(x1t_lo, TILES * g)
                else:
                    pe.wait_ge(v_done, TILES * g + 1)
                out = B[1 + t]
                for k in range(KT):
                    b0, b1_, h = SPAN0[k]
                    for s in range(2):
                        n = TILES * t + s
                        r = pe.matmul(out[64 * s:64 * s + 64, h * NODES:(h + b1_ - b0) * NODES],
                                      q[:, k, n * NODES:(n + 1) * NODES],
                                      k_blocks[:, n, b0:b1_, :].rearrange("p b n -> p (b n)"),
                                      start=k == 0, stop=k == KT - 1, skip_group_check=True)
                r.then_inc(s_mm, 1)

            def turn_p(g, t):
                if isinstance(g, int) and g == 0:
                    pe.wait_ge(early_loaded, 16 * N_EARLY)
                pe.wait_ge(exp_done, TILES * g + t + 1)
                if t == 0:
                    pe.wait_ge(v_done, TILES * g + 2)
                for h in range(H0 // 2):
                    r = pe.transpose(B[2 * t][:, h * P:(h + 1) * P], prob[:, t, h * P:(h + 1) * P], ident[:])
                r.then_inc(pt_mm, 1)

            def pv(g, t):
                pe.wait_ge(pt_done, TILES * g + t + 1)
                pe.wait_ge(v_swapped[t], 32 * (g + 1))
                pe.wait_ge(v_kept, TILES * g + t + 1)
                if t == 0:
                    pe.wait_ge(biased, TILES * g + 1)
                out = B[1 - t]
                for h in range(H0 // 2):
                    for s in range(2):
                        n = TILES * t + s
                        vv = v_pairs[:, n, :].rearrange("p (r h c) -> p h r c", r=2, h=H0 // 2)[:, h]
                        r = pe.matmul(out[64 * s:64 * s + 64, h * 2 * VW:(h + 1) * 2 * VW].rearrange("p (r c) -> p r c", r=2),
                                      pt[:, t, h * P + 64 * s:h * P + 64 * s + 64], vv, start=True, stop=True,
                                      skip_group_check=True)
                r.then_inc(pv_mm, 1)

            def turn_ctx(g, t):
                pe.wait_ge(ctx_done, TILES * g + t + 1)
                if t == 1:
                    pe.wait_ge(pt_done, TILES * g + 2)
                for k in range(KT):
                    r = pe.transpose(B[1 + t][:, k * P:(k + 1) * P], ctxt[:, t, k * P:(k + 1) * P], ident[:])
                r.then_inc(ct_mm, 1)

            def attn_out(g, t):
                if isinstance(g, int) and g == 0:
                    pe.wait_ge(w_lo, WO + 1)
                pe.wait_ge(ctxt_lo, TILES * g + t + 1)
                if t == 0:
                    pe.wait_ge(ctx_done, TILES * g + 2)
                for k in range(KT):
                    r = mm3(B[t][:, 0:D], [ctx_t[j][:, t, k * P:(k + 1) * P] for j in range(2)],
                            [W["wo"][j][:, k, :] for j in range(2)], k == 0, k == KT - 1)
                r.then_inc(o_mm, 1)

            def turn_x1(f, t):
                pe.wait_ge(x1_done, TILES * f + t + 1)
                for k in range(KT):
                    r = pe.transpose(B[t][:, k * P:(k + 1) * P], x1[:, t, k * P:(k + 1) * P], ident[:])
                r.then_inc(x1t_mm, 1)

            def ffn1(f, p, att):
                if isinstance(f, int) and f == 0 and p == 0:
                    pe.wait_ge(part_lo["w1"], len(parts["w1"]))
                if p == 0:
                    pe.wait_ge(x1t_lo, TILES * (f + 1))
                if p < 3 and att:
                    pe.wait_ge(*((q_done, 2 * (f + 1) + p + 1) if p < 2 else (k_done, f + 2)))
                else:
                    pe.wait_ge(silu_done, FP * f + p - 2)
                for s in range(2):
                    m = 2 * p + s
                    for k in range(KT):
                        r = mm3(A[p % 3][:, s * GROUP:(s + 1) * GROUP],
                                [W["w1"][j][:, k, m * P:(m + 1) * P] for j in range(2)],
                                [x1_t[j][:, k, :] for j in range(2)], k == 0, k == KT - 1)
                r.then_inc(f1_mm, 1)

            def ffn2(f, p):
                pe.wait_ge(hid_lo, FP * f + p + 1)
                if p == 0:
                    wait(pe, y2_done, TILES * f)
                    if isinstance(f, int) and f == 0:
                        pe.wait_ge(part_lo["w2"], FC)
                for s in range(2):
                    for t in range(TILES):
                        c = s * GROUP + t * P
                        r = mm3(ACC[t][:, 0:D], [hid[j][:, p % RING, c:c + P] for j in range(2)],
                                [W["w2"][j][:, 2 * p + s, :] for j in range(2)],
                                p == 0 and s == 0, p == FP - 1 and s == 1)
                r.then_inc(f2_mm, 1)

            def step(g, att=True, ffn=True, more=True):
                f = g - 1
                if att and not (isinstance(g, int) and g == 1):
                    qk(g)
                if ffn:
                    for t in range(TILES):
                        turn_x1(f, t)
                if att:
                    for t in range(TILES):
                        values(g, t, ffn)
                if ffn:
                    ffn1(f, 0, att)
                    ffn1(f, 1, att)
                if att:
                    for t in range(TILES):
                        scores(g, t, ffn)
                if att and not ffn:
                    qk(g + 1)
                if ffn:
                    ffn2(f, 0)
                    ffn1(f, 2, att)
                    ffn1(f, 3, att)
                    ffn2(f, 1)
                if att:
                    for t in range(TILES):
                        turn_p(g, t)
                if ffn:
                    ffn2(f, 2)
                if att:
                    for t in range(TILES):
                        pv(g, t)
                if ffn:
                    ffn1(f, 4, att)
                    ffn2(f, 3)
                if att:
                    for t in range(TILES):
                        turn_ctx(g, t)
                if ffn:
                    ffn1(f, 5, att)
                if att:
                    for t in range(TILES):
                        attn_out(g, t)
                if ffn:
                    ffn2(f, 4)
                    ffn2(f, 5)

            step(0, ffn=False)
            step(1)
            with pe.Fori(2, NG - 1) as g:
                step(g)
            step(NG - 1, more=False)
            step(NG, att=False)

        @block.scalar
        def _(act):
            def high(piece, loaded, done):
                act.wait_ge(loaded, pieces_of(piece))
                act.activation(halves(piece, 0), stage(piece), ACT.Copy).then_inc(done, 1)

            def part_high(name, which):
                for i in which:
                    act.wait_ge(part_loaded[name][i % len(slots[name])], 16 * (i // len(slots[name]) + 1))
                    act.activation(part(name, i, 0), staged(name, i), ACT.Copy).then_inc(part_hi[name], 1)

            def split_x(g):
                act.wait_ge(xt_loaded, 16 * KT * (g + 1))
                wait(act, v_mm, TILES * g)
                act.activation(xt[0][:].rearrange("p k n -> p (k n)"), xt_raw, ACT.Copy).then_inc(xt_hi, 1)

            def take_q(g):
                wait(act, s_mm, TILES * g)
                act.wait_ge(qk_mm, 3 * g + 1)
                for m in range(2):
                    r = act.activation(q[:, m, :], A[0][:, m * GROUP:(m + 1) * GROUP], ACT.Identity, bias=bq[:, m:m + 1])
                r.then_inc(q_done, 1)
                act.wait_ge(qk_mm, 3 * g + 2)
                act.activation(q[:, 2, :], A[1][:, 0:GROUP], ACT.Identity, bias=bq[:, 2:3])
                for b in range(*SPAN0[0][:2]):
                    r = act.activation(k_blocks[:, :, b, :], A[1][:, GROUP:2 * GROUP].rearrange("p (g n) -> p g n", g=GB),
                                       ACT.Identity, bias=kbias[:, b:b + 1], scale=mask[:, b:b + 1])
                r.then_inc(q_done, 1)

            def keep_v(g, t):
                a, b = TILES * t, TILES * t + 1
                act.wait_ge(v_done, TILES * g + t + 1)
                act.activation(v_pairs[0:64, a, 0:VE], v_nat[0:64, t, 0:VE], ACT.Copy)
                act.activation(v_pairs[64:P, b, VE:2 * VE], v_nat[64:P, t, VE:2 * VE], ACT.Copy).then_inc(v_kept, 1)

            def x1t_high(f, t):
                act.wait_ge(x1t_mm, TILES * f + t + 1)
                wait(act, f1_mm, FP * f)
                act.activation(x1_t[0][:, :, t * P:(t + 1) * P], B[t][:, 0:D].rearrange("p (k n) -> p k n", k=KT),
                               ACT.Copy).then_inc(x1t_hi, 1)

            def hidden(f, p):
                act.wait_ge(f1_mm, FP * f + p + 1)
                if isinstance(f, int) and f == 0 and p == 0:
                    act.wait_ge(part_lo["w2"], FC)
                wait(act, hid_lo, FP * f + p - 1)
                for s in range(2):
                    m = 2 * p + s
                    r = act.activation(silu[:, p % 2, s * GROUP:(s + 1) * GROUP], A[p % 3][:, s * GROUP:(s + 1) * GROUP],
                                       ACT.Silu, bias=b1[:, m:m + 1])
                r.then_inc(silu_done, 1)
                act.wait_ge(silu_done, FP * f + p + 1)
                wait(act, f2_mm, FP * f + p + 1 - RING)
                act.activation(hid[0][:, p % RING, :], silu[:, p % 2, :], ACT.Copy).then_inc(hid_hi, 1)

            def exp(g, t):
                act.wait_ge(shifted, TILES * g + t + 1)
                act.activation(prob[:, t, :], prob[:, t, :], ACT.Exp).then_inc(exp_done, 1)

            def take_pt(g, t):
                act.wait_ge(pt_mm, TILES * g + t + 1)
                wait(act, pv_mm, TILES * (g - 1) + t + 1)
                act.activation(pt[:, t, :], B[2 * t][:, :], ACT.Copy).then_inc(pt_done, 1)

            def ctxt_high(g, t):
                act.wait_ge(ct_mm, TILES * g + t + 1)
                wait(act, o_mm, TILES * (g - 1) + t + 1)
                act.activation(ctx_t[0][:, t, :], B[1 + t][:, 0:D], ACT.Copy).then_inc(ctxt_hi, 1)

            def square(src, done, out, result, n, t, junk, bias=0.0):
                act.wait_ge(done, n)
                act.activation(junk, src[:, t, :], ACT.Square, bias=bias, scale=ROOT, accum_out=out[:, t:t + 1]).then_inc(result, 1)

            def mean_square(f):
                for t in range(TILES):
                    square(z, y2_done, ssq2, sq2_done, TILES * f + t + 1, t, silu[:, t, 0:D])

            def variance(e):
                for t in range(TILES):
                    square(z, mean_done, ssq3, sq3_done, 2 * (e + 1), t, ctxt[:, t, :], bias=nmean_c[:, t:t + 1])

            split_x(0)
            for i in range(WV + 1):
                high(pieces[i], w_loaded[i], w_hi)
            act.wait_ge(early_loaded, 16 * N_EARLY)
            act.wait_ge(kbias_set, 1)

            def step(g, att=True, ffn=True, late=True, more=True):
                f, e = g - 1, g - 2
                fresh = att and not ffn
                if att:
                    take_q(g)
                if fresh:
                    high(pieces[WO], w_loaded[WO], w_hi)
                if ffn:
                    for t in range(TILES):
                        x1t_high(f, t)
                if ffn and isinstance(f, int) and f == 0:
                    part_high("w2", range(8, FC))
                if late and att:
                    variance(e)
                if ffn:
                    hidden(f, 0)
                if late and not att:
                    variance(e)
                if fresh:
                    split_x(g + 1)
                    act.wait_ge(pairs_zeroed, 1)
                if att:
                    for t in range(TILES):
                        keep_v(g, t)
                if ffn:
                    hidden(f, 1)
                if fresh:
                    part_high("w1", range(0, 6))
                if att:
                    for t in range(TILES):
                        exp(g, t)
                if fresh:
                    part_high("w1", range(6, 9))
                if ffn:
                    hidden(f, 2)
                if att:
                    for t in range(TILES):
                        take_pt(g, t)
                if ffn:
                    for p in (3, 4):
                        if not att:
                            high(next_pieces[p - 3], next_loaded[p - 3], next_hi)
                        hidden(f, p)
                if fresh:
                    part_high("w2", range(0, 4))
                elif att and more:
                    split_x(g + 1)
                if att:
                    for t in range(TILES):
                        ctxt_high(g, t)
                elif ffn:
                    high(next_pieces[2], next_loaded[2], next_hi)
                if ffn:
                    hidden(f, 5)
                if att:
                    for t in range(TILES):
                        square(x1, y1_done, ssq1, sq1_done, TILES * g + t + 1, t, ctxt[:, t, :])
                if fresh:
                    part_high("w2", range(4, 8))
                    act.wait_ge(const_loaded, 16 * N_CONST)
                if not att and ffn:
                    high(next_pieces[3], next_loaded[3], next_hi)
                if ffn and att:
                    mean_square(f)

            step(0, ffn=False, late=False)
            step(1, late=False)
            with act.Fori(2, NG - 1) as g:
                step(g)
            step(NG - 1, more=False)
            step(NG, att=False)
            last["scalar"] = (lambda: mean_square(NG - 1), lambda: variance(NG - 1))

        @block.vector
        def _(dve):
            dve.memset(bv[:], 1.0)
            dve.memset(shared["bv"][:], 1.0).then_inc(row_set, 1)
            dve.memset(stage(pieces[WV]), 0.0).then_inc(stage_set, 1)

            def low(piece, hi, count, done):
                dve.wait_ge(hi, count)
                dve.tensor_tensor(halves(piece, 1), stage(piece),
                                  halves(piece, 0).bitcast(F32), ALU.subtract).then_inc(done, 1)

            def part_low(which):
                for i in which:
                    dve.wait_ge(part_hi["w2"], i + 1)
                    dve.tensor_tensor(part("w2", i, 1), staged("w2", i), part("w2", i, 0).bitcast(F32),
                                      ALU.subtract).then_inc(part_lo["w2"], 1)

            def split_x(g):
                dve.wait_ge(xt_hi, g + 1)
                dve.tensor_tensor(xt[1][:].rearrange("p k n -> p (k n)"), xt_raw,
                                  xt[0][:].bitcast(F32).rearrange("p k n -> p (k n)"), ALU.subtract).then_inc(xt_lo, 1)

            def take_k(g):
                dve.wait_ge(qk_mm, 3 * g + 3)
                wait(dve, s_mm, TILES * g)
                for k in (1, 2):
                    for b in range(*SPAN0[k][:2]):
                        r = dve.tensor_scalar(k_blocks[:, :, b, :],
                                              A[2][:, (k - 1) * GROUP:k * GROUP].rearrange("p (g n) -> p g n", g=GB),
                                              bk[:, k:k + 1], mask[:, b:b + 1], ALU.add, ALU.mult)
                r.then_inc(k_done, 1)

            def x1t_low(f, t):
                dve.wait_ge(x1t_hi, TILES * f + t + 1)
                hi, lo = (x1_t[j][:, :, t * P:(t + 1) * P] for j in range(2))
                dve.tensor_tensor(lo, B[t][:, 0:D].rearrange("p (k n) -> p k n", k=KT), hi.bitcast(F32),
                                  ALU.subtract).then_inc(x1t_lo, 1)

            def take_v(g, t):
                dve.wait_ge(v_mm, TILES * g + t + 1)
                wait(dve, v_swapped[t], 32 * g)
                wait(dve, v_kept, TILES * (g - 1) + t + 1)
                wait(dve, pv_mm, TILES * (g - 1) + t + 1)
                dve.tensor_tensor(v_nat[:, t, :], B[2 if t == 0 else 0][:, 0:2 * VE],
                                  bv[:].rearrange("p r h c -> p (r h c)"), ALU.add).then_inc(v_done, 1)

            def hidden_low(f, p):
                dve.wait_ge(hid_hi, FP * f + p + 1)
                dve.tensor_tensor(hid[1][:, p % RING, :], silu[:, p % 2, :], hid[0][:, p % RING, :].bitcast(F32),
                                  ALU.subtract).then_inc(hid_lo, 1)

            def soften(g, t):
                s = prob[:, t, :].rearrange("p (h n) -> p h n", h=H0)
                dve.wait_ge(s_mm, TILES * g + t + 1)
                if t == 0:
                    dve.wait_ge(adj_loaded, 16 * (g + 1))
                wait(dve, pt_mm, TILES * (g - 1) + t + 1)
                dve.scalar_tensor_tensor(out=s, in0=B[1 + t][:, :].rearrange("p (h n) -> p h n", h=H0), scalar=SCALE0,
                                         in1=adj_in[:, t, :].unsqueeze(1).broadcast_to([P, H0, NODES]),
                                         op0=ALU.mult, op1=ALU.add).then_inc(biased, 1)
                dve.wait_ge(biased, TILES * g + t + 1)
                dve.tensor_reduce(smax[:, t, :], s, AX_X, ALU.max).then_inc(maxed, 1)
                dve.wait_ge(maxed, TILES * g + t + 1)
                dve.tensor_tensor(s, s, smax[:, t, :].unsqueeze(2).broadcast_to([P, H0, NODES]),
                                  ALU.subtract).then_inc(shifted, 1)

            def take_ctx(g, t):
                o = B[1 - t][:, 0:2 * VE].rearrange("p (h c) -> p h c", c=VW)
                dve.wait_ge(pv_mm, TILES * g + t + 1)
                dve.reciprocal(rden[:, t, :], o[:, :, DH0]).then_inc(rden_done, 1)
                dve.wait_ge(rden_done, TILES * g + t + 1)
                wait(dve, ct_mm, TILES * (g - 1) + t + 1)
                dve.tensor_tensor(ctxt[:, t, :].rearrange("p (h c) -> p h c", h=H0), o[:, :, 0:DH0],
                                  rden[:, t, :].unsqueeze(2).broadcast_to([P, H0, DH0]), ALU.mult).then_inc(ctx_done, 1)

            def ctxt_low(g, t):
                dve.wait_ge(ctxt_hi, TILES * g + t + 1)
                dve.tensor_tensor(ctx_t[1][:, t, :], B[1 + t][:, 0:D], ctx_t[0][:, t, :].bitcast(F32),
                                  ALU.subtract).then_inc(ctxt_lo, 1)

            def take_y1(g, t):
                dve.wait_ge(o_mm, TILES * g + t + 1)
                if t == 0:
                    dve.wait_ge(xbo_done, g + 1)
                wait(dve, x1t_mm, TILES * (g - 1) + t + 1)
                wait(dve, x1b2_done, TILES * (g - 1) + t + 1)
                dve.tensor_tensor(x1[:, t, :], B[t][:, 0:D], x_bo[:, t, :], ALU.add).then_inc(y1_done, 1)

            def scale_x1(g, t):
                dve.wait_ge(rstd1_done, g + 1)
                dve.scalar_tensor_tensor(out=x1[:, t, :], in0=x1[:, t, :], scalar=rstd1[:, t:t + 1], in1=rows["alpha1"][:],
                                         op0=ALU.mult, op1=ALU.mult).then_inc(x1_scaled, 1)

            def take_y2(f, t):
                dve.wait_ge(f2_mm, FP * (f + 1))
                dve.wait_ge(x1b2_done, TILES * f + t + 1)
                if t == 0:
                    wait(dve, x2_stored, 16 * f)
                dve.tensor_tensor(z[:, t, :], ACC[t][:, 0:D], x1_b2[:, t, :], ALU.add).then_inc(y2_done, 1)

            def rms_norm(e):
                dve.wait_ge(rstd2_done, e + 1)
                for t in range(TILES):
                    dve.scalar_tensor_tensor(out=z[:, t, :], in0=z[:, t, :], scalar=rstd2[:, t:t + 1],
                                             in1=rows["alpha2"][:], op0=ALU.mult, op1=ALU.mult).then_inc(z_scaled, 1)
                dve.wait_ge(xres_done, e + 1)
                for t in range(TILES):
                    dve.wait_ge(z_scaled, TILES * e + t + 1)
                    dve.scalar_tensor_tensor(out=z[:, t, :], in0=z[:, t, :], scalar=1.0, in1=x_res[:, t, :], op0=ALU.mult,
                                             op1=ALU.add, accum_out=zsum[:, t:t + 1]).then_inc(z_done, 1)
                dve.wait_ge(z_done, TILES * (e + 1))
                dve.tensor_scalar(nmean[:], zsum[:], -1.0 / D, None, ALU.mult).then_inc(mean_done, 1)
                dve.tensor_scalar(nmean_c[:], zsum[:], -ROOT / D, None, ALU.mult).then_inc(mean_done, 1)

            def layer_norm(e):
                dve.wait_ge(rstd3_done, e + 1)
                for t in range(TILES):
                    dve.tensor_scalar(z[:, t, :], z[:, t, :], nmean[:, t:t + 1], rstd3[:, t:t + 1],
                                      ALU.add, ALU.mult).then_inc(x2_done, 1)

            split_x(0)
            for i in range(WV + 1):
                low(pieces[i], w_hi, i + 1, w_lo)
            dve.wait_ge(early_loaded, 16 * N_EARLY)
            dve.wait_ge(w_lo, WV + 1)
            for k in range(KT):
                b0, b1_, _h = SPAN0[k]
                r = dve.tensor_scalar(kbias[:, b0:b1_], mask[:, b0:b1_], bk[:, k:k + 1], None, ALU.mult)
            r.then_inc(kbias_set, 1)
            def step(g, att=True, ffn=True, late=True, more=True):
                f, e = g - 1, g - 2
                fresh = att and not ffn
                if ffn:
                    for t in range(TILES):
                        x1t_low(f, t)
                if ffn and isinstance(f, int) and f == 0:
                    part_low(range(8, FC))
                if ffn and not att:
                    rms_norm(f - 1)
                if att:
                    take_k(g)
                    for t in range(TILES):
                        take_v(g, t)
                if ffn and not att:
                    dve.wait_ge(o_mm, TILES * NG)
                    dve.memset(stage(next_pieces[2]), 0.0).then_inc(next_set, 1)
                if late and att:
                    layer_norm(e)
                if ffn:
                    hidden_low(f, 0)
                if fresh:
                    split_x(g + 1)
                    low(pieces[WO], w_hi, WO + 1, w_lo)
                    dve.wait_ge(w_lo, WO + 1)
                if att:
                    for t in range(TILES):
                        soften(g, t)
                if ffn:
                    hidden_low(f, 1)
                if late and not att:
                    layer_norm(e)
                if ffn:
                    hidden_low(f, 2)
                if ffn:
                    if not att:
                        low(next_pieces[0], next_hi, 1, next_lo)
                    hidden_low(f, 3)
                if att:
                    for t in range(TILES):
                        take_ctx(g, t)
                if ffn:
                    if not att:
                        low(next_pieces[1], next_hi, 2, next_lo)
                    hidden_low(f, 4)
                if att and more and not fresh:
                    split_x(g + 1)
                if att:
                    for t in range(TILES):
                        ctxt_low(g, t)
                elif ffn:
                    low(next_pieces[2], next_hi, 3, next_lo)
                if ffn:
                    hidden_low(f, 5)
                if fresh:
                    part_low(range(0, 4))
                    dve.wait_ge(part_lo["w1"], len(parts["w1"]))
                if att:
                    for t in range(TILES):
                        take_y1(g, t)
                if fresh:
                    part_low(range(4, 6))
                    dve.wait_ge(const_loaded, 16 * N_CONST)
                if att:
                    for t in range(TILES):
                        scale_x1(g, t)
                if fresh:
                    part_low(range(6, 8))
                if ffn and not att:
                    low(next_pieces[3], next_hi, 4, next_lo)
                if ffn:
                    for t in range(TILES):
                        take_y2(f, t)
                if ffn and att and more:
                    rms_norm(f)

            step(0, ffn=False, late=False)
            step(1, late=False)
            with dve.Fori(2, NG - 1) as g:
                step(g)
            step(NG - 1, more=False)
            step(NG, att=False)
            last["vector"] = (lambda: rms_norm(NG - 1), lambda: layer_norm(NG - 1))

        @block.gpsimd
        def _(pool):
            pool.memset(half[:], -0.5).then_inc(half_set, 1)
            pool.memset(eps_rms[:], EPS_RMS).then_inc(half_set, 1)
            pool.memset(eps_ln[:], EPS_LN).then_inc(half_set, 1)
            pool.wait_ge(half_set, 3)
            pool.memset(v["v_pairs"], 0.0).then_inc(pairs_zeroed, 1)

            def part_low():
                for i in range(len(parts["w1"])):
                    pool.wait_ge(part_hi["w1"], i + 1)
                    pool.tensor_tensor(part("w1", i, 1), staged("w1", i), part("w1", i, 0).bitcast(F32),
                                       ALU.subtract).then_inc(part_lo["w1"], 1)

            def add_row(tensor, row, t):
                return pool.tensor_tensor(tensor[:, t, :], tensor[:, t, :], rows[row][:], ALU.add)

            def bias_x(g):
                pool.wait_ge(x_loaded, 16 * (g + 1))
                for t in range(TILES):
                    r = add_row(x_bo, "bo", t)
                r.then_inc(xbo_done, 1)

            def bias_res(e):
                pool.wait_ge(res_loaded, 16 * (e + 1))
                for t in range(TILES):
                    r = add_row(x_res, "gamma2", t)
                r.then_inc(xres_done, 1)

            def root(g, mean_sq, ready, ms, ms_done, eps, out, done):
                pool.wait_ge(ready, TILES * (g + 1))
                pool.tensor_tensor(ms[:], mean_sq[:], eps[:], ALU.add).then_inc(ms_done, 1)
                pool.wait_ge(ms_done, g + 1)
                pool.tensor_tensor(out[:], ms[:], half[:], ALU.pow).then_inc(done, 1)

            def step(g, att=True, ffn=True, late=True, more=True):
                f, e = g - 1, g - 2
                if late:
                    root(e, ssq3, sq3_done, ms3, ms3_done, eps_ln, rstd3, rstd3_done)
                if ffn:
                    bias_res(f)
                if att and not ffn:
                    part_low()
                    pool.wait_ge(early_loaded, 16 * N_EARLY)
                if att:
                    bias_x(g)
                if att and not ffn:
                    pool.wait_ge(const_loaded, 16 * N_CONST)
                if att:
                    root(g, ssq1, sq1_done, ms1, ms1_done, eps_rms, rstd1, rstd1_done)
                    for t in range(TILES):
                        pool.wait_ge(x1_scaled, TILES * g + t + 1)
                        add_row(x1, "gamma1", t).then_inc(x1_done, 1)
                if ffn:
                    root(f, ssq2, sq2_done, ms2, ms2_done, eps_rms, rstd2, rstd2_done)
                if att:
                    for t in range(TILES):
                        pool.wait_ge(x1_done, TILES * g + t + 1)
                        wait(pool, y2_done, TILES * (g - 1) + t + 1)
                        pool.tensor_tensor(x1_b2[:, t, :], x1[:, t, :], rows["b2"][:], ALU.add).then_inc(x1b2_done, 1)

            step(0, ffn=False, late=False)
            step(1, late=False)
            with pool.Fori(2, NG - 1) as g:
                step(g)
            step(NG - 1, more=False)
            step(NG, att=False)
            last["gpsimd"] = lambda: root(NG - 1, ssq3, sq3_done, ms3, ms3_done, eps_ln, rstd3, rstd3_done)

    return last, {"f1_mm": (f1_mm, FP * NG), "silu_done": (silu_done, FP * NG), "y2_done": (y2_done, TILES * NG),
                  "next_lo": (next_lo, len(next_pieces)), "x2_stored": x2_stored}


def layer1(nc, block, sem, x2, adj, out, shared, last, free):
    VW = DH1 + 1
    VE = H1 // 2 * VW
    S = H1 * NODES
    with ExitStack() as ctx:
        def sb(name, shape, dt=F32):
            return ctx.enter_context(nc.sbuf_tensor(name, shape, dt))

        one = [ctx.enter_context(nc.psum_tensor(f"b_bank{i}", [P, 512], F32)) for i in range(4)]
        two = [ctx.enter_context(nc.psum_tensor(f"b_banks{i}", [P, 1024], F32)) for i in range(2)]

        W = {n: shared["W"][n.lower()] for n in ("Wq", "Wk", "Wv", "Wo")}
        ident, mask, bo = shared["ident"], shared["mask"], shared["bo"]
        half, eps_ln, bv = shared["half"], shared["eps_ln"], shared["bv"]

        x_in, res, y = sb("b_x", [P, TILES, D]), sb("b_res", [P, TILES, D]), sb("b_y", [P, TILES, D])
        adj_in, bias = sb("b_adj", [P, TILES, NODES]), sb("b_bias", [P, TILES, NODES])
        v_pairs = sb("b_v_pairs", [P, GB, 2 * VE])
        xt = [sb(f"b_xt_{s}", [P, KT, GROUP], F32R) for s in ("hi", "lo")]
        q = sb("b_q", [P, KT, GROUP])
        k_blocks = sb("b_k_blocks", [P, GB, NB1, NODES])
        v_nat = sb("b_v_nat", [P, TILES, 2 * VE])
        score, prob, pt = (sb(f"b_{n}", [P, TILES, S]) for n in ("score", "p", "pt"))
        ctxt = sb("b_ctx", [P, TILES, D])
        unused = sb("b_unused", [P, TILES, D])
        ctx_t = [sb(f"b_ctxt_{s}", [P, TILES, D], F32R) for s in ("hi", "lo")]
        smax, samax, rden = (sb(f"b_{n}", [P, TILES, H1]) for n in ("smax", "samax", "rden"))
        ysum, nmean, nmean_c, ssq = (sb(f"b_{n}", [P, TILES]) for n in ("ysum", "nmean", "nmean_c", "ssq"))
        var, rstd = sb("b_var", [P, TILES]), sb("b_rstd", [P, TILES])

        pairs_zeroed = sem("b_pairs_zeroed")
        x_loaded, res_loaded, adj_loaded, out_stored = (sem("b_" + n) for n in (
            "x_loaded", "res_loaded", "adj_loaded", "out_stored"))
        v_swapped = [sem(f"b_v_swapped{t}") for t in range(TILES)]
        xt_mm, qk_mm, v_mm, s_mm, pt_mm, pv_mm, ct_mm, o_mm = (sem("b_" + n) for n in (
            "xt_mm", "qk_mm", "v_mm", "s_mm", "pt_mm", "pv_mm", "ct_mm", "o_mm"))
        xt_hi, q_done, exp_done, pt_done, ctxt_hi = (sem("b_" + n) for n in (
            "xt_hi", "q_done", "exp_done", "pt_done", "ctxt_hi"))
        xt_lo, k_done, v_done, biased, maxed, magnitude, rden_done, rden_masked, ctx_done, ctxt_lo = (
            sem("b_" + n) for n in ("xt_lo", "k_done", "v_done", "biased", "maxed", "magnitude", "rden_done",
                                    "rden_masked", "ctx_done", "ctxt_lo"))
        y_done, mean_done, out_done, sq_done = (sem("b_" + n) for n in ("y_done", "mean_done", "out_done", "sq_done"))
        bias_done, v_kept, shifted, var_done, rstd_done, res_done = (sem("b_" + n) for n in (
            "bias_done", "v_kept", "shifted", "var_done", "rstd_done", "res_done"))

        @block.sync
        def _(sp):
            def load_x(g):
                wait(sp, xt_mm, TILES * g)
                sp.dma_start(x_in[:], x2[g]).then_inc(x_loaded, 16)

            def load_res(g):
                wait(sp, y_done, TILES * g)
                sp.dma_start(res[:], x2[g]).then_inc(res_loaded, 16)

            def load_adj(g):
                wait(sp, bias_done, g)
                sp.dma_start(adj_in[:], adj[g]).then_inc(adj_loaded, 16)

            def swap_v(g, t):
                a, b = TILES * t, TILES * t + 1
                sp.wait_ge(v_done, TILES * g + t + 1)
                sp.dma_start(v_pairs[64:P, a, VE:2 * VE], v_nat[0:64, t, VE:2 * VE]).then_inc(v_swapped[t], 16)
                sp.dma_start(v_pairs[0:64, b, 0:VE], v_nat[64:P, t, 0:VE]).then_inc(v_swapped[t], 16)

            def store(g):
                sp.wait_ge(out_done, TILES * (g + 1))
                sp.dma_start(out[g], y[:]).then_inc(out_stored, 16)

            sp.wait_ge(*free["f1_mm"])
            sp.wait_ge(free["x2_stored"], 16 * (NG - 1))
            load_x(0)
            load_adj(0)

            def step(g, front=True, back=True, late=True, more=True):
                if front and more:
                    load_x(g + 1)
                if front and not back:
                    last["sync"]()
                if late:
                    store(g - 2)
                if back:
                    load_res(g - 1)
                if front:
                    for t in range(TILES):
                        swap_v(g, t)
                    if more:
                        load_adj(g + 1)

            step(0, back=False, late=False)
            sp.wait_ge(free["x2_stored"], 16 * NG)
            step(1, late=False)
            with sp.Fori(2, NG - 1) as g:
                step(g)
            step(NG - 1, more=False)
            step(NG, front=False)
            step(NG + 1, front=False, back=False)
            sp.wait_ge(out_stored, 16 * NG)

        @block.tensor
        def _(pe):
            def mm3(out, lhs, rhs, first, last):
                for n, (a, b) in enumerate(((0, 0), (1, 0), (0, 1))):
                    r = pe.matmul(out, lhs[a], rhs[b], start=first and n == 0, stop=last and n == 2)
                return r

            def turn_x(g, t):
                pe.wait_ge(x_loaded, 16 * (g + 1))
                wait(pe, q_done, 2 * g)
                wait(pe, k_done, g)
                for k in range(KT):
                    r = pe.transpose(one[1 + t][:, k * P:(k + 1) * P], x_in[:, t, k * P:(k + 1) * P], ident[:])
                r.then_inc(xt_mm, 1)

            def qk(g):
                pe.wait_ge(xt_lo, TILES * (g + 1))
                wait(pe, ctxt_lo, TILES * (g - 1))
                for u in range(3):
                    for s in range(2):
                        m = 2 * u + s
                        n, m = ("Wq", m) if m < KT else ("Wk", m - KT)
                        for k in range(KT):
                            r = mm3(one[u][:, s * GROUP:(s + 1) * GROUP],
                                    [W[n][j][:, k, m * P:(m + 1) * P] for j in range(2)],
                                    [xt[j][:, k, :] for j in range(2)], k == 0, k == KT - 1)
                    r.then_inc(qk_mm, 1)

            def values(g, t):
                if t == 0:
                    wait(pe, y_done, TILES * (g - 1))
                else:
                    pe.wait_ge(q_done, 2 * g + 1)
                out = one[3 if t == 0 else 0]
                for k in range(KT):
                    r = mm3(out[:, 0:2 * VE], [xt[j][:, k, t * P:(t + 1) * P] for j in range(2)],
                            [W["Wv"][j][:, k, :] for j in range(2)], k == 0, k == KT - 1)
                r.then_inc(v_mm, 1)

            def scores(g, t, back):
                pe.wait_ge(q_done, 2 * (g + 1))
                pe.wait_ge(k_done, g + 1)
                if back:
                    pe.wait_ge(pt_done, TILES * (g - 1) + t + 1)
                for k in range(KT):
                    b0, b1_, h = SPAN1[k]
                    for s in range(2):
                        n = TILES * t + s
                        r = pe.matmul(two[t][64 * s:64 * s + 64, h * NODES:(h + b1_ - b0) * NODES],
                                      q[:, k, n * NODES:(n + 1) * NODES],
                                      k_blocks[:, n, b0:b1_, :].rearrange("p b n -> p (b n)"),
                                      start=True, stop=True, skip_group_check=True)
                r.then_inc(s_mm, 1)

            def turn_p(g, t):
                pe.wait_ge(exp_done, TILES * g + t + 1)
                if t == 0:
                    wait(pe, y_done, TILES * g)
                for h in range(H1 // 2):
                    r = pe.transpose(two[t][:, h * P:(h + 1) * P], prob[:, t, h * P:(h + 1) * P], ident[:])
                r.then_inc(pt_mm, 1)

            def pv(g, t, front):
                pe.wait_ge(pt_done, TILES * g + t + 1)
                pe.wait_ge(v_swapped[t], 32 * (g + 1))
                pe.wait_ge(v_kept, TILES * g + t + 1)
                if front:
                    pe.wait_ge(*((q_done, 2 * (g + 2)) if t == 0 else (k_done, g + 2)))
                for s in range(2):
                    for h in range(H1 // 2):
                        n = TILES * t + s
                        vv = v_pairs[:, n, :].rearrange("p (r h c) -> p h r c", r=2, h=H1 // 2)[:, h]
                        r = pe.matmul(one[1 + t][64 * s:64 * s + 64, h * 2 * VW:(h + 1) * 2 * VW].rearrange("p (r c) -> p r c", r=2),
                                      pt[:, t, h * P + 64 * s:h * P + 64 * s + 64], vv, start=True, stop=True,
                                      skip_group_check=True)
                r.then_inc(pv_mm, 1)

            def turn_ctx(g, t, front):
                pe.wait_ge(ctx_done, TILES * g + t + 1)
                if front:
                    pe.wait_ge(v_done, TILES * (g + 1) + t + 1)
                for k in range(KT):
                    r = pe.transpose(one[3 if t == 0 else 0][:, k * P:(k + 1) * P], ctxt[:, t, k * P:(k + 1) * P], ident[:])
                r.then_inc(ct_mm, 1)

            def attn_out(g, t, front):
                pe.wait_ge(ctxt_lo, TILES * g + t + 1)
                if t == 1 and front:
                    pe.wait_ge(biased, TILES * (g + 1) + 1)
                o = one[3] if t == 0 else two[0]
                for k in range(KT):
                    r = mm3(o[:, 0:D], [ctx_t[j][:, t, k * P:(k + 1) * P] for j in range(2)],
                            [W["Wo"][j][:, k, :] for j in range(2)], k == 0, k == KT - 1)
                r.then_inc(o_mm, 1)

            pe.wait_ge(*free["silu_done"])
            for t in range(TILES):
                turn_x(0, t)
            pe.wait_ge(*free["next_lo"])
            pe.wait_ge(*free["y2_done"])

            def step(g, front=True, back=True, more=True):
                b = g - 1
                if front:
                    qk(g)
                if back:
                    for t in range(TILES):
                        turn_p(b, t)
                if front:
                    values(g, 0)
                if back:
                    for t in range(TILES):
                        pv(b, t, front)
                if front:
                    values(g, 1)
                if back:
                    turn_ctx(b, 0, front)
                if front and more:
                    for t in range(TILES):
                        if back:
                            pe.wait_ge(ctx_done, TILES * b + t + 1)
                        turn_x(g + 1, t)
                if back:
                    turn_ctx(b, 1, front)
                if front:
                    for t in range(TILES):
                        scores(g, t, back)
                if back:
                    for t in range(TILES):
                        attn_out(b, t, front)

            step(0, back=False)
            step(1)
            with pe.Fori(2, NG - 1) as g:
                step(g)
            step(NG - 1, more=False)
            step(NG, front=False)

        @block.scalar
        def _(act):
            def xt_high(g, t):
                act.wait_ge(xt_mm, TILES * g + t + 1)
                wait(act, v_mm, TILES * g)
                act.activation(xt[0][:, :, t * P:(t + 1) * P], one[1 + t][:, 0:D].rearrange("p (k n) -> p k n", k=KT),
                               ACT.Copy).then_inc(xt_hi, 1)

            def take_q(g):
                wait(act, s_mm, TILES * g)
                act.wait_ge(qk_mm, 3 * g + 1)
                act.activation(q[:, 0:2, :].rearrange("p k n -> p (k n)"), one[0][:], ACT.Copy).then_inc(q_done, 1)
                act.wait_ge(qk_mm, 3 * g + 2)
                act.activation(q[:, 2, :], one[1][:, 0:GROUP], ACT.Copy)
                for b in range(*SPAN1[0][:2]):
                    r = act.activation(k_blocks[:, :, b, :], one[1][:, GROUP:2 * GROUP].rearrange("p (g n) -> p g n", g=GB),
                                       ACT.Copy, scale=mask[:, b:b + 1])
                r.then_inc(q_done, 1)

            def keep_v(g, t):
                a, b = TILES * t, TILES * t + 1
                act.wait_ge(v_done, TILES * g + t + 1)
                act.activation(v_pairs[0:64, a, 0:VE], v_nat[0:64, t, 0:VE], ACT.Copy)
                act.activation(v_pairs[64:P, b, VE:2 * VE], v_nat[64:P, t, VE:2 * VE], ACT.Copy).then_inc(v_kept, 1)

            def exp(g, t):
                act.wait_ge(shifted, TILES * g + t + 1)
                act.activation(prob[:, t, :], prob[:, t, :], ACT.Exp).then_inc(exp_done, 1)

            def take_pt(g, t):
                act.wait_ge(pt_mm, TILES * g + t + 1)
                wait(act, pv_mm, TILES * (g - 1) + t + 1)
                act.activation(pt[:, t, :], two[t][:, 0:S], ACT.Copy).then_inc(pt_done, 1)

            def ctxt_high(g, t):
                act.wait_ge(ct_mm, TILES * g + t + 1)
                wait(act, o_mm, TILES * (g - 1) + t + 1)
                act.activation(ctx_t[0][:, t, :], one[3 if t == 0 else 0][:, 0:D], ACT.Copy).then_inc(ctxt_hi, 1)

            def square(g, t):
                act.wait_ge(mean_done, 2 * (g + 1))
                act.activation(unused[:, t, :], y[:, t, :], ACT.Square, bias=nmean_c[:, t:t + 1], scale=ROOT,
                               accum_out=ssq[:, t:t + 1]).then_inc(sq_done, 1)

            for t in range(TILES):
                xt_high(0, t)
            last["scalar"][0]()
            act.wait_ge(pairs_zeroed, 1)

            def step(g, front=True, back=True, late=True, more=True):
                b = g - 1
                if front:
                    take_q(g)
                if front and not back:
                    last["scalar"][1]()
                if back:
                    for t in range(TILES):
                        take_pt(b, t)
                if late:
                    for t in range(TILES):
                        square(g - 2, t)
                if front:
                    for t in range(TILES):
                        keep_v(g, t)
                if back:
                    ctxt_high(b, 0)
                if front and more:
                    for t in range(TILES):
                        xt_high(g + 1, t)
                if back:
                    ctxt_high(b, 1)
                if front:
                    for t in range(TILES):
                        exp(g, t)

            step(0, back=False, late=False)
            step(1, late=False)
            with act.Fori(2, NG - 1) as g:
                step(g)
            step(NG - 1, more=False)
            step(NG, front=False)
            step(NG + 1, front=False, back=False)

        @block.vector
        def _(dve):
            def xt_low(g, t):
                dve.wait_ge(xt_hi, TILES * g + t + 1)
                hi, lo = (xt[j][:, :, t * P:(t + 1) * P] for j in range(2))
                dve.tensor_tensor(lo, one[1 + t][:, 0:D].rearrange("p (k n) -> p k n", k=KT), hi.bitcast(F32),
                                  ALU.subtract).then_inc(xt_lo, 1)

            def take_k(g):
                dve.wait_ge(qk_mm, 3 * g + 3)
                wait(dve, s_mm, TILES * g)
                for k in (1, 2):
                    for b in range(*SPAN1[k][:2]):
                        r = dve.tensor_scalar(k_blocks[:, :, b, :],
                                              one[2][:, (k - 1) * GROUP:k * GROUP].rearrange("p (g n) -> p g n", g=GB),
                                              mask[:, b:b + 1], None, ALU.mult)
                r.then_inc(k_done, 1)

            def take_v(g, t):
                dve.wait_ge(v_mm, TILES * g + t + 1)
                wait(dve, v_swapped[t], 32 * g)
                wait(dve, v_kept, TILES * (g - 1) + t + 1)
                wait(dve, pv_mm, TILES * (g - 1) + t + 1)
                dve.tensor_tensor(v_nat[:, t, :], one[3 if t == 0 else 0][:, 0:2 * VE],
                                  bv[:].rearrange("p r h c -> p (r h c)"), ALU.add).then_inc(v_done, 1)

            def soften(g, t):
                s = score[:, t, :].rearrange("p (h n) -> p h n", h=H1)
                dve.wait_ge(s_mm, TILES * g + t + 1)
                if t == 0:
                    dve.wait_ge(bias_done, g + 1)
                wait(dve, shifted, TILES * (g - 1) + t + 1)
                dve.scalar_tensor_tensor(out=s, in0=two[t][:, 0:S].rearrange("p (h n) -> p h n", h=H1), scalar=SCALE1,
                                         in1=bias[:, t, :].unsqueeze(1).broadcast_to([P, H1, NODES]),
                                         op0=ALU.mult, op1=ALU.add).then_inc(biased, 1)
                dve.wait_ge(biased, TILES * g + t + 1)
                dve.tensor_reduce(smax[:, t, :], s, AX_X, ALU.max).then_inc(maxed, 1)

            def find_magnitude(g, t):
                s = score[:, t, :].rearrange("p (h n) -> p h n", h=H1)
                wait(dve, rden_masked, TILES * (g - 1) + t + 1)
                dve.tensor_reduce(samax[:, t, :], s, AX_X, ALU.max, apply_absolute_value=True).then_inc(magnitude, 1)

            def take_ctx(g, t):
                o = one[1 + t][:, 0:2 * VE].rearrange("p (h c) -> p h c", c=VW)
                dve.wait_ge(pv_mm, TILES * g + t + 1)
                dve.reciprocal(rden[:, t, :], o[:, :, DH1]).then_inc(rden_done, 1)
                dve.wait_ge(rden_done, TILES * g + t + 1)
                dve.wait_ge(magnitude, TILES * g + t + 1)
                dve.scalar_tensor_tensor(out=rden[:, t, :], in0=samax[:, t, :], scalar=0.0, in1=rden[:, t, :],
                                         op0=ALU.is_gt, op1=ALU.mult).then_inc(rden_masked, 1)
                dve.wait_ge(rden_masked, TILES * g + t + 1)
                wait(dve, ct_mm, TILES * (g - 1) + t + 1)
                dve.tensor_tensor(ctxt[:, t, :].rearrange("p (h c) -> p h c", h=H1), o[:, :, 0:DH1],
                                  rden[:, t, :].unsqueeze(2).broadcast_to([P, H1, DH1]), ALU.mult).then_inc(ctx_done, 1)

            def ctxt_low(g, t):
                dve.wait_ge(ctxt_hi, TILES * g + t + 1)
                dve.tensor_tensor(ctx_t[1][:, t, :], one[3 if t == 0 else 0][:, 0:D], ctx_t[0][:, t, :].bitcast(F32),
                                  ALU.subtract).then_inc(ctxt_lo, 1)

            def finish(g):
                dve.wait_ge(res_done, g + 1)
                wait(dve, out_stored, 16 * g)
                for t in range(TILES):
                    dve.wait_ge(o_mm, TILES * g + t + 1)
                    o = one[3] if t == 0 else two[0]
                    dve.scalar_tensor_tensor(out=y[:, t, :], in0=o[:, 0:D], scalar=1.0, in1=res[:, t, :], op0=ALU.mult,
                                             op1=ALU.add, accum_out=ysum[:, t:t + 1]).then_inc(y_done, 1)
                dve.wait_ge(y_done, TILES * (g + 1))
                dve.tensor_scalar(nmean[:], ysum[:], -1.0 / D, None, ALU.mult).then_inc(mean_done, 1)
                dve.tensor_scalar(nmean_c[:], ysum[:], -ROOT / D, None, ALU.mult).then_inc(mean_done, 1)

            def norm(g):
                dve.wait_ge(rstd_done, g + 1)
                for t in range(TILES):
                    dve.tensor_scalar(y[:, t, :], y[:, t, :], nmean[:, t:t + 1], rstd[:, t:t + 1],
                                      ALU.add, ALU.mult).then_inc(out_done, 1)

            for t in range(TILES):
                xt_low(0, t)
            last["vector"][0]()
            dve.memset(v_pairs[:], 0.0).then_inc(pairs_zeroed, 1)

            def step(g, front=True, back=True, late=True, more=True):
                b = g - 1
                if front:
                    take_k(g)
                if front and not back:
                    last["vector"][1]()
                if front:
                    take_v(g, 0)
                if back:
                    for t in range(TILES):
                        take_ctx(b, t)
                if front:
                    take_v(g, 1)
                if late:
                    norm(g - 2)
                if back:
                    ctxt_low(b, 0)
                if front and more:
                    for t in range(TILES):
                        xt_low(g + 1, t)
                if back:
                    ctxt_low(b, 1)
                if front:
                    for t in range(TILES):
                        soften(g, t)
                    for t in range(TILES):
                        find_magnitude(g, t)
                if back:
                    finish(b)

            step(0, back=False, late=False)
            step(1, late=False)
            with dve.Fori(2, NG - 1) as g:
                step(g)
            step(NG - 1, more=False)
            step(NG, front=False)
            step(NG + 1, front=False, back=False)

        @block.gpsimd
        def _(pool):
            def double_adj(g):
                pool.wait_ge(adj_loaded, 16 * (g + 1))
                wait(pool, biased, TILES * g)
                pool.tensor_tensor(bias[:], adj_in[:], adj_in[:], ALU.add).then_inc(bias_done, 1)

            def bias_res(g):
                pool.wait_ge(res_loaded, 16 * (g + 1))
                for t in range(TILES):
                    r = pool.tensor_tensor(res[:, t, :], res[:, t, :], bo[:], ALU.add)
                r.then_inc(res_done, 1)

            def shift(g, t):
                s, p = (b[:, t, :].rearrange("p (h n) -> p h n", h=H1) for b in (score, prob))
                pool.wait_ge(maxed, TILES * g + t + 1)
                wait(pool, pt_mm, TILES * (g - 1) + t + 1)
                pool.tensor_tensor(p, s, smax[:, t, :].unsqueeze(2).broadcast_to([P, H1, NODES]),
                                   ALU.subtract).then_inc(shifted, 1)

            def root(g):
                pool.wait_ge(sq_done, TILES * (g + 1))
                pool.tensor_tensor(var[:], ssq[:], eps_ln[:], ALU.add).then_inc(var_done, 1)
                pool.wait_ge(var_done, g + 1)
                pool.tensor_tensor(rstd[:], var[:], half[:], ALU.pow).then_inc(rstd_done, 1)

            def step(g, front=True, back=True, late=True, more=True):
                if front and not back:
                    last["gpsimd"]()
                if front:
                    double_adj(g)
                if late:
                    root(g - 2)
                if back:
                    bias_res(g - 1)
                if front:
                    for t in range(TILES):
                        shift(g, t)

            step(0, back=False, late=False)
            step(1, late=False)
            with pool.Fori(2, NG - 1) as g:
                step(g)
            step(NG - 1, more=False)
            step(NG, front=False)
            step(NG + 1, front=False, back=False)


def program(nc, a, out):
    x2 = nc.dram_tensor("x2", (TOKENS, D), F32).ap()

    def groups(ap):
        return ap.rearrange("(g t p) d -> g p t d", t=TILES, p=P)

    xT = a["xT"].rearrange("(k p) (g n) -> k g p n", p=P, n=GROUP)
    w0 = {n: a[f"L0_gnn_{n}"] for n in ("wq", "bq", "wk", "bk", "wv", "bv", "wo", "bo", "w1", "b1", "w2", "b2",
                                        "alpha1", "gamma1", "alpha2", "gamma2")}
    w0 |= {"ident": a["ident"], "mask0": a["mask0"]}
    w1 = {n: a[f"L1_gnn_{n}"] for n in ("Wq", "Wk", "Wv", "Wo")}
    w0 |= {"mask1": a["mask1"], "bv1": a["L1_gnn_bv"], "bo1": a["L1_gnn_bo"]}
    VE1 = H1 // 2 * (DH1 + 1)
    with ExitStack() as ctx:
        def sb(name, shape, dt=F32):
            return ctx.enter_context(nc.sbuf_tensor(name, shape, dt))

        def sem(name):
            return ctx.enter_context(nc.semaphore(name))

        shared = {"W": {n: [sb(f"{n}_{s}", [P, KT, 2 * VE1 if n == "wv" else D], F32R) for s in ("hi", "lo")]
                        for n in ("wq", "wk", "wv", "wo")},
                  "ident": sb("ident", [P, P]), "mask": sb("mask_l1", [P, NB1]), "bo": sb("bo_l1", [P, D]),
                  "bv": sb("bv_l1", [P, 2, H1 // 2, DH1 + 1]), "VE1": VE1}
        shared |= {n: sb(n, [P, TILES]) for n in ("half", "eps_rms", "eps_ln")}
        block = ctx.enter_context(nc.Block())
        last, free = layer0(nc, block, sem, groups(a["x"]), xT, groups(a["adj"]), w0, w1, groups(x2), shared)
        layer1(nc, block, sem, groups(x2), groups(a["adj"]), groups(out), shared, last, free)


def kernel(**inputs):
    import numpy as np
    import concourse.bacc as bacc
    from concourse.bass_utils import run_bass_kernel_spmd

    def block_mask(heads, blocks):
        rows = np.arange(P)[:, None]
        tile = np.array([t for t, _ in blocks])[None, :]
        head = np.array([h for _, h in blocks])[None, :]
        return ((rows + P * tile) // (D // heads) == head).astype(np.float32)

    host = {}
    for name, value in inputs.items():
        value = np.asarray(value)
        if name in ("x", "adj"):
            value = value.reshape(TOKENS, -1)
        elif name.startswith("L1_gnn_W"):
            value = value.T
        elif name in ("L0_gnn_bq", "L0_gnn_bk", "L0_gnn_b1"):
            value = value.reshape(-1, P).T
        host[name] = np.ascontiguousarray(value)
    host["xT"] = np.ascontiguousarray(host["x"].T)
    host["ident"] = np.eye(P, dtype=np.float32)
    host["mask0"] = block_mask(H0, BLOCKS0)
    host["mask1"] = block_mask(H1, BLOCKS1)

    nc = bacc.Bacc("TRN2", target_bir_lowering=False, num_devices=1, dynamic_dma_scratch_size=8192)
    arrays, args = {}, {}
    for name, value in host.items():
        arrays[f"in_{name}"] = value
        args[name] = nc.dram_tensor(f"in_{name}", value.shape, F32, kind="ExternalInput").ap()
    out = nc.dram_tensor("out", (TOKENS, D), F32, kind="ExternalOutput").ap()
    program(nc, args, out)
    r = run_bass_kernel_spmd(nc, [arrays], core_ids=[0])
    return np.asarray(r.results[0]["out"]).reshape(GRAPHS, NODES, D)
```
